# Optimizing a Trainium2 kernel written in Bass

```python
import numpy as np
import jax
import jax.numpy as jnp

def _softmax(x, axis=-1):
    return jax.nn.softmax(x, axis=axis)

def _gelu(x):
    return jax.nn.gelu(x, approximate=True)

def _silu(x):
    return jax.nn.silu(x)

def _sigmoid(x):
    return jax.nn.sigmoid(x)

def _layernorm(x, axis=-1, eps=1e-05):
    m = jnp.mean(x, axis=axis, keepdims=True)
    v = jnp.var(x, axis=axis, keepdims=True)
    return (x - m) / jnp.sqrt(v + eps)

def _scatter_add(tgt, idx, src, axis=0):
    return tgt.at[idx].add(src)

def _segment_sum(src, seg, n):
    return jax.ops.segment_sum(src, seg, n)
kernel_name = 'mk_macaron_d2_jaxref_r8_5babd3'

def setup_inputs(seed: int=0):
    np.random.seed(seed)
    _w = jnp.asarray

    def _L0_attn_setup():
        import math
        import jax, jax.numpy as jnp
        import numpy as np
        B, T, E, H = (2, 256, 256, 16)
        D = E // H

        def _alibi_slopes(n):
            start = 2.0 ** (-2.0 ** (-(math.log2(n) - 3)))
            return np.array([start * start ** i for i in range(n)], dtype=np.float32)
        key = jax.random.key(seed)
        ks = jax.random.split(key, 5)
        w_scale = 0.02
        return {'x': jax.random.normal(ks[0], (B, T, E), dtype=jnp.float32), 'Wq': jax.random.normal(ks[1], (E, E), dtype=jnp.float32) * w_scale, 'bq': jnp.zeros((E,), jnp.float32), 'Wk': jax.random.normal(ks[2], (E, E), dtype=jnp.float32) * w_scale, 'bk': jnp.zeros((E,), jnp.float32), 'Wv': jax.random.normal(ks[3], (E, E), dtype=jnp.float32) * w_scale, 'bv': jnp.zeros((E,), jnp.float32), 'Wo': jax.random.normal(ks[4], (E, E), dtype=jnp.float32) * w_scale, 'bo': jnp.zeros((E,), jnp.float32), 'slopes': jnp.asarray(_alibi_slopes(H))}
    _L0_attn_in = _L0_attn_setup()

    def _L0_ffn_setup():
        import jax, jax.numpy as jnp
        import numpy as np
        B, S, H = (2, 128, 256)
        E, K = (8, 2)
        F = 176
        FS = 704
        NORM_TOPK = False

        def _swiglu(x, wg, wu, wd):
            return jax.nn.silu(x @ wg) * (x @ wu) @ wd
        key = jax.random.key(seed)
        ks = jax.random.split(key, 9)
        s = 0.02
        return {'hidden_states': jax.random.normal(ks[0], (B, S, H), dtype=jnp.float32), 'Wr': jax.random.normal(ks[1], (H, E), dtype=jnp.float32) * s, 'Wg': jax.random.normal(ks[2], (E, H, F), dtype=jnp.float32) * s, 'Wu': jax.random.normal(ks[3], (E, H, F), dtype=jnp.float32) * s, 'Wd': jax.random.normal(ks[4], (E, F, H), dtype=jnp.float32) * s, 'Sg': jax.random.normal(ks[5], (H, FS), dtype=jnp.float32) * s, 'Su': jax.random.normal(ks[6], (H, FS), dtype=jnp.float32) * s, 'Sd': jax.random.normal(ks[7], (FS, H), dtype=jnp.float32) * s, 'Wsg': jax.random.normal(ks[8], (H, 1), dtype=jnp.float32) * s}
    _L0_ffn_in = _L0_ffn_setup()

    def _L1_attn_setup():
        import jax, jax.numpy as jnp
        import numpy as np
        NH = 16
        key = jax.random.key(seed)
        ks = jax.random.split(key, 5)
        B, T, D = (2, 256, 256)
        scale = 0.02
        return {'x': jax.random.normal(ks[0], (B, T, D), dtype=jnp.float32), 'Wq': jax.random.normal(ks[1], (D, D), dtype=jnp.float32) * scale, 'Wk': jax.random.normal(ks[2], (D, D), dtype=jnp.float32) * scale, 'Wv': jax.random.normal(ks[3], (D, D), dtype=jnp.float32) * scale, 'Wo': jax.random.normal(ks[4], (D, D), dtype=jnp.float32) * scale}
    _L1_attn_in = _L1_attn_setup()

    def _L1_ffn_setup():
        import jax, jax.numpy as jnp
        import numpy as np
        TOP_K = 4
        key = jax.random.key(seed)
        ks = jax.random.split(key, 8)
        B, S, D, E, H, HS = (2, 256, 256, 16, 128, 512)
        scaled = lambda k, shape, fan: jax.random.normal(k, shape, jnp.float32) * fan ** (-0.5)
        return {'x': jax.random.normal(ks[0], (B, S, D), jnp.float32), 'w_router': scaled(ks[1], (D, E), D), 'we1': scaled(ks[2], (E, D, H), D), 'we3': scaled(ks[3], (E, D, H), D), 'we2': scaled(ks[4], (E, H, D), H), 'ws1': scaled(ks[5], (D, HS), D), 'ws3': scaled(ks[6], (D, HS), D), 'ws2': scaled(ks[7], (HS, D), HS)}
    _L1_ffn_in = _L1_ffn_setup()
    _d = {'L0_attn_x': _L0_attn_in['x'], 'L0_attn_Wq': _L0_attn_in['Wq'], 'L0_attn_bq': _L0_attn_in['bq'], 'L0_attn_Wk': _L0_attn_in['Wk'], 'L0_attn_bk': _L0_attn_in['bk'], 'L0_attn_Wv': _L0_attn_in['Wv'], 'L0_attn_bv': _L0_attn_in['bv'], 'L0_attn_Wo': _L0_attn_in['Wo'], 'L0_attn_bo': _L0_attn_in['bo'], 'L0_attn_slopes': _L0_attn_in['slopes'], 'L0_ffn_Wr': _L0_ffn_in['Wr'], 'L0_ffn_Wg': _L0_ffn_in['Wg'], 'L0_ffn_Wu': _L0_ffn_in['Wu'], 'L0_ffn_Wd': _L0_ffn_in['Wd'], 'L0_ffn_Sg': _L0_ffn_in['Sg'], 'L0_ffn_Su': _L0_ffn_in['Su'], 'L0_ffn_Sd': _L0_ffn_in['Sd'], 'L0_ffn_Wsg': _L0_ffn_in['Wsg'], 'L1_attn_Wq': _L1_attn_in['Wq'], 'L1_attn_Wk': _L1_attn_in['Wk'], 'L1_attn_Wv': _L1_attn_in['Wv'], 'L1_attn_Wo': _L1_attn_in['Wo'], 'L1_ffn_w_router': _L1_ffn_in['w_router'], 'L1_ffn_we1': _L1_ffn_in['we1'], 'L1_ffn_we3': _L1_ffn_in['we3'], 'L1_ffn_we2': _L1_ffn_in['we2'], 'L1_ffn_ws1': _L1_ffn_in['ws1'], 'L1_ffn_ws3': _L1_ffn_in['ws3'], 'L1_ffn_ws2': _L1_ffn_in['ws2']}
    _x0 = _d['L0_attn_x']
    _d['L0_attn_x'] = jax.random.normal(jax.random.fold_in(jax.random.key(seed), 1), (1, 1024, 256), dtype=_x0.dtype)
    del _x0
    return _d

def reference(L0_attn_x, L0_attn_Wq, L0_attn_bq, L0_attn_Wk, L0_attn_bk, L0_attn_Wv, L0_attn_bv, L0_attn_Wo, L0_attn_bo, L0_attn_slopes, L0_ffn_Wr, L0_ffn_Wg, L0_ffn_Wu, L0_ffn_Wd, L0_ffn_Sg, L0_ffn_Su, L0_ffn_Sd, L0_ffn_Wsg, L1_attn_Wq, L1_attn_Wk, L1_attn_Wv, L1_attn_Wo, L1_ffn_w_router, L1_ffn_we1, L1_ffn_we3, L1_ffn_we2, L1_ffn_ws1, L1_ffn_ws3, L1_ffn_ws2):

    def _L0_attn_ref(x, Wq, bq, Wk, bk, Wv, bv, Wo, bo, slopes):
        import math
        import jax, jax.numpy as jnp
        import numpy as np
        B, T, E, H = (2, 256, 256, 16)
        D = E // H

        def _alibi_slopes(n):
            start = 2.0 ** (-2.0 ** (-(math.log2(n) - 3)))
            return np.array([start * start ** i for i in range(n)], dtype=np.float32)
        b, t, e = x.shape
        h, d = (H, e // H)
        scaling = d ** (-0.5)
        q = (jnp.einsum('bte,fe->btf', x, Wq) + bq) * scaling
        k = jnp.einsum('bte,fe->btf', x, Wk) + bk
        v = jnp.einsum('bte,fe->btf', x, Wv) + bv
        q = q.reshape(b, t, h, d)
        k = k.reshape(b, t, h, d)
        v = v.reshape(b, t, h, d)
        scores = jnp.einsum('bihd,bjhd->bhij', q, k)
        pos = jnp.arange(t)
        alibi = -jnp.abs(pos[None, :] - pos[:, None]).astype(scores.dtype)
        scores = scores + slopes[:, None, None] * alibi
        probs = jax.nn.softmax(scores.astype(jnp.float32), axis=-1).astype(scores.dtype)
        out = jnp.einsum('bhij,bjhd->bihd', probs, v).reshape(b, t, e)
        return jnp.einsum('bte,fe->btf', out, Wo) + bo

    def _L0_ffn_ref(hidden_states, Wr, Wg, Wu, Wd, Sg, Su, Sd, Wsg):
        import jax, jax.numpy as jnp
        import numpy as np
        B, S, H = (2, 128, 256)
        E, K = (8, 2)
        F = 176
        FS = 704
        NORM_TOPK = False

        def _swiglu(x, wg, wu, wd):
            return jax.nn.silu(x @ wg) * (x @ wu) @ wd
        b, s, h = hidden_states.shape
        x = hidden_states.reshape(-1, h)
        router_logits = x @ Wr
        probs = jax.nn.softmax(router_logits.astype(jnp.float32), axis=-1)
        routing_weights, selected = jax.lax.top_k(probs, K)
        if NORM_TOPK:
            routing_weights = routing_weights / routing_weights.sum(-1, keepdims=True)
        routing_weights = routing_weights.astype(x.dtype)
        C = jnp.einsum('tk,tke->te', routing_weights, jax.nn.one_hot(selected, E, dtype=x.dtype))
        expert_out = jax.vmap(lambda wg, wu, wd: _swiglu(x, wg, wu, wd))(Wg, Wu, Wd)
        moe_out = jnp.einsum('te,eth->th', C, expert_out)
        shared = _swiglu(x, Sg, Su, Sd)
        shared = jax.nn.sigmoid(x @ Wsg) * shared
        out = (moe_out + shared).reshape(b, s, h)
        return out

    def _L1_attn_ref(x, Wq, Wk, Wv, Wo):
        import jax, jax.numpy as jnp
        import numpy as np
        NH = 16
        B, T, D = x.shape
        hd = D // NH
        q = (x @ Wq.T).reshape(B, T, NH, hd).transpose(0, 2, 1, 3)
        k = (x @ Wk.T).reshape(B, T, NH, hd).transpose(0, 2, 1, 3)
        v = (x @ Wv.T).reshape(B, T, NH, hd).transpose(0, 2, 1, 3)
        att = jnp.einsum('bhtd,bhsd->bhts', q, k) / jnp.sqrt(jnp.asarray(hd, x.dtype))
        neg = jnp.finfo(att.dtype).min
        mask = jnp.triu(jnp.full((T, T), neg, dtype=att.dtype), k=1)
        att = att + mask
        w = jax.nn.softmax(att, axis=-1)
        z = jnp.einsum('bhts,bhsd->bhtd', w, v)
        z = z.transpose(0, 2, 1, 3).reshape(B, T, D)
        return z @ Wo.T

    def _L1_ffn_ref(x, w_router, we1, we3, we2, ws1, ws3, ws2):
        import jax, jax.numpy as jnp
        import numpy as np
        TOP_K = 4
        B, S, D = x.shape
        T = B * S
        E = w_router.shape[1]
        xt = x.reshape(T, D)
        probs = jax.nn.softmax(xt @ w_router, axis=-1)
        top_w, top_i = jax.lax.top_k(probs, TOP_K)
        top_w = top_w / jnp.sum(top_w, axis=-1, keepdims=True)
        cw = jnp.zeros((T, E), xt.dtype).at[jnp.arange(T)[:, None], top_i].add(top_w)
        g = jax.nn.silu(jnp.einsum('td,edh->teh', xt, we1)) * jnp.einsum('td,edh->teh', xt, we3)
        g = g * cw[:, :, None]
        moe_out = jnp.einsum('teh,ehd->td', g, we2)
        shared = jax.nn.silu(xt @ ws1) * (xt @ ws3) @ ws2
        k = TOP_K
        out = shared / (k + 1) + moe_out * (k / (k + 1))
        return out.reshape(B, S, D)
    x = L0_attn_x
    x = x + 0.5 * _L0_ffn_ref(_layernorm(x, axis=-1), L0_ffn_Wr, L0_ffn_Wg, L0_ffn_Wu, L0_ffn_Wd, L0_ffn_Sg, L0_ffn_Su, L0_ffn_Sd, L0_ffn_Wsg)
    x = x + _L0_attn_ref(_layernorm(x, axis=-1), L0_attn_Wq, L0_attn_bq, L0_attn_Wk, L0_attn_bk, L0_attn_Wv, L0_attn_bv, L0_attn_Wo, L0_attn_bo, L0_attn_slopes)
    x = x + 0.5 * _L0_ffn_ref(_layernorm(x, axis=-1), L0_ffn_Wr, L0_ffn_Wg, L0_ffn_Wu, L0_ffn_Wd, L0_ffn_Sg, L0_ffn_Su, L0_ffn_Sd, L0_ffn_Wsg)
    x = x + 0.5 * _L1_ffn_ref(_layernorm(x, axis=-1), L1_ffn_w_router, L1_ffn_we1, L1_ffn_we3, L1_ffn_we2, L1_ffn_ws1, L1_ffn_ws3, L1_ffn_ws2)
    x = x + _L1_attn_ref(_layernorm(x, axis=-1), L1_attn_Wq, L1_attn_Wk, L1_attn_Wv, L1_attn_Wo)
    x = x + 0.5 * _L1_ffn_ref(_layernorm(x, axis=-1), L1_ffn_w_router, L1_ffn_we1, L1_ffn_we3, L1_ffn_we2, L1_ffn_ws1, L1_ffn_ws3, L1_ffn_ws2)
    return x

_drawn_inputs = setup_inputs


def setup_inputs(seed=0):
    import zlib

    import numpy as np

    out = dict(_drawn_inputs(seed))
    spreads = {'L0_attn_bq': (0.0, 0.8),
     'L0_attn_bk': (0.0, 2.0),
     'L0_attn_bv': (0.0, 0.299),
     'L0_attn_bo': (0.0, 0.1)}
    factors = {'L0_attn_Wq': 8.0,
     'L0_attn_Wk': 8.0,
     'L0_ffn_Wr': 8.0,
     'L0_ffn_Wg': 8.0,
     'L0_ffn_Wu': 7.35,
     'L0_ffn_Wd': 7.812,
     'L0_ffn_Sg': 3.054,
     'L0_ffn_Su': 3.076,
     'L0_ffn_Sd': 3.083,
     'L0_ffn_Wsg': 8.0,
     'L1_attn_Wq': 8.0,
     'L1_attn_Wk': 8.0,
     'L1_attn_Wv': 3.524,
     'L1_attn_Wo': 3.685}
    for name, (base, spread) in spreads.items():
        noise = np.random.default_rng([zlib.crc32(name.encode()), seed]).standard_normal(out[name].shape)
        drawn = base * np.exp(spread * noise) if base else spread * noise
        out[name] = jnp.asarray(drawn.astype(out[name].dtype))
    for name, factor in factors.items():
        out[name] = (out[name] * factor).astype(out[name].dtype)
    return out
```

```python
from contextlib import ExitStack

import concourse.bass as bass
from concourse import mybir

F32 = mybir.dt.float32
F32R = mybir.dt.float32r
U32 = mybir.dt.uint32
ALU = mybir.AluOpType
ACT = mybir.ActivationFunctionType
AX = mybir.AxisListType

P = 128
T = 1024
D = 256
TILES = T // P
KC = D // P
HALF = 512
HALVES = T // HALF
NH = 16
HD = D // NH
QUAD = 4
QUADS = NH // QUAD
EPS = 1e-5
WG, WU, WD, WSEL = 0, 2 * P, 4 * P, 6 * P
WCOLS = 7 * P
RC = 32
QX = 64
MROW = 80
BIG = 3.0e38

FFN0 = dict(experts=8, topk=2, chunks=17, gated=True)
FFN1 = dict(experts=16, topk=4, chunks=20, gated=False)


def attention_order(causal):
    items = [(j, qt, kh, min(HALF, P * (qt + 1) - HALF * kh) if causal else HALF)
             for j in range(QUAD) for qt in range(TILES) for kh in range(HALVES)]
    items = [it for it in items if it[3] > 0]
    steps = [(qh, kt, max(0, kt - 4 * qh) * P if causal else 0)
             for qh in range(HALVES) for kt in range(4 * qh + 4 if causal else TILES)]
    last_kt = [max(kt for qh, kt, _ in steps if qh == h) for h in range(HALVES)]
    per_pair = -(-len(items) // (2 * len(steps) - 4))

    order = [("max", 0, it) for it in items] + [("maxend", 0, None)]
    pairs = [(g, st, pair) for g in range(QUADS) for st in steps for pair in range(2)]
    for n, (g, st, pair) in enumerate(pairs):
        if st == steps[0] and pair == 0:
            left = list(items) if g + 1 < QUADS else []
        order.append(("score", g, (st, pair, st == steps[0])))
        if left:
            order += [("max", g + 1, it) for it in left[:per_pair]]
            left = left[per_pair:]
            if not left:
                order.append(("maxend", g + 1, None))
        for g2, st2, pair2 in pairs[n - 1:n] if n else []:
            order.append(("pv", g2, (st2, pair2)))
            if pair2 == 1 and st2[1] == last_kt[st2[0]]:
                order.append(("z", g2, st2[0]))
    order += [("pv", g, (st, pair)), ("z", g, st[0])]

    at_z = [n for n, (kind, _, _) in enumerate(order) if kind == "z"]
    return dict(order=order, nitems=len(items), nsteps=len(steps), last_kt=last_kt, pairs=len(pairs),
                z_pv=[sum(k == "pv" for k, _, _ in order[:n]) for n in at_z],
                mdone=[2 * sum(k == "maxend" for k, _, _ in order[:n]) for n in at_z])


def signals(cfg):
    each = dict(x_added=4, bn=TILES, var=TILES, std=1, rstd=1, ln_in=TILES, ln_banks=4, ln_hi=4, ln_lo=4,
                sums=1, ot_done=4, out_banks=4)
    if cfg["kind"] == "ffn":
        n = cfg["chunks"]
        steps = dict.fromkeys(("gate", "up", "silu", "su_done", "comb", "h_done", "h_hi", "h_lo", "down_done"), 2 * n)
        return dict(each, w_loaded0=16 * ((n + 1) // 2), w_loaded1=16 * (n // 2), w_hi=n, w_lo=n, logits=1, dv_done=1,
                    dl_done=int(cfg["gated"]), exps=3 if cfg["gated"] else 1, cw_done=1, cw_banks=1, cwT_hi=2,
                    cwT_lo=2, **steps)
    rows = 16 * QUAD * (6 + 8)
    nmax, quads, zs = QUADS * cfg["nitems"], QUADS, QUADS * HALVES
    return dict(each, region_free=1, aw_loaded0=32, aw_loaded1=32, aw_split=4, kx_loaded=32, v_init=1,
                slots_zeroed=1, qx_done=1, kx_done=quads, p_quad_done=quads - 2, rows_loaded0=rows, rows_loaded1=rows,
                m_loaded=16 * 2 * NH, qk_banks=8, tmp_q=8, hi_q=8, lo_q=8, v_banks=TILES, v_done=TILES,
                nmax_init=int(cfg["causal"]), max_banks=nmax, reduced=nmax, nm_done=quads, m_bank=2 * quads,
                mh_done=2 * quads, ml_done=2 * quads, score_banks=cfg["pairs"], exp_done=cfg["pairs"],
                pv_done=cfg["pairs"], z_raw=zs, z_bank=zs, rden=zs, z_norm=zs, z_in=TILES, z_banks=4, z_hi=4, z_lo=4)


def program(nc, A, out, phases):
    for cfg in phases:
        if cfg["kind"] == "attn":
            cfg.update(attention_order(cfg["causal"]))
    ctx = ExitStack()
    with ctx:
        def sb(name, shape, dt=F32, stack=ctx):
            return stack.enter_context(nc.sbuf_tensor(name, shape, dt))

        def sem(name):
            return ctx.enter_context(nc.semaphore(name))

        ps = ctx.enter_context(nc.psum_tensor("ps", [P, 8, 512], F32))

        x = sb("x", [P, TILES, D])
        xz = sb("xz", [P, 2 * KC, T], F32R)
        xn = sb("xn", [P, TILES, D])
        ident = sb("ident", [P, P])
        dist = sb("dist", [P, P])
        causal = sb("causal", [P, P])
        iota = sb("iota", [P, 16])
        eps = sb("eps", [P, 1])
        zero_r = sb("zero_r", [P, HALF], F32R)
        ident_r = sb("ident_r", [P, P], F32R)
        dist_r = sb("dist_r", [P, P], F32R)
        causal_r = sb("causal_r", [P, P], F32R)
        wr0 = sb("wr0", [P, KC, RC])
        wr1 = sb("wr1", [P, KC, RC])
        wrh = sb("wrh", [P, 2, KC, RC], F32R)
        wrl = sb("wrl", [P, 2, KC, RC], F32R)
        stats = sb("stats", [P, TILES, 6])
        mv = sb("mv", [P, TILES, 2])
        std = sb("std", [P, TILES])
        rstd = sb("rstd", [P, TILES])
        cols = sb("cols", [P, 8])
        bvb = sb("bvb", [P, D])
        slopes = sb("slopes", [P, NH])
        keep = sb("keep", [P, 2])
        srow = sb("srow", [P, NH])

        ffn = ExitStack()
        wraw = sb("wraw", [P, 2, WCOLS], F32, ffn)
        whi = sb("whi", [P, 2, WCOLS], F32R, ffn)
        wlo = sb("wlo", [P, 2, WSEL], F32R, ffn)
        sg = sb("sg", [P, 2, HALF], F32, ffn)
        su = sb("su", [P, 2, HALF], F32, ffn)
        hf = sb("hf", [P, 2, HALF], F32, ffn)
        hh = sb("hh", [P, 2, HALF], F32R, ffn)
        hl = sb("hl", [P, 2, HALF], F32R, ffn)
        cwT = sb("cwT", [P, T], F32R, ffn)
        lg = sb("lg", [P, TILES, RC], F32, ffn)
        top8 = sb("top8", [P, TILES, 8], F32, ffn)
        idx8 = sb("idx8", [P, TILES, 8], U32, ffn)
        idxf = sb("idxf", [P, TILES, 8], F32, ffn)
        dl = sb("dl", [P, TILES, RC], F32, ffn)
        el = sb("el", [P, TILES, RC], F32, ffn)
        ev = sb("ev", [P, TILES, 4], F32, ffn)
        dv = sb("dv", [P, TILES, 4], F32, ffn)
        wk = sb("wk", [P, TILES, 4], F32, ffn)
        ssum = sb("ssum", [P, TILES], F32, ffn)
        rsum = sb("rsum", [P, TILES], F32, ffn)
        zg = sb("zg", [P, TILES], F32, ffn)
        zg1 = sb("zg1", [P, TILES], F32, ffn)
        zg2 = sb("zg2", [P, TILES], F32, ffn)
        onehot = sb("onehot", [P, TILES * 4, 16], F32, ffn)
        onew = sb("onew", [P, TILES * 4, 16], F32, ffn)
        cw = sb("cw", [P, TILES, RC], F32, ffn)
        ffn.close()

        qs = sb("qs", [P, 2 * QUAD, T], F32R)
        ks = sb("ks", [P, 2 * QUAD, T], F32R)
        vaug = sb("vaug", [P, TILES, NH, 32])
        chi = sb("chi", [P, 2, KC, T], F32R)
        clo = sb("clo", [P, 2, KC, T], F32R)
        tmp = sb("tmp", [P, 2, HALF])
        kx = sb("kx", [P, T])
        kxs = sb("kxs", [P, T])
        slope_i = sb("slope_i", [P, 2, QUAD, P])
        slope_h = sb("slope_h", [P, 2, QUAD, P], F32R)
        slope_l = sb("slope_l", [P, 2, QUAD, P], F32R)
        nmax = sb("nmax", [P, QUAD * TILES, 2])
        nm = sb("nm", [P, 2, QUAD * TILES])
        mhl = sb("mhl", [RC + QUAD, T], F32R)
        zraw = sb("zraw", [P, 2, HALF])
        rden = sb("rden", [P, 2, 16])
        awo = sb("awo", [P, 2, KC * D], F32R)
        early = ExitStack()
        araw = sb("araw", [P, 2, KC * D], F32, early)
        awh = sb("awh", [P, 3, KC * D], F32R, early)
        awl = sb("awl", [P, 3, KC * D], F32R, early)
        early.close()
        late = ExitStack()
        RING = 3
        pt = sb("pt", [P, RING, 2, HALF], F32, late)
        late.close()
        ot = sb("ot", [P, 4, HALF])

        S = {}
        router_steps, pool_steps = [0], [0]
        def s(name):
            if name not in S:
                S[name] = sem(name)
            return S[name]

        def nth(p, name, n):
            last = p - 1 if name == "x_added" else p
            return s(name), n + sum(signals(phases[q])[name] for q in range(last) if name in signals(phases[q]))

        consts = sem("consts_loaded")
        x_loaded = sem("x_loaded")
        wr_hi = sem("router_hi_split")
        setup = sem("setup_done")
        out_done = sem("out_written")

        def hi_f(ap):
            return ap.bitcast(F32)

        def three(pairs):
            r = []
            for a_h, a_l, b_h, b_l in pairs:
                r += [(a_h, b_h), (a_l, b_h), (a_h, b_l)]
            return r

        n_consts = 0
        const_loads = []
        for tile, name in ((ident, "ident"), (dist, "dist"), (causal, "causal"), (iota, "iota"), (cols, "cols"),
                           (bvb, "bvb"), (slopes, "slopes"), (keep, "keep")):
            const_loads.append((tile[:, :], A[name]))
        const_loads.append((wr0[:, :, :], A["wr0"]))
        const_loads.append((wr1[:, :, :], A["wr1"]))
        n_consts = 16 * len(const_loads)

        block = ctx.enter_context(nc.Block())
        nphase = len(phases)

        def sp_ffn(e, p, cfg):
            n = cfg["chunks"]
            w = A[cfg["w"]]

            def load(c, b):
                e.dma_start(wraw[:, b, :], w[bass.ds(c, 1), :, :].rearrange("o p n -> (o p) n"))\
                    .then_inc(s("w_loaded%d" % b), 16)

            if p > 0:
                prev = phases[p - 1]
                if prev["kind"] == "ffn":
                    e.wait_ge(*nth(p - 1, "w_hi", prev["chunks"]))
                    e.wait_ge(*nth(p - 1, "w_lo", prev["chunks"]))
                else:
                    e.wait_ge(*nth(p - 1, "pv_done", prev["pairs"]))
            load(0, 0)
            load(1, 1)
            with e.Fori(0, (n - 2) // 2) as i:
                for b in range(2):
                    e.wait_ge(*nth(p, "w_hi", 2 * i + b + 1))
                    e.wait_ge(*nth(p, "w_lo", 2 * i + b + 1))
                    load(2 * i + b + 2, b)
            if n % 2:
                e.wait_ge(*nth(p, "w_hi", n - 2))
                e.wait_ge(*nth(p, "w_lo", n - 2))
                load(n - 1, (n - 1) % 2)

        def sp_attn(e, p, cfg):
            e.wait_ge(*nth(p, "region_free", 1))
            for w in range(4):
                if w >= 2:
                    e.wait_ge(*nth(p, "aw_split", w - 1))
                e.dma_start(araw[:, w % 2, :], A[cfg["w"]][w, :, :]).then_inc(s("aw_loaded%d" % (w % 2)), 16)

            def quad_rows(g):
                if g >= 2:
                    e.wait_ge(*nth(p, "p_quad_done", g - 1))
                for j in range(QUAD):
                    h = QUAD * g + j
                    c, r = h // 8, HD * (h % 8)
                    sl = QUAD * (g % 2) + j
                    for dst, src in ((qs[0:16, sl, :], chi[r:r + HD, 0, c, :]), (qs[16:32, sl, :], chi[r:r + HD, 0, c, :]),
                                     (qs[32:48, sl, :], clo[r:r + HD, 0, c, :]), (ks[0:16, sl, :], chi[r:r + HD, 1, c, :]),
                                     (ks[16:32, sl, :], clo[r:r + HD, 1, c, :]), (ks[32:48, sl, :], chi[r:r + HD, 1, c, :])):
                        e.dma_start(hi_f(dst), hi_f(src)).then_inc(s("rows_loaded%d" % (g % 2)), 16)
                    if g >= 2:
                        for half in range(HALVES):
                            e.dma_start(hi_f(qs[MROW:MROW + 2, sl, HALF * half:HALF * (half + 1)]),
                                        hi_f(zero_r[0:2, :])).then_inc(s("rows_loaded%d" % (g % 2)), 16)

            def max_rows(g):
                e.wait_ge(*nth(p, "mh_done", 2 * (g + 1)))
                e.wait_ge(*nth(p, "ml_done", 2 * (g + 1)))
                for j in range(QUAD):
                    sl = QUAD * (g % 2) + j
                    for row in range(2):
                        e.dma_start(hi_f(qs[MROW + row:MROW + row + 1, sl, :]),
                                    hi_f(mhl[RC * row + j:RC * row + j + 1, :])).then_inc(s("m_loaded"), 16)

            e.wait_ge(*nth(p, "lo_q", 8))
            e.wait_ge(*nth(p, "slots_zeroed", 1))
            e.wait_ge(*nth(p, "qx_done", 1))
            quad_rows(0)
            quad_rows(1)
            for g in range(QUADS):
                max_rows(g)
                if g + 2 < QUADS:
                    quad_rows(g + 2)

        def rows_value(g):
            first = QUAD * 6 * 16
            again = QUAD * 8 * 16
            return first + (g // 2) * again

        @block.sync
        def _(e):
            e.dma_start(x[:, :, :], A["x"].rearrange("o (t p) d -> p (o t) d", p=P)).then_inc(x_loaded, 16)
            for dst, src in const_loads:
                e.dma_start(dst, src).then_inc(consts, 16)
            for p, cfg in enumerate(phases):
                if cfg["kind"] == "ffn":
                    sp_ffn(e, p, cfg)
                else:
                    sp_attn(e, p, cfg)
            e.wait_ge(*nth(nphase, "x_added", 4))
            e.dma_start(out.rearrange("o (t p) d -> p (o t) d", p=P), x[:, :, :]).then_inc(out_done, 16)
            e.wait_ge(out_done, 16)

        def pe_to_features(e, p, tag):
            for half in range(HALVES):
                e.wait_ge(*nth(p, tag + "_in", 4 * (half + 1)))
                for c in range(KC):
                    for t in range(4):
                        mm = e.transpose(ps[:, 4 + 2 * c + half, P * t:P * (t + 1)],
                                         xn[:, 4 * half + t, P * c:P * (c + 1)], ident[:, :])
                    mm.then_inc(s(tag + "_banks"), 1)

        def pe_finish(e, p):
            e.wait_ge(*nth(p, "ot_done", 4))
            for b in range(4):
                for k in range(2):
                    t = 2 * b + k
                    for c in range(KC):
                        mm = e.transpose(ps[:, 4 + b, D * k + P * c:D * k + P * (c + 1)],
                                         ot[:, 2 * c + t // 4, P * (t % 4):P * (t % 4 + 1)], ident[:, :])
                mm.then_inc(s("out_banks"), 1)

        def pe_ffn(e, p, cfg):
            n, r = cfg["chunks"], cfg["router"]
            pe_to_features(e, p, "ln")
            e.wait_ge(*nth(p, "ln_hi", 4))
            e.wait_ge(*nth(p, "ln_lo", 4))
            for t in range(TILES):
                tok = slice(P * t, P * (t + 1))
                terms = three([(xz[:, c, tok], xz[:, KC + c, tok], wrh[:, r, c, :], wrl[:, r, c, :]) for c in range(KC)])
                for k, (a, b) in enumerate(terms):
                    mm = e.matmul(ps[:, 7, RC * t:RC * (t + 1)], a, b, start=(k == 0), stop=(k == len(terms) - 1))
            mm.then_inc(s("logits"), 1)

            def proj(c, b, t, bank, col, last):
                tok = slice(HALF * t, HALF * (t + 1))
                terms = three([(whi[:, b, col + P * k:col + P * (k + 1)], wlo[:, b, col + P * k:col + P * (k + 1)],
                                xz[:, k, tok], xz[:, KC + k, tok]) for k in range(KC)])
                for k, (w, v) in enumerate(terms):
                    mm = e.matmul(ps[:, bank, :], w, v, start=(k == 0), stop=(k == len(terms) - 1))
                mm.then_inc(s(last), 1)

            def down(step, b, t):
                e.wait_ge(*nth(p, "h_hi", step + 1))
                e.wait_ge(*nth(p, "h_lo", step + 1))
                for d in range(KC):
                    terms = three([(whi[:, b, WD + P * d:WD + P * (d + 1)], wlo[:, b, WD + P * d:WD + P * (d + 1)],
                                    hh[:, t, :], hl[:, t, :])])
                    for w, v in terms:
                        mm = e.matmul(ps[:, 2 * d + t, :], w, v, start=False, stop=False, skip_group_check=True)
                mm.then_inc(s("down_done"), 1)

            def step(c, b, t, first):
                k = 2 * c + t
                if t == 0:
                    e.wait_ge(*nth(p, "w_hi", c + 1))
                    e.wait_ge(*nth(p, "w_lo", c + 1))
                if not first:
                    e.wait_ge(*nth(p, "silu", k))
                proj(c, b, t, 4, WG, "gate")
                if not first:
                    e.wait_ge(*nth(p, "su_done", k))
                proj(c, b, t, 5, WU, "up")
                if first:
                    e.wait_ge(*nth(p, "cw_done", 1))
                    for tt in range(TILES):
                        mm = e.transpose(ps[0:RC, 6 + tt // 4, P * (tt % 4):P * (tt % 4 + 1)], cw[:, tt, :], ident[:, :])
                    mm.then_inc(s("cw_banks"), 1)
                    e.wait_ge(*nth(p, "cwT_lo", 2))
                    for o in range(4):
                        e.matmul(ps[:, o, :], zero_r[:, 0:P], zero_r[:, :], start=True, stop=False,
                                 skip_group_check=True)
                else:
                    down(k - 1, b if t else 1 - b, 1 - t)
                    e.wait_ge(*nth(p, "h_done", k))
                e.matmul(ps[:, 6, :], whi[:, b, WSEL:WSEL + P], cwT[:, HALF * t:HALF * (t + 1)],
                         start=True, stop=True).then_inc(s("comb"), 1)

            if p > 0:
                e.wait_ge(*nth(p, "x_added", 4))
                e.wait_ge(*nth(p - 1, "ot_done", 4))
            step(0, 0, 0, True)
            step(0, 0, 1, False)
            with e.Fori(0, (n - 1) // 2) as i:
                for u in range(2):
                    for t in range(2):
                        step(2 * i + 1 + u, (1 + u) % 2, t, False)
            if n % 2 == 0:
                step(n - 1, (n - 1) % 2, 0, False)
                step(n - 1, (n - 1) % 2, 1, False)
            down(2 * n - 1, (n - 1) % 2, 1)
            for o in range(4):
                mm = e.matmul(ps[:, o, :], zero_r[:, 0:P], zero_r[:, :], start=False, stop=True, skip_group_check=True)
            mm.then_inc(s("sums"), 1)
            pe_finish(e, p)

        def pe_attn(e, p, cfg):
            pe_to_features(e, p, "ln")
            e.wait_ge(*nth(p, "ln_hi", 4))
            e.wait_ge(*nth(p, "ln_lo", 4))
            n = 0
            for w in range(2):
                e.wait_ge(*nth(p, "aw_split", w + 1))
                for m in range(KC):
                    for half in range(HALVES):
                        if n >= 4:
                            e.wait_ge(*nth(p, "tmp_q", n - 3))
                        tok = slice(HALF * half, HALF * (half + 1))
                        terms = three([(awh[:, w, D * c + P * m:D * c + P * (m + 1)], awl[:, w, D * c + P * m:D * c + P * (m + 1)],
                                        xz[:, c, tok], xz[:, KC + c, tok]) for c in range(KC)])
                        for k, (a, b) in enumerate(terms):
                            mm = e.matmul(ps[:, n % 4, :], a, b, start=(k == 0), stop=(k == len(terms) - 1))
                        mm.then_inc(s("qk_banks"), 1)
                        n += 1
            e.wait_ge(*nth(p, "aw_split", 3))
            for t in range(TILES):
                if t >= 4:
                    e.wait_ge(*nth(p, "v_done", t - 3))
                tok = slice(P * t, P * (t + 1))
                terms = three([(xz[:, c, tok], xz[:, KC + c, tok], awh[:, 2, D * c:D * (c + 1)], awl[:, 2, D * c:D * (c + 1)])
                               for c in range(KC)])
                for k, (a, b) in enumerate(terms):
                    mm = e.matmul(ps[:, 4 + t % 4, 0:D], a, b, start=(k == 0), stop=(k == len(terms) - 1))
                mm.then_inc(s("v_banks"), 1)
            e.wait_ge(*nth(p, "tmp_q", 8))
            e.wait_ge(*nth(p, "v_done", 8))

            nmx = nsc = npv = nz = 0
            for kind, g, arg in cfg["order"]:
                par = g % 2
                if kind == "max":
                    j, qt, kh, w = arg
                    sl = QUAD * par + j
                    if nmx % cfg["nitems"] == 0:
                        e.wait_ge(*nth(p, "rows_loaded%d" % par, rows_value(g)))
                        e.wait_ge(*nth(p, "kx_done", g + 1))
                    if nmx >= 2:
                        e.wait_ge(*nth(p, "reduced", nmx - 1))
                    bank = 4 + nmx % 2
                    diag = qt // 4 == kh
                    mm = e.matmul(ps[:, bank, 0:w], qs[:, sl, P * qt:P * (qt + 1)], ks[:, sl, HALF * kh:HALF * kh + w],
                                  start=True, stop=not diag)
                    if diag:
                        o = ps[:, bank, P * (qt % 4):P * (qt % 4 + 1)]
                        if cfg["causal"]:
                            mm = e.matmul(o, ident_r[:, :], causal_r[:, :], start=False, stop=True)
                        else:
                            e.matmul(o, slope_h[:, par, j, :], dist_r[:, :], start=False, stop=False)
                            mm = e.matmul(o, slope_l[:, par, j, :], dist_r[:, :], start=False, stop=True)
                    mm.then_inc(s("max_banks"), 1)
                    nmx += 1
                elif kind == "maxend":
                    e.wait_ge(*nth(p, "nm_done", g + 1))
                    if nz >= 1:
                        e.wait_ge(*nth(p, "z_norm", nz))
                    for half in range(HALVES):
                        if half:
                            e.wait_ge(*nth(p, "mh_done", 2 * g + 1))
                            e.wait_ge(*nth(p, "ml_done", 2 * g + 1))
                        for t in range(4):
                            qt = 4 * half + t
                            mm = e.transpose(ps[0:QUAD, 7, P * t:P * (t + 1)], nm[:, par, QUAD * qt:QUAD * (qt + 1)],
                                             ident[:, :])
                        mm.then_inc(s("m_bank"), 1)
                elif kind == "score":
                    (qh, kt, off), pair, first = arg
                    if first and pair == 0:
                        e.wait_ge(*nth(p, "m_loaded", 16 * 8 * (g + 1)))
                    if nsc >= 2:
                        e.wait_ge(*nth(p, "exp_done", nsc - 1))
                    diag = kt // 4 == qh
                    for u in range(2):
                        j = 2 * pair + u
                        sl = QUAD * par + j
                        bank = 2 * (nsc % 2) + u
                        mm = e.matmul(ps[:, bank, off:HALF], ks[:, sl, P * kt:P * (kt + 1)],
                                      qs[:, sl, HALF * qh + off:HALF * (qh + 1)], start=True, stop=not diag)
                        if diag:
                            dcol = P * (kt - 4 * qh)
                            o = ps[:, bank, dcol:dcol + P]
                            if cfg["causal"]:
                                mm = e.matmul(o, causal_r[:, :], ident_r[:, :], start=False, stop=True)
                            else:
                                e.matmul(o, slope_h[:, par, j, :], dist_r[:, :], start=False, stop=False)
                                mm = e.matmul(o, slope_l[:, par, j, :], dist_r[:, :], start=False, stop=True)
                    mm.then_inc(s("score_banks"), 1)
                    nsc += 1
                elif kind == "pv":
                    (qh, kt, off), pair = arg
                    e.wait_ge(*nth(p, "exp_done", npv + 1))
                    if kt == 0 and pair == 0 and nz >= 1:
                        e.wait_ge(*nth(p, "z_raw", nz))
                    for u in range(2):
                        j = 2 * pair + u
                        mm = e.matmul(ps[32 * j:32 * (j + 1), 6, off:HALF], vaug[:, kt, QUAD * g + j, :],
                                      pt[:, npv % RING, u, off:HALF], start=(kt == 0), stop=(kt == cfg["last_kt"][qh]))
                    mm.then_inc(s("pv_done"), 1)
                    npv += 1
                else:
                    e.wait_ge(*nth(p, "z_raw", nz + 1))
                    e.wait_ge(*nth(p, "mh_done", cfg["mdone"][nz]))
                    e.wait_ge(*nth(p, "ml_done", cfg["mdone"][nz]))
                    if nz >= 1:
                        e.wait_ge(*nth(p, "z_norm", nz))
                    for t in range(4):
                        mm = e.transpose(ps[:, 7, P * t:P * (t + 1)], zraw[:, nz % 2, P * t:P * (t + 1)], ident[:, :])
                    mm.then_inc(s("z_bank"), 1)
                    nz += 1
            e.wait_ge(*nth(p, "z_norm", nz))
            e.wait_ge(*nth(p, "exp_done", nsc))
            pe_to_features(e, p, "z")
            e.wait_ge(*nth(p, "z_hi", 4))
            e.wait_ge(*nth(p, "z_lo", 4))
            e.wait_ge(*nth(p, "aw_split", 4))
            for m in range(KC):
                for half in range(HALVES):
                    tok = slice(HALF * half, HALF * (half + 1))
                    terms = three([(awo[:, 0, D * c + P * m:D * c + P * (m + 1)], awo[:, 1, D * c + P * m:D * c + P * (m + 1)],
                                    xz[:, c, tok], xz[:, KC + c, tok]) for c in range(KC)])
                    for k, (a, b) in enumerate(terms):
                        mm = e.matmul(ps[:, 2 * m + half, :], a, b, start=(k == 0), stop=(k == len(terms) - 1))
            mm.then_inc(s("sums"), 1)
            pe_finish(e, p)

        @block.tensor
        def _(e):
            e.wait_ge(consts, n_consts)
            e.wait_ge(setup, 7)
            for p, cfg in enumerate(phases):
                (pe_ffn if cfg["kind"] == "ffn" else pe_attn)(e, p, cfg)

        def act_to_features(e, p, tag):
            for k in range(4):
                half, c = k // 2, k % 2
                e.wait_ge(*nth(p, tag + "_banks", k + 1))
                e.activation(xz[:, c, HALF * half:HALF * (half + 1)], ps[:, 4 + 2 * c + half, :], ACT.Copy)\
                    .then_inc(s(tag + "_hi"), 1)

        def act_norm(e, p):
            e.wait_ge(*nth(p, "var", TILES))
            e.activation(std[:, :], mv[:, :, 1], ACT.Sqrt, bias=eps[:, 0:1]).then_inc(s("std"), 1)

        def act_finish(e, p, bias):
            e.wait_ge(*nth(p, "sums", 1))
            for o in range(0, 4, 2):
                if bias:
                    e.activation(ot[:, o, :], ps[:, o, :], ACT.Identity, bias=cols[:, 4 + o // 2:5 + o // 2])\
                        .then_inc(s("ot_done"), 1)
                else:
                    e.activation(ot[:, o, :], ps[:, o, :], ACT.Copy).then_inc(s("ot_done"), 1)

        def act_ffn(e, p, cfg):
            n, K, E = cfg["chunks"], cfg["topk"], cfg["experts"]

            def split_hi(c, b, pair, first=False):
                e.wait_ge(*nth(p, "w_loaded%d" % b, 16 * (pair + 1)))
                if not first:
                    e.wait_ge(*nth(p, "down_done", 2 * (c - 1)))
                e.activation(whi[:, b, :], wraw[:, b, :], ACT.Copy).then_inc(s("w_hi"), 1)

            def step(c, t):
                k = 2 * c + t
                e.wait_ge(*nth(p, "gate", k + 1))
                if not isinstance(k, int) or k >= 2:
                    e.wait_ge(*nth(p, "su_done", k - 1))
                e.activation(sg[:, t, :], ps[:, 4, :], ACT.Silu).then_inc(s("silu"), 1)
                e.wait_ge(*nth(p, "h_done", k + 1))
                if not isinstance(k, int) or k >= 2:
                    e.wait_ge(*nth(p, "down_done", k - 1))
                e.activation(hh[:, t, :], hf[:, t, :], ACT.Copy).then_inc(s("h_hi"), 1)

            act_norm(e, p)
            act_to_features(e, p, "ln")
            split_hi(0, 0, 0, True)
            split_hi(1, 1, 0, True)
            e.wait_ge(*nth(p, "dv_done", 1))
            e.activation(ev[:, :, 0:K], dv[:, :, 0:K], ACT.Exp).then_inc(s("exps"), 1)
            if cfg["gated"]:
                e.wait_ge(*nth(p, "dl_done", 1))
                e.activation(el[:, :, 0:E], dl[:, :, 0:E], ACT.Exp).then_inc(s("exps"), 1)
                e.activation(zg[:, :], lg[:, :, E], ACT.Exp, scale=-1.0).then_inc(s("exps"), 1)
            e.wait_ge(*nth(p, "cw_banks", 1))
            for k in range(2):
                e.activation(cwT[0:RC, HALF * k:HALF * (k + 1)], ps[0:RC, 6 + k, :], ACT.Copy).then_inc(s("cwT_hi"), 1)
            step(0, 0)
            step(0, 1)
            last = n - 1 - (n - 1) % 2
            with e.Fori(0, (n - 1) // 2 - 1) as i:
                for u in range(2):
                    split_hi(2 * i + 2 + u, u, i + 1)
                    step(2 * i + 1 + u, 0)
                    step(2 * i + 1 + u, 1)
            for c in range(n - 2 if n % 2 else n - 3, n):
                if c + 1 < n:
                    split_hi(c + 1, (c + 1) % 2, (c + 1) // 2)
                step(c, 0)
                step(c, 1)
            act_finish(e, p, False)

        def act_attn(e, p, cfg):
            act_norm(e, p)
            act_to_features(e, p, "ln")
            for k in range(8):
                w, m, half = k // 4, (k // 2) % 2, k % 2
                e.wait_ge(*nth(p, "tmp_q", k + 1))
                e.activation(chi[:, w, m, HALF * half:HALF * (half + 1)], tmp[:, k % 2, :], ACT.Copy)\
                    .then_inc(s("hi_q"), 1)
            if cfg["causal"]:
                for t in range(TILES):
                    e.wait_ge(*nth(p, "v_banks", t + 1))
                    if t == 0:
                        e.wait_ge(*nth(p, "v_init", 1))
                    e.activation(vaug[:, t, :, 0:HD], ps[:, 4 + t % 4, 0:D].rearrange("p (h d) -> p h d", d=HD), ACT.Copy)\
                        .then_inc(s("v_done"), 1)
            nsc = nz = npv = 0
            for kind, g, arg in cfg["order"]:
                if kind == "maxend":
                    if g >= 1:
                        e.wait_ge(*nth(p, "m_loaded", 16 * 8 * g))
                    for half in range(HALVES):
                        e.wait_ge(*nth(p, "m_bank", 2 * g + half + 1))
                        e.activation(mhl[0:QUAD, HALF * half:HALF * (half + 1)], ps[0:QUAD, 7, :], ACT.Copy)\
                            .then_inc(s("mh_done"), 1)
                elif kind == "score":
                    (qh, kt, off), pair, _ = arg
                    e.wait_ge(*nth(p, "score_banks", nsc + 1))
                    if nsc >= RING:
                        e.wait_ge(*nth(p, "pv_done", nsc - RING + 1))
                    b = 2 * (nsc % 2)
                    e.activation(pt[:, nsc % RING, :, off:HALF], ps[:, b:b + 2, off:HALF], ACT.Exp)\
                        .then_inc(s("exp_done"), 1)
                    nsc += 1
                elif kind == "z":
                    npv = cfg["z_pv"][nz]
                    e.wait_ge(*nth(p, "pv_done", npv))
                    if nz >= 2:
                        e.wait_ge(*nth(p, "z_bank", nz - 1))
                    e.activation(zraw[:, nz % 2, :], ps[:, 6, :], ACT.Copy).then_inc(s("z_raw"), 1)
                    nz += 1
            act_to_features(e, p, "z")
            act_finish(e, p, not cfg["causal"])

        @block.scalar
        def _(e):
            e.wait_ge(setup, 7)
            for p, cfg in enumerate(phases):
                (act_ffn if cfg["kind"] == "ffn" else act_attn)(e, p, cfg)

        def dve_to_features(e, p, tag):
            for k in range(4):
                half, c = k // 2, k % 2
                e.wait_ge(*nth(p, tag + "_hi", k + 1))
                sl = slice(HALF * half, HALF * (half + 1))
                e.tensor_tensor(xz[:, KC + c, sl], ps[:, 4 + 2 * c + half, :], hi_f(xz[:, c, sl]), ALU.subtract)\
                    .then_inc(s(tag + "_lo"), 1)

        def dve_norm(e, p):
            for t in range(TILES):
                if p == 0 and t == 0:
                    e.wait_ge(x_loaded, 16)
                elif p > 0:
                    e.wait_ge(*nth(p, "x_added", t // 2 + 1))
                e.bn_stats(stats[:, t, :], x[:, t, :]).then_inc(s("bn"), 1)
            for t in range(TILES):
                e.wait_ge(*nth(p, "bn", t + 1))
                e.bn_aggr(mv[:, t, :], stats[:, t, :]).then_inc(s("var"), 1)
            e.wait_ge(*nth(p, "std", 1))
            e.reciprocal(rstd[:, :], std[:, :]).then_inc(s("rstd"), 1)
            e.wait_ge(*nth(p, "rstd", 1))
            for t in range(TILES):
                e.tensor_scalar(xn[:, t, :], x[:, t, :], mv[:, t, 0:1], rstd[:, t:t + 1], ALU.subtract, ALU.mult)\
                    .then_inc(s("ln_in"), 1)

        def dve_finish(e, p):
            for o in (1, 3):
                e.wait_ge(*nth(p, "sums", 1))
                if phases[p]["kind"] == "attn" and not phases[p]["causal"]:
                    e.tensor_scalar(ot[:, o, :], ps[:, o, :], cols[:, 4 + o // 2:5 + o // 2], None, ALU.add)\
                        .then_inc(s("ot_done"), 1)
                else:
                    e.tensor_copy(ot[:, o, :], ps[:, o, :]).then_inc(s("ot_done"), 1)
            for b in range(4):
                e.wait_ge(*nth(p, "out_banks", b + 1))
                xx = x[:, 2 * b:2 * b + 2, :].rearrange("p t d -> p (t d)")
                e.tensor_tensor(xx, ps[:, 4 + b, :], xx, ALU.add).then_inc(s("x_added"), 1)

        def dve_ffn(e, p, cfg):
            n, K, E = cfg["chunks"], cfg["topk"], cfg["experts"]
            dve_norm(e, p)
            dve_to_features(e, p, "ln")
            ch, cnt = s("router_step"), router_steps

            def did(ins):
                cnt[0] += 1
                ins.then_inc(ch, 1)

            def settle():
                e.wait_ge(ch, cnt[0])

            if p == 0 or phases[p - 1]["kind"] == "attn":
                did(e.memset(hi_f(cwT[:, :]), 0.0))
            did(e.memset(cw[:, :, :], 0.0))
            e.wait_ge(*nth(p, "logits", 1))
            did(e.tensor_copy(lg[:, :, :], ps[:, 7, 0:TILES * RC].rearrange("p (t r) -> p t r", r=RC)))
            settle()
            for t in range(TILES):
                did(e.max(top8[:, t, :], lg[:, t, 0:E]))
            settle()
            best = top8[:, :, 0:1]
            e.tensor_tensor(dv[:, :, 0:K], top8[:, :, 0:K], best.to_broadcast([P, TILES, K]), ALU.subtract)\
                .then_inc(s("dv_done"), 1)
            if cfg["gated"]:
                e.tensor_tensor(dl[:, :, 0:E], lg[:, :, 0:E], best.to_broadcast([P, TILES, E]), ALU.subtract)\
                    .then_inc(s("dl_done"), 1)
            for t in range(TILES):
                did(e.max_index(idx8[:, t, :], top8[:, t, :], lg[:, t, 0:E]))
            settle()
            did(e.tensor_copy(idxf[:, :, :], idx8[:, :, :]))
            settle()
            oh = onehot[:, 0:TILES * K, 0:E].rearrange("p (t k) e -> p t k e", k=K)
            ow = onew[:, 0:TILES * K, 0:E].rearrange("p (t k) e -> p t k e", k=K)
            did(e.tensor_tensor(oh, idxf[:, :, 0:K].unsqueeze(3).to_broadcast([P, TILES, K, E]),
                                iota[:, 0:E].unsqueeze(1).unsqueeze(1).to_broadcast([P, TILES, K, E]), ALU.is_equal))
            e.wait_ge(*nth(p, "exps", 3 if cfg["gated"] else 1))
            if cfg["gated"]:
                did(e.tensor_reduce(ssum[:, :], el[:, :, 0:E], AX.X, ALU.add))
                did(e.tensor_scalar(zg1[:, :], zg[:, :], 1.0, None, ALU.add))
            else:
                did(e.tensor_reduce(ssum[:, :], ev[:, :, 0:K], AX.X, ALU.add))
            settle()
            did(e.reciprocal(rsum[:, :], ssum[:, :]))
            if cfg["gated"]:
                did(e.reciprocal(zg2[:, :], zg1[:, :]))
            settle()
            did(e.scalar_tensor_tensor(wk[:, :, 0:K], ev[:, :, 0:K], cfg["moe_scale"],
                                       rsum[:, :].unsqueeze(2).to_broadcast([P, TILES, K]), ALU.mult, ALU.mult))
            if cfg["gated"]:
                did(e.tensor_scalar(cw[:, :, E], zg2[:, :], cfg["shared_scale"], None, ALU.mult))
            else:
                did(e.memset(cw[:, :, E:E + 1], cfg["shared_scale"]))
            settle()
            did(e.tensor_tensor(ow, oh, wk[:, :, 0:K].unsqueeze(3).to_broadcast([P, TILES, K, E]), ALU.mult))
            settle()
            e.tensor_reduce(cw[:, :, 0:E], ow.rearrange("p t k e -> p t e k"), AX.X, ALU.add)\
                .then_inc(s("cw_done"), 1)
            for k in range(2):
                e.wait_ge(*nth(p, "cwT_hi", k + 1))
                sl = slice(HALF * k, HALF * (k + 1))
                e.tensor_tensor(cwT[RC:2 * RC, sl], ps[0:RC, 6 + k, :], hi_f(cwT[0:RC, sl]), ALU.subtract)\
                    .then_inc(s("cwT_lo"), 1)

            def step(c, t):
                k = 2 * c + t
                e.wait_ge(*nth(p, "up", k + 1))
                e.wait_ge(*nth(p, "silu", k + 1))
                e.tensor_tensor(su[:, t, :], ps[:, 5, :], sg[:, t, :], ALU.mult).then_inc(s("su_done"), 1)
                e.wait_ge(*nth(p, "comb", k + 1))
                e.wait_ge(*nth(p, "su_done", k + 1))
                if not isinstance(k, int) or k >= 2:
                    e.wait_ge(*nth(p, "h_hi", k - 1))
                e.tensor_tensor(hf[:, t, :], ps[:, 6, :], su[:, t, :], ALU.mult).then_inc(s("h_done"), 1)
                e.wait_ge(*nth(p, "h_hi", k + 1))
                if not isinstance(k, int) or k >= 2:
                    e.wait_ge(*nth(p, "down_done", k - 1))
                e.tensor_tensor(hl[:, t, :], hf[:, t, :], hi_f(hh[:, t, :]), ALU.subtract).then_inc(s("h_lo"), 1)

            step(0, 0)
            step(0, 1)
            with e.Fori(0, (n - 1) // 2) as i:
                for u in range(2):
                    step(2 * i + 1 + u, 0)
                    step(2 * i + 1 + u, 1)
            if n % 2 == 0:
                step(n - 1, 0)
                step(n - 1, 1)
            dve_finish(e, p)

        def dve_attn(e, p, cfg):
            dve_norm(e, p)
            dve_to_features(e, p, "ln")
            for k in range(8):
                w, m, half = k // 4, (k // 2) % 2, k % 2
                e.wait_ge(*nth(p, "qk_banks", k + 1))
                if k >= 2:
                    e.wait_ge(*nth(p, "lo_q", k - 1))
                    e.wait_ge(*nth(p, "hi_q", k - 1))
                scale = HD ** -0.5 if w == 0 else 1.0
                if cfg["causal"]:
                    e.tensor_scalar(tmp[:, k % 2, :], ps[:, k % 4, :], scale, None, ALU.mult).then_inc(s("tmp_q"), 1)
                else:
                    e.tensor_scalar(tmp[:, k % 2, :], ps[:, k % 4, :], cols[:, 2 * w + m:2 * w + m + 1], scale,
                                    ALU.add, ALU.mult).then_inc(s("tmp_q"), 1)
                sl = slice(HALF * half, HALF * (half + 1))
                e.wait_ge(*nth(p, "hi_q", k + 1))
                e.tensor_tensor(clo[:, w, m, sl], tmp[:, k % 2, :], hi_f(chi[:, w, m, sl]), ALU.subtract)\
                    .then_inc(s("lo_q"), 1)
            if not cfg["causal"]:
                for t in range(TILES):
                    e.wait_ge(*nth(p, "v_banks", t + 1))
                    if t == 0:
                        e.wait_ge(*nth(p, "v_init", 1))
                    e.tensor_tensor(vaug[:, t, :, 0:HD], ps[:, 4 + t % 4, 0:D].rearrange("p (h d) -> p h d", d=HD),
                                    bvb[:, :].rearrange("p (h d) -> p h d", d=HD), ALU.add).then_inc(s("v_done"), 1)
            else:
                e.memset(nmax[:, :, 1], BIG).then_inc(s("nmax_init"), 1)
                e.wait_ge(*nth(p, "nmax_init", 1))
            nmx = nz = 0
            for kind, g, arg in cfg["order"]:
                if kind == "max":
                    j, qt, kh, w = arg
                    e.wait_ge(*nth(p, "max_banks", nmx + 1))
                    if nmx % cfg["nitems"] == 0 and g >= 1:
                        e.wait_ge(*nth(p, "nm_done", g))
                    e.tensor_reduce(nmax[:, QUAD * qt + j, kh:kh + 1], ps[:, 4 + nmx % 2, 0:w], AX.X, ALU.max,
                                    negate=True).then_inc(s("reduced"), 1)
                    nmx += 1
                elif kind == "maxend":
                    e.wait_ge(*nth(p, "reduced", nmx))
                    if g >= 2:
                        e.wait_ge(*nth(p, "m_bank", 2 * (g - 1)))
                    e.tensor_tensor(nm[:, g % 2, :], nmax[:, :, 0], nmax[:, :, 1], ALU.min).then_inc(s("nm_done"), 1)
                    if g >= 1:
                        e.wait_ge(*nth(p, "m_loaded", 16 * 8 * g))
                    for half in range(HALVES):
                        e.wait_ge(*nth(p, "mh_done", 2 * g + half + 1))
                        sl = slice(HALF * half, HALF * (half + 1))
                        e.tensor_tensor(mhl[RC:RC + QUAD, sl], ps[0:QUAD, 7, :], hi_f(mhl[0:QUAD, sl]), ALU.subtract)\
                            .then_inc(s("ml_done"), 1)
                elif kind == "z":
                    e.wait_ge(*nth(p, "z_bank", nz + 1))
                    den = ps[:, 7, :].rearrange("p (a r) -> p a r", r=32)
                    e.reciprocal(rden[:, nz % 2, :], den[:, :, HD]).then_inc(s("rden"), 1)
                    e.wait_ge(*nth(p, "rden", nz + 1))
                    qh = arg
                    e.tensor_tensor(xn[:, 4 * qh:4 * qh + 4, QUAD * HD * g:QUAD * HD * (g + 1)].rearrange(
                                        "p t (j d) -> p t j d", d=HD),
                                    ps[:, 7, :].rearrange("p (t j r) -> p t j r", t=4, r=32)[:, :, :, 0:HD],
                                    rden[:, nz % 2, :].rearrange("p (t j) -> p t j", t=4).unsqueeze(3)
                                    .to_broadcast([P, 4, QUAD, HD]), ALU.mult).then_inc(s("z_norm"), 1)
                    nz += 1
            e.wait_ge(*nth(p, "z_norm", nz))
            e.sem_inc(s("z_in"), 8)
            dve_to_features(e, p, "z")
            dve_finish(e, p)

        @block.vector
        def _(e):
            e.memset(eps[:, :], EPS).then_inc(setup, 1)
            e.memset(hi_f(zero_r[:, :]), 0.0).then_inc(setup, 1)
            e.wait_ge(consts, n_consts)
            e.tensor_copy(ident_r[:, :], ident[:, :]).then_inc(setup, 1)
            e.tensor_copy(dist_r[:, :], dist[:, :]).then_inc(setup, 1)
            e.tensor_copy(causal_r[:, :], causal[:, :]).then_inc(setup, 1)
            e.tensor_copy(wrh[:, 0, :, :], wr0[:, :, :]).then_inc(wr_hi, 1)
            e.tensor_copy(wrh[:, 1, :, :], wr1[:, :, :]).then_inc(wr_hi, 1)
            e.wait_ge(wr_hi, 2)
            e.tensor_tensor(wrl[:, 0, :, :], wr0[:, :, :], hi_f(wrh[:, 0, :, :]), ALU.subtract).then_inc(setup, 1)
            e.tensor_tensor(wrl[:, 1, :, :], wr1[:, :, :], hi_f(wrh[:, 1, :, :]), ALU.subtract).then_inc(setup, 1)
            for p, cfg in enumerate(phases):
                (dve_ffn if cfg["kind"] == "ffn" else dve_attn)(e, p, cfg)

        def pool_ffn(e, p, cfg):
            n = cfg["chunks"]

            def split_lo(c, b, first=False):
                e.wait_ge(*nth(p, "w_hi", c + 1))
                if not first:
                    e.wait_ge(*nth(p, "down_done", 2 * (c - 1)))
                e.tensor_tensor(wlo[:, b, :], wraw[:, b, 0:WSEL], hi_f(whi[:, b, 0:WSEL]), ALU.subtract)\
                    .then_inc(s("w_lo"), 1)

            split_lo(0, 0, True)
            split_lo(1, 1, True)
            with e.Fori(0, (n - 2) // 2) as i:
                for b in range(2):
                    split_lo(2 * i + 2 + b, b)
            if n % 2:
                split_lo(n - 1, (n - 1) % 2)

        def pool_attn(e, p, cfg):
            steps, cnt = s("pool_step"), pool_steps

            def did(ins):
                cnt[0] += 1
                ins.then_inc(steps, 1)

            def settle():
                e.wait_ge(steps, cnt[0])

            if p > 0:
                e.wait_ge(*nth(p - 1, "sums", 1))
                e.wait_ge(*nth(p - 1, "out_banks", 4))
            e.dma_start(kx[:, :], A["kx"]).then_inc(s("kx_loaded"), 16)
            e.dma_start(kxs[:, :], A["qx"]).then_inc(s("kx_loaded"), 16)
            e.sem_inc(s("region_free"), 1)
            def split(w):
                e.wait_ge(*nth(p, "aw_loaded%d" % (w % 2), 16 * (w // 2 + 1)))
                h_, l_ = (awh[:, w, :], awl[:, w, :]) if w < 3 else (awo[:, 0, :], awo[:, 1, :])
                did(e.tensor_copy(h_, araw[:, w % 2, :]))
                settle()
                did(e.tensor_tensor(l_, araw[:, w % 2, :], hi_f(h_), ALU.subtract))
                settle()
                e.sem_inc(s("aw_split"), 1)

            for w in range(3):
                split(w)
            did(e.memset(vaug[:, :, :, :], 0.0))
            settle()
            e.memset(vaug[:, :, :, HD:HD + 1], 1.0).then_inc(s("v_init"), 1)
            e.wait_ge(*nth(p, "v_init", 1))
            for half in range(2):
                for q in (ks, qs):
                    did(e.memset(hi_f(q[:, 4 * half:4 * half + 4, :]), 0.0))
            settle()
            e.sem_inc(s("slots_zeroed"), 1)
            split(3)
            e.wait_ge(*nth(p, "kx_loaded", 32))
            if not cfg["causal"]:
                for sl in range(2 * QUAD):
                    did(e.tensor_copy(qs[QX:P, sl, :], kxs[QX:P, :]))
                    settle()
                did(e.tensor_scalar(srow[:, :], slopes[:, :], keep[:, 0:1], keep[:, 1:2], ALU.mult, ALU.add))
                settle()
            e.sem_inc(s("qx_done"), 1)
            for g in range(QUADS):
                par = g % 2
                if g >= 2:
                    e.wait_ge(*nth(p, "score_banks", 2 * cfg["nsteps"] * (g - 1)))
                    e.sem_inc(s("p_quad_done"), 1)
                for j in range(QUAD):
                    h, sl = QUAD * g + j, QUAD * par + j
                    if cfg["causal"]:
                        did(e.tensor_copy(ks[QX:QX + 32, sl, :], kx[QX:QX + 32, :]))
                        settle()
                        continue
                    did(e.tensor_scalar(slope_i[:, par, j, :], ident[:, :], slopes[:, h:h + 1], None, ALU.mult))
                    settle()
                    did(e.tensor_copy(slope_h[:, par, j, :], slope_i[:, par, j, :]))
                    settle()
                    did(e.tensor_tensor(slope_l[:, par, j, :], slope_i[:, par, j, :], hi_f(slope_h[:, par, j, :]),
                                        ALU.subtract))
                    settle()
                    did(e.tensor_scalar(kxs[QX:QX + 32, :], kx[QX:QX + 32, :], srow[QX:QX + 32, h:h + 1], None, ALU.mult))
                    settle()
                    did(e.tensor_copy(ks[QX:QX + 32, sl, :], kxs[QX:QX + 32, :]))
                    settle()
                    did(e.tensor_tensor(ks[QX + 32:P, sl, :], kxs[QX:QX + 32, :], hi_f(ks[QX:QX + 32, sl, :]),
                                        ALU.subtract))
                    settle()
                e.sem_inc(s("kx_done"), 1)

        @block.gpsimd
        def _(e):
            e.wait_ge(consts, n_consts)
            for p, cfg in enumerate(phases):
                (pool_ffn if cfg["kind"] == "ffn" else pool_attn)(e, p, cfg)


def position_tables(np):
    i = np.arange(P)
    ident = np.eye(P, dtype=np.float32)
    dist = -np.abs(i[:, None] - i[None, :]).astype(np.float32)
    causal = np.where(i[None, :] > i[:, None], np.float32(-2.0 ** 127), np.float32(0)).astype(np.float32)
    iota = np.ascontiguousarray(np.broadcast_to(np.arange(16, dtype=np.float32), (P, 16)))
    t = np.arange(T)
    tile = t // P
    qx = np.zeros((P, T), np.float32)
    kx = np.zeros((P, T), np.float32)
    for c in range(TILES):
        centre = P * c + P // 2
        side = np.sign(tile - c).astype(np.float32)
        for base in (QX, QX + 32):
            qx[base + c] = -np.abs(t - centre) * np.abs(side)
            qx[base + TILES + c] = side
        kx[QX + c] = tile == c
        kx[QX + TILES + c] = (t - centre) * (tile == c)
    kx[MROW:MROW + 2] = 1.0
    keep = np.zeros((P, 2), np.float32)
    keep[QX:MROW, 0] = 1.0
    keep[MROW:, 1] = 1.0
    return dict(ident=ident, dist=dist, causal=causal, iota=iota, qx=qx, kx=kx, keep=keep)


def pack_ffn(np, wg, wu, wd, sg, su, sd, experts, hidden, chunks):
    pad = chunks * P
    n = experts * hidden
    G, U = np.zeros((D, pad), np.float32), np.zeros((D, pad), np.float32)
    W = np.zeros((pad, D), np.float32)
    sel = np.zeros((P, pad), np.float32)
    m = n + sg.shape[1]
    G[:, :n] = wg.transpose(1, 0, 2).reshape(D, n)
    U[:, :n] = wu.transpose(1, 0, 2).reshape(D, n)
    G[:, n:m], U[:, n:m] = sg, su
    W[:n], W[n:m] = wd.reshape(n, D), sd
    for e in range(experts):
        sel[[e, RC + e], e * hidden:(e + 1) * hidden] = 1.0
    sel[[experts, RC + experts], n:m] = 1.0
    out = np.zeros((chunks, P, WCOLS), np.float32)
    for c in range(chunks):
        s = slice(c * P, (c + 1) * P)
        out[c, :, WG:WG + P], out[c, :, WG + P:WU] = G[:P, s], G[P:, s]
        out[c, :, WU:WU + P], out[c, :, WU + P:WD] = U[:P, s], U[P:, s]
        out[c, :, WD:WSEL] = W[s]
        out[c, :, WSEL:] = sel[:, s]
    return out


PLAN = ["f0", "a0", "f0", "f1", "a1", "f1"]


def kernel(**inputs):
    import numpy as _np
    import concourse.bacc as _bacc
    from concourse.bass_utils import run_bass_kernel_spmd as _run

    I = {k: _np.asarray(v) for k, v in inputs.items()}

    def chunked(w):
        return _np.ascontiguousarray(w.reshape(KC, P, -1).transpose(1, 0, 2))

    def router(*ws):
        r = _np.zeros((D, RC), _np.float32)
        c = 0
        for w in ws:
            r[:, c:c + w.shape[1]] = w
            c += w.shape[1]
        return chunked(r)

    def attn(*ws):
        return _np.stack([chunked(w.T).reshape(P, KC * D) for w in ws])

    arrays = position_tables(_np)
    arrays["x"] = I["L0_attn_x"]
    arrays["wr0"] = router(I["L0_ffn_Wr"], I["L0_ffn_Wsg"])
    arrays["wr1"] = router(I["L1_ffn_w_router"])
    cols = _np.zeros((P, 8), _np.float32)
    for k, name in enumerate(("bq", "bk", "bo")):
        cols[:, 2 * k:2 * k + 2] = I["L0_attn_" + name].reshape(KC, P).T
    arrays["cols"] = cols
    arrays["bvb"] = _np.ascontiguousarray(_np.broadcast_to(I["L0_attn_bv"], (P, D)))
    arrays["slopes"] = _np.ascontiguousarray(_np.broadcast_to(I["L0_attn_slopes"], (P, NH)))
    arrays["f0"] = pack_ffn(_np, I["L0_ffn_Wg"], I["L0_ffn_Wu"], I["L0_ffn_Wd"], I["L0_ffn_Sg"], I["L0_ffn_Su"],
                            I["L0_ffn_Sd"], FFN0["experts"], 176, FFN0["chunks"])
    arrays["f1"] = pack_ffn(_np, I["L1_ffn_we1"], I["L1_ffn_we3"], I["L1_ffn_we2"], I["L1_ffn_ws1"], I["L1_ffn_ws3"],
                            I["L1_ffn_ws2"], FFN1["experts"], 128, FFN1["chunks"])
    arrays["a0"] = attn(*(I["L0_attn_W" + c] for c in "qkvo"))
    arrays["a1"] = attn(*(I["L1_attn_W" + c] for c in "qkvo"))

    kinds = {
        "f0": dict(kind="ffn", w="f0", router=0, moe_scale=0.5, shared_scale=0.5, **FFN0),
        "f1": dict(kind="ffn", w="f1", router=1, moe_scale=0.5 * 4 / 5, shared_scale=0.5 / 5, **FFN1),
        "a0": dict(kind="attn", w="a0", causal=False),
        "a1": dict(kind="attn", w="a1", causal=True),
    }
    nc = _bacc.Bacc("TRN2", target_bir_lowering=False, num_devices=1)
    A = {}
    for name, a in arrays.items():
        arrays[name] = a = _np.ascontiguousarray(a)
        A[name] = nc.dram_tensor(f"in_{name}", a.shape, F32, kind="ExternalInput").ap()
    out = nc.dram_tensor("out_x", (1, T, D), F32, kind="ExternalOutput").ap()
    program(nc, A, out, [dict(kinds[k]) for k in PLAN])
    r = _run(nc, [{f"in_{name}": a for name, a in arrays.items()}], core_ids=[0])
    return r.results[0]["out_x"]
```

```python
from contextlib import ExitStack

import concourse.bass as bass
from concourse import mybir

F32 = mybir.dt.float32
F32R = mybir.dt.float32r
U32 = mybir.dt.uint32
ALU = mybir.AluOpType
ACT = mybir.ActivationFunctionType
AX = mybir.AxisListType

P = 128
T = 1024
D = 256
TILES = T // P
KC = D // P
HALF = 512
HALVES = T // HALF
NH = 16
HD = D // NH
QUAD = 4
QUADS = NH // QUAD
SETS = 3
EPS = 1e-5
WG, WU, WD, WSEL = 0, 2 * P, 4 * P, 6 * P
WCOLS = 7 * P
RC = 32
QX = 64
MROW = 80
BIG = 3.0e38

FFN0 = dict(experts=8, topk=2, chunks=17, gated=True)
FFN1 = dict(experts=16, topk=4, chunks=20, gated=False)


def attention_order(causal):
    items = [(j, qt, kh, min(HALF, P * (qt + 1) - HALF * kh) if causal else HALF)
             for half in range(HALVES) for j in range(QUAD) for qt in range(4 * half, 4 * half + 4)
             for kh in range(HALVES)]
    items = [it for it in items if it[3] > 0]
    nhalf = [sum(it[1] // 4 == half for it in items) for half in range(HALVES)]
    steps = [(qh, kt, max(0, kt - 4 * qh) * P if causal else 0)
             for qh in range(HALVES) for kt in range(4 * qh + 4 if causal else TILES)]
    last_kt = [max(kt for qh, kt, _ in steps if qh == h) for h in range(HALVES)]
    def maxima(g):
        half0 = [("max", g, it) for it in items[:nhalf[0]]]
        half1 = [("max", g, it) for it in items[nhalf[0]:]]
        return half0 + [("maxend", g, 0)] + half1 + [("maxend", g, 1)]

    order = maxima(0)
    pairs = [(g, st, pair) for g in range(QUADS) for st in steps for pair in range(2)]
    per_quad = 2 * len(steps)
    for n, (g, st, pair) in enumerate(pairs):
        if n % per_quad == 0:
            left = maxima(g + 1) if g + 1 < QUADS else []
            total, given = len(left), 0
        order.append(("score", g, (st, pair, st[1] == 0 and pair == 0)))
        upto = total * (n % per_quad + 1) // (per_quad - 1)
        order += left[given:upto]
        given = max(given, upto)
        if n:
            g2, st2, pair2 = pairs[n - 1]
            order.append(("pv", g2, (st2, pair2)))
            if pair2 == 1 and st2[1] == last_kt[st2[0]]:
                order.append(("z", g2, st2[0]))
    order += [("pv", g, (st, pair)), ("z", g, st[0])]

    at_z = [n for n, (kind, _, _) in enumerate(order) if kind == "z"]
    return dict(order=order, nitems=len(items), nsteps=len(steps), last_kt=last_kt, pairs=len(pairs),
                z_pv=[sum(k == "pv" for k, _, _ in order[:n]) for n in at_z],
                mdone=[sum(k == "maxend" for k, _, _ in order[:n]) for n in at_z])


def signals(cfg):
    each = dict(x_added=4, bn=TILES, var=TILES, std=1, rstd=1, ln_in=TILES, ln_banks=4, ln_hi=4, ln_lo=4,
                sums=1, ot_done=4, out_banks=4)
    if cfg["kind"] == "ffn":
        n = cfg["chunks"]
        steps = dict.fromkeys(("gate", "up", "silu", "su_done", "comb", "h_done", "h_hi", "h_lo", "down_done"), 2 * n)
        return dict(each, w_loaded0=16 * ((n + 1) // 2), w_loaded1=16 * (n // 2), w_hi=n, w_lo=n, logits=1, dv_done=1,
                    dl_done=int(cfg["gated"]), exps=3 if cfg["gated"] else 1, cw_done=1, cw_banks=1, cwT_hi=2,
                    cwT_lo=2, **steps)
    nmax, quads, zs = QUADS * cfg["nitems"], QUADS, QUADS * HALVES
    ext = 0 if cfg["causal"] else 3
    return dict(each, aw_loaded0=32, aw_loaded1=32, aw_split=4, v_init=1, region_free=1, ext_loaded=16 * (3 if cfg["causal"] else 1),
                rows_loaded0=16 * (8 + ext), rows_loaded1=16 * (8 + ext), rows_loaded2=16 * (8 + ext),
                rows_loaded3=16 * (9 + ext), hi_stored0=64, hi_stored1=64, lo_stored0=64, lo_stored1=64,
                m_loaded0=16 * 2 * NH, m_loaded1=16 * 2 * NH, qk_banks=8, tmp_q=8, hi_q=8, lo_q=8,
                v_banks=TILES, v_done=TILES, nmax_init=int(cfg["causal"]), max_banks=nmax, reduced=nmax,
                nm_done=2 * quads, m_bank=2 * quads, mh_done=2 * quads, ml_done=2 * quads, score_banks=cfg["pairs"],
                exp_done=cfg["pairs"], pv_done=cfg["pairs"], z_raw=zs, z_bank=zs, rden=zs, z_norm=zs, z_in=TILES,
                z_banks=4, z_hi=4, z_lo=4)


def program(nc, A, out, phases):
    for cfg in phases:
        if cfg["kind"] == "attn":
            cfg.update(attention_order(cfg["causal"]))
    ctx = ExitStack()
    with ctx:
        def sb(name, shape, dt=F32, stack=ctx):
            return stack.enter_context(nc.sbuf_tensor(name, shape, dt))

        def sem(name):
            return ctx.enter_context(nc.semaphore(name))

        ps = ctx.enter_context(nc.psum_tensor("ps", [P, 8, 512], F32))

        x = sb("x", [P, TILES, D])
        early = ExitStack()
        ot = sb("ot", [P, 4, HALF], F32, early)
        early.close()
        xz = sb("xz", [P, 2 * KC, T], F32R)
        xn = sb("xn", [P, TILES, D])
        ident = sb("ident", [P, P])
        dist = sb("dist", [P, P])
        causal = sb("causal", [P, P])
        iota = sb("iota", [P, 16])
        eps = sb("eps", [P, 1])
        zero_r = sb("zero_r", [P, HALF], F32R)
        ident_r = sb("ident_r", [P, P], F32R)
        dist_r = sb("dist_r", [P, P], F32R)
        causal_r = sb("causal_r", [P, P], F32R)
        wr0 = sb("wr0", [P, KC, RC])
        wr1 = sb("wr1", [P, KC, RC])
        wrh = sb("wrh", [P, 2, KC, RC], F32R)
        wrl = sb("wrl", [P, 2, KC, RC], F32R)
        stats = sb("stats", [P, TILES, 6])
        mv = sb("mv", [P, TILES, 2])
        std = sb("std", [P, TILES])
        rstd = sb("rstd", [P, TILES])
        cols = sb("cols", [P, 8])
        bvb = sb("bvb", [P, D])
        slopes = sb("slopes", [P, NH])
        keep = sb("keep", [P, 2])
        srow4 = sb("srow4", [P, QUADS])
        slope4 = sb("slope4", [P, QUADS])

        awo = sb("awo", [P, 2, KC * D], F32R)
        early = ExitStack()
        awh = sb("awh", [P, 3, KC * D], F32R, early)
        awl = sb("awl", [P, 3, KC * D], F32R, early)
        early.close()
        RING = 3
        pt = sb("pt", [P, RING, 2, HALF])
        early = ExitStack()
        araw = sb("araw", [P, 2, KC * D], F32, early)
        early.close()
        zraw = sb("zraw", [P, 2, HALF])
        vaug = sb("vaug", [P, TILES, NH, 32])

        ffn = ExitStack()
        wraw = sb("wraw", [P, 2, WCOLS], F32, ffn)
        whi = sb("whi", [P, 2, WCOLS], F32R, ffn)
        wlo = sb("wlo", [P, 2, WSEL], F32R, ffn)
        sg = sb("sg", [P, 2, HALF], F32, ffn)
        su = sb("su", [P, 2, HALF], F32, ffn)
        hf = sb("hf", [P, 2, HALF], F32, ffn)
        hh = sb("hh", [P, 2, HALF], F32R, ffn)
        hl = sb("hl", [P, 2, HALF], F32R, ffn)
        cwT = sb("cwT", [P, T], F32R, ffn)
        lg = sb("lg", [P, TILES, RC], F32, ffn)
        top8 = sb("top8", [P, TILES, 8], F32, ffn)
        idx8 = sb("idx8", [P, TILES, 8], U32, ffn)
        idxf = sb("idxf", [P, TILES, 8], F32, ffn)
        dl = sb("dl", [P, TILES, RC], F32, ffn)
        el = sb("el", [P, TILES, RC], F32, ffn)
        ev = sb("ev", [P, TILES, 4], F32, ffn)
        dv = sb("dv", [P, TILES, 4], F32, ffn)
        wk = sb("wk", [P, TILES, 4], F32, ffn)
        ssum = sb("ssum", [P, TILES], F32, ffn)
        rsum = sb("rsum", [P, TILES], F32, ffn)
        zg = sb("zg", [P, TILES], F32, ffn)
        zg1 = sb("zg1", [P, TILES], F32, ffn)
        zg2 = sb("zg2", [P, TILES], F32, ffn)
        onehot = sb("onehot", [P, TILES * 4, 16], F32, ffn)
        onew = sb("onew", [P, TILES * 4, 16], F32, ffn)
        cw = sb("cw", [P, TILES, RC], F32, ffn)
        kx4 = sb("kx4", [P, T], F32, ffn)
        qxf = sb("qxf", [P, T], F32, ffn)
        qxr = sb("qxr", [P, T], F32R, ffn)
        kxp = sb("kxp", [P, 2, T], F32, ffn)
        kxh = sb("kxh", [P, QUADS, T], F32R, ffn)
        kxl = sb("kxl", [P, QUADS, T], F32R, ffn)
        slope_i = sb("slope_i", [P, NH, P], F32, ffn)
        slope_h = sb("slope_h", [P, NH, P], F32R, ffn)
        slope_l = sb("slope_l", [P, NH, P], F32R, ffn)
        ffn.close()

        qs = sb("qs", [P, SETS * QUAD, T], F32R)
        ks = sb("ks", [P, SETS * QUAD, T], F32R)
        chi = sb("chi", [P, 4, HALF], F32R)
        clo = sb("clo", [P, 4, HALF], F32R)
        early = ExitStack()
        tmp = sb("tmp", [P, 2, HALF], F32, early)
        early.close()
        mhl = sb("mhl", [RC + QUAD, T], F32R)
        sdiag = sb("sdiag", [P, SETS, 2, QUAD, P], F32R)
        nmax = sb("nmax", [P, QUAD * TILES, 2])
        nm = sb("nm", [P, 2, QUAD * TILES])
        rden = sb("rden", [P, 2, 16])

        def dram(name, shape):
            return nc.dram_tensor(name, shape, F32, kind="Internal").ap()

        qk_d = dram("qk_d", (2, 2, D, T))
        kext_d = dram("kext_d", (2, NH, 32, T))
        qext_d = dram("qext_d", (P - QX, T))
        sdiag_d = dram("sdiag_d", (2, P, NH * P))
        zero_d = dram("zero_d", (P - QX, HALF))

        S = {}
        router_steps, pool_steps = [0], [0]
        def s(name):
            if name not in S:
                S[name] = sem(name)
            return S[name]

        def nth(p, name, n):
            last = p - 1 if name == "x_added" else p
            return s(name), n + sum(signals(phases[q])[name] for q in range(last) if name in signals(phases[q]))

        consts = sem("consts_loaded")
        x_loaded = sem("x_loaded")
        wr_hi = sem("router_hi_split")
        setup = sem("setup_done")
        out_done = sem("out_written")
        srow_done = sem("slope_rows_done")
        slope_done = sem("slope_identity_done")
        slope_hi = sem("slope_identity_hi_done")
        kxp_done = sem("key_rows_done")
        kxh_done = sem("key_rows_hi_done")
        kxl_done = sem("key_rows_lo_done")
        qxr_done = sem("query_rows_done")
        tables = sem("tables_stored")

        def hi_f(ap):
            return ap.bitcast(F32)

        def three(pairs):
            r = []
            for a_h, a_l, b_h, b_l in pairs:
                r += [(a_h, b_h), (a_l, b_h), (a_h, b_l)]
            return r

        n_consts = 0
        const_loads = []
        for tile, name in ((ident, "ident"), (dist, "dist"), (causal, "causal"), (iota, "iota"), (cols, "cols"),
                           (bvb, "bvb"), (slopes, "slopes"), (keep, "keep")):
            const_loads.append((tile[:, :], A[name]))
        const_loads.append((slope4[:, :], A["slope4"]))
        const_loads.append((kx4[:, :], A["kx4"]))
        const_loads.append((qxf[QX:P, :], A["qx"]))
        const_loads.append((wr0[:, :, :], A["wr0"]))
        const_loads.append((wr1[:, :, :], A["wr1"]))
        n_consts = 16 * len(const_loads)

        attn_at = [p for p, cfg in enumerate(phases) if cfg["kind"] == "attn"]
        ready_in = {0 if n == 0 else attn_at[n - 1] + 1: p for n, p in enumerate(attn_at)}

        block = ctx.enter_context(nc.Block())
        nphase = len(phases)

        def sp_ffn(e, p, cfg):
            n = cfg["chunks"]
            w = A[cfg["w"]]

            def load(c, b):
                e.dma_start(wraw[:, b, :], w[bass.ds(c, 1), :, :].rearrange("o p n -> (o p) n"))\
                    .then_inc(s("w_loaded%d" % b), 16)

            if p > 0:
                prev = phases[p - 1]
                if prev["kind"] == "ffn":
                    e.wait_ge(*nth(p - 1, "w_hi", prev["chunks"]))
                    e.wait_ge(*nth(p - 1, "w_lo", prev["chunks"]))
                else:
                    e.wait_ge(*nth(p - 1, "pv_done", prev["pairs"]))
            load(0, 0)
            load(1, 1)
            if p in ready_in:
                load_attn_weights(e, ready_in[p], phases[ready_in[p]])
            with e.Fori(0, (n - 2) // 2) as i:
                for b in range(2):
                    e.wait_ge(*nth(p, "w_hi", 2 * i + b + 1))
                    e.wait_ge(*nth(p, "w_lo", 2 * i + b + 1))
                    load(2 * i + b + 2, b)
            if n % 2:
                e.wait_ge(*nth(p, "w_hi", n - 2))
                e.wait_ge(*nth(p, "w_lo", n - 2))
                load(n - 1, (n - 1) % 2)

        def load_attn_weights(e, p, cfg):
            if p != attn_at[0]:
                e.wait_ge(*nth(attn_at[attn_at.index(p) - 1], "sums", 1))
            for w in range(4):
                if w >= 2:
                    e.wait_ge(*nth(p, "aw_split", w - 1))
                e.dma_start(araw[:, w % 2, :], A[cfg["w"]][w, :, :]).then_inc(s("aw_loaded%d" % (w % 2)), 16)

        def sp_attn(e, p, cfg):
            e.wait_ge(*nth(p, "region_free", 1))
            halves = "p (s h) c -> p s h c"
            if cfg["causal"]:
                e.dma_start(hi_f(qs[QX:P, :, :]).rearrange("p s (h c) -> p (s h) c", h=2),
                            zero_d.unsqueeze(1).to_broadcast([P - QX, SETS * QUAD * 2, HALF])).then_inc(s("ext_loaded"), 16)
                for part in range(2):
                    e.dma_start(hi_f(ks[QX + 32 * part:QX + 32 * (part + 1), :, :]),
                                kext_d[part, 0, :, :].unsqueeze(1).to_broadcast([32, SETS * QUAD, T]))\
                        .then_inc(s("ext_loaded"), 16)
            else:
                e.dma_start(hi_f(qs[QX:P, :, :]), qext_d.unsqueeze(1).to_broadcast([P - QX, SETS * QUAD, T]))\
                    .then_inc(s("ext_loaded"), 16)
            for k in range(8):
                m, w, half = k // 4, (k // 2) % 2, k % 2
                for name, part, src in (("hi", 0, chi), ("lo", 1, clo)):
                    e.wait_ge(*nth(p, name + "_q", k + 1))
                    e.dma_start(qk_d[w, part, P * m:P * (m + 1), HALF * half:HALF * (half + 1)],
                                hi_f(src[:, k % 4, :])).then_inc(s("%s_stored%d" % (name, m)), 16)
            for g in range(QUADS):
                for half in range(HALVES):
                    e.wait_ge(*nth(p, "mh_done", 2 * g + half + 1))
                    e.wait_ge(*nth(p, "ml_done", 2 * g + half + 1))
                    sl = slice(HALF * half, HALF * (half + 1))
                    for j in range(QUAD):
                        for row in range(2):
                            e.dma_start(hi_f(qs[MROW + row:MROW + row + 1, QUAD * (g % SETS) + j, sl]),
                                        hi_f(mhl[RC * row + j:RC * row + j + 1, sl])).then_inc(s("m_loaded%d" % half), 16)

        @block.sync
        def _(e):
            e.dma_start(x[:, :, :], A["x"].rearrange("o (t p) d -> p (o t) d", p=P)).then_inc(x_loaded, 16)
            for dst, src in const_loads:
                e.dma_start(dst, src).then_inc(consts, 16)
            for p, cfg in enumerate(phases):
                if cfg["kind"] == "ffn":
                    sp_ffn(e, p, cfg)
                else:
                    sp_attn(e, p, cfg)
            e.wait_ge(*nth(nphase, "x_added", 4))
            e.dma_start(out.rearrange("o (t p) d -> p (o t) d", p=P), x[:, :, :]).then_inc(out_done, 16)
            e.wait_ge(out_done, 16)

        def pe_to_features(e, p, tag):
            for half in range(HALVES):
                e.wait_ge(*nth(p, tag + "_in", 4 * (half + 1)))
                for c in range(KC):
                    for t in range(4):
                        mm = e.transpose(ps[:, 4 + 2 * c + half, P * t:P * (t + 1)],
                                         xn[:, 4 * half + t, P * c:P * (c + 1)], ident[:, :])
                    mm.then_inc(s(tag + "_banks"), 1)

        def pe_finish(e, p):
            e.wait_ge(*nth(p, "ot_done", 4))
            for b in range(4):
                for k in range(2):
                    t = 2 * b + k
                    for c in range(KC):
                        mm = e.transpose(ps[:, 4 + b, D * k + P * c:D * k + P * (c + 1)],
                                         ot[:, 2 * c + t // 4, P * (t % 4):P * (t % 4 + 1)], ident[:, :])
                mm.then_inc(s("out_banks"), 1)

        def pe_ffn(e, p, cfg):
            n, r = cfg["chunks"], cfg["router"]
            pe_to_features(e, p, "ln")
            e.wait_ge(*nth(p, "ln_hi", 4))
            e.wait_ge(*nth(p, "ln_lo", 4))
            for t in range(TILES):
                tok = slice(P * t, P * (t + 1))
                terms = three([(xz[:, c, tok], xz[:, KC + c, tok], wrh[:, r, c, :], wrl[:, r, c, :]) for c in range(KC)])
                for k, (a, b) in enumerate(terms):
                    mm = e.matmul(ps[:, 7, RC * t:RC * (t + 1)], a, b, start=(k == 0), stop=(k == len(terms) - 1))
            mm.then_inc(s("logits"), 1)

            def proj(c, b, t, bank, col, last):
                tok = slice(HALF * t, HALF * (t + 1))
                terms = three([(whi[:, b, col + P * k:col + P * (k + 1)], wlo[:, b, col + P * k:col + P * (k + 1)],
                                xz[:, k, tok], xz[:, KC + k, tok]) for k in range(KC)])
                for k, (w, v) in enumerate(terms):
                    mm = e.matmul(ps[:, bank, :], w, v, start=(k == 0), stop=(k == len(terms) - 1))
                mm.then_inc(s(last), 1)

            def down(step, b, t):
                e.wait_ge(*nth(p, "h_hi", step + 1))
                e.wait_ge(*nth(p, "h_lo", step + 1))
                for d in range(KC):
                    terms = three([(whi[:, b, WD + P * d:WD + P * (d + 1)], wlo[:, b, WD + P * d:WD + P * (d + 1)],
                                    hh[:, t, :], hl[:, t, :])])
                    for w, v in terms:
                        mm = e.matmul(ps[:, 2 * d + t, :], w, v, start=False, stop=False, skip_group_check=True)
                mm.then_inc(s("down_done"), 1)

            def step(c, b, t, first):
                k = 2 * c + t
                if t == 0:
                    e.wait_ge(*nth(p, "w_hi", c + 1))
                    e.wait_ge(*nth(p, "w_lo", c + 1))
                if not first:
                    e.wait_ge(*nth(p, "silu", k))
                proj(c, b, t, 4, WG, "gate")
                if not first:
                    e.wait_ge(*nth(p, "su_done", k))
                proj(c, b, t, 5, WU, "up")
                if first:
                    e.wait_ge(*nth(p, "cw_done", 1))
                    for tt in range(TILES):
                        mm = e.transpose(ps[0:RC, 6 + tt // 4, P * (tt % 4):P * (tt % 4 + 1)], cw[:, tt, :], ident[:, :])
                    mm.then_inc(s("cw_banks"), 1)
                    e.wait_ge(*nth(p, "cwT_lo", 2))
                    for o in range(4):
                        e.matmul(ps[:, o, :], zero_r[:, 0:P], zero_r[:, :], start=True, stop=False,
                                 skip_group_check=True)
                else:
                    down(k - 1, b if t else 1 - b, 1 - t)
                    e.wait_ge(*nth(p, "h_done", k))
                e.matmul(ps[:, 6, :], whi[:, b, WSEL:WSEL + P], cwT[:, HALF * t:HALF * (t + 1)],
                         start=True, stop=True).then_inc(s("comb"), 1)

            if p > 0:
                e.wait_ge(*nth(p, "x_added", 4))
                e.wait_ge(*nth(p - 1, "ot_done", 4))
            step(0, 0, 0, True)
            step(0, 0, 1, False)
            with e.Fori(0, (n - 1) // 2) as i:
                for u in range(2):
                    for t in range(2):
                        step(2 * i + 1 + u, (1 + u) % 2, t, False)
            if n % 2 == 0:
                step(n - 1, (n - 1) % 2, 0, False)
                step(n - 1, (n - 1) % 2, 1, False)
            down(2 * n - 1, (n - 1) % 2, 1)
            for o in range(4):
                mm = e.matmul(ps[:, o, :], zero_r[:, 0:P], zero_r[:, :], start=False, stop=True, skip_group_check=True)
            mm.then_inc(s("sums"), 1)
            pe_finish(e, p)

        def pe_attn(e, p, cfg):
            pe_to_features(e, p, "ln")
            e.wait_ge(*nth(p, "ln_hi", 4))
            e.wait_ge(*nth(p, "ln_lo", 4))
            n = 0
            e.wait_ge(*nth(p, "aw_split", 4))
            for m in range(KC):
                for w in range(2):
                    for half in range(HALVES):
                        if n >= 4:
                            e.wait_ge(*nth(p, "tmp_q", n - 3))
                        tok = slice(HALF * half, HALF * (half + 1))
                        terms = three([(awh[:, w, D * c + P * m:D * c + P * (m + 1)], awl[:, w, D * c + P * m:D * c + P * (m + 1)],
                                        xz[:, c, tok], xz[:, KC + c, tok]) for c in range(KC)])
                        for k, (a, b) in enumerate(terms):
                            mm = e.matmul(ps[:, n % 4, :], a, b, start=(k == 0), stop=(k == len(terms) - 1))
                        mm.then_inc(s("qk_banks"), 1)
                        n += 1
            for t in range(TILES):
                if t >= 4:
                    e.wait_ge(*nth(p, "v_done", t - 3))
                tok = slice(P * t, P * (t + 1))
                terms = three([(xz[:, c, tok], xz[:, KC + c, tok], awh[:, 2, D * c:D * (c + 1)], awl[:, 2, D * c:D * (c + 1)])
                               for c in range(KC)])
                for k, (a, b) in enumerate(terms):
                    mm = e.matmul(ps[:, 4 + t % 4, 0:D], a, b, start=(k == 0), stop=(k == len(terms) - 1))
                mm.then_inc(s("v_banks"), 1)
            e.wait_ge(*nth(p, "tmp_q", 8))
            e.wait_ge(*nth(p, "v_done", 8))

            nmx = nsc = npv = nz = 0
            for kind, g, arg in cfg["order"]:
                par = g % SETS
                if kind == "max":
                    j, qt, kh, w = arg
                    sl = QUAD * par + j
                    if nmx == 0:
                        e.wait_ge(*nth(p, "ext_loaded", signals(cfg)["ext_loaded"]))
                    if nmx % cfg["nitems"] == 0:
                        e.wait_ge(*nth(p, "rows_loaded%d" % g, signals(cfg)["rows_loaded%d" % g]))
                    if nmx >= 2:
                        e.wait_ge(*nth(p, "reduced", nmx - 1))
                    bank = 4 + nmx % 2
                    diag = qt // 4 == kh
                    mm = e.matmul(ps[:, bank, 0:w], qs[:, sl, P * qt:P * (qt + 1)], ks[:, sl, HALF * kh:HALF * kh + w],
                                  start=True, stop=not diag)
                    if diag:
                        o = ps[:, bank, P * (qt % 4):P * (qt % 4 + 1)]
                        if cfg["causal"]:
                            mm = e.matmul(o, ident_r[:, :], causal_r[:, :], start=False, stop=True)
                        else:
                            e.matmul(o, sdiag[:, par, 0, j, :], dist_r[:, :], start=False, stop=False)
                            mm = e.matmul(o, sdiag[:, par, 1, j, :], dist_r[:, :], start=False, stop=True)
                    mm.then_inc(s("max_banks"), 1)
                    nmx += 1
                elif kind == "maxend":
                    half = arg
                    e.wait_ge(*nth(p, "nm_done", 2 * g + half + 1))
                    if nz >= 1:
                        e.wait_ge(*nth(p, "z_norm", nz))
                    if 2 * g + half:
                        e.wait_ge(*nth(p, "mh_done", 2 * g + half))
                        e.wait_ge(*nth(p, "ml_done", 2 * g + half))
                    for t in range(4):
                        qt = 4 * half + t
                        mm = e.transpose(ps[0:QUAD, 7, P * t:P * (t + 1)], nm[:, g % 2, QUAD * qt:QUAD * (qt + 1)],
                                         ident[:, :])
                    mm.then_inc(s("m_bank"), 1)
                elif kind == "score":
                    (qh, kt, off), pair, first = arg
                    if first:
                        e.wait_ge(*nth(p, "m_loaded%d" % qh, 16 * 8 * (g + 1)))
                    if nsc >= 2:
                        e.wait_ge(*nth(p, "exp_done", nsc - 1))
                    diag = kt // 4 == qh
                    for u in range(2):
                        j = 2 * pair + u
                        sl = QUAD * par + j
                        bank = 2 * (nsc % 2) + u
                        mm = e.matmul(ps[:, bank, off:HALF], ks[:, sl, P * kt:P * (kt + 1)],
                                      qs[:, sl, HALF * qh + off:HALF * (qh + 1)], start=True, stop=not diag)
                        if diag:
                            dcol = P * (kt - 4 * qh)
                            o = ps[:, bank, dcol:dcol + P]
                            if cfg["causal"]:
                                mm = e.matmul(o, causal_r[:, :], ident_r[:, :], start=False, stop=True)
                            else:
                                e.matmul(o, sdiag[:, par, 0, j, :], dist_r[:, :], start=False, stop=False)
                                mm = e.matmul(o, sdiag[:, par, 1, j, :], dist_r[:, :], start=False, stop=True)
                    mm.then_inc(s("score_banks"), 1)
                    nsc += 1
                elif kind == "pv":
                    (qh, kt, off), pair = arg
                    e.wait_ge(*nth(p, "exp_done", npv + 1))
                    if kt == 0 and pair == 0 and nz >= 1:
                        e.wait_ge(*nth(p, "z_raw", nz))
                    for u in range(2):
                        j = 2 * pair + u
                        mm = e.matmul(ps[32 * j:32 * (j + 1), 6, off:HALF], vaug[:, kt, QUAD * g + j, :],
                                      pt[:, npv % RING, u, off:HALF], start=(kt == 0), stop=(kt == cfg["last_kt"][qh]))
                    mm.then_inc(s("pv_done"), 1)
                    npv += 1
                else:
                    e.wait_ge(*nth(p, "z_raw", nz + 1))
                    e.wait_ge(*nth(p, "mh_done", cfg["mdone"][nz]))
                    e.wait_ge(*nth(p, "ml_done", cfg["mdone"][nz]))
                    if nz >= 1:
                        e.wait_ge(*nth(p, "z_norm", nz))
                    for t in range(4):
                        mm = e.transpose(ps[:, 7, P * t:P * (t + 1)], zraw[:, nz % 2, P * t:P * (t + 1)], ident[:, :])
                    mm.then_inc(s("z_bank"), 1)
                    nz += 1
            e.wait_ge(*nth(p, "z_norm", nz))
            e.wait_ge(*nth(p, "exp_done", nsc))
            pe_to_features(e, p, "z")
            e.wait_ge(*nth(p, "z_hi", 4))
            e.wait_ge(*nth(p, "z_lo", 4))
            for m in range(KC):
                for half in range(HALVES):
                    tok = slice(HALF * half, HALF * (half + 1))
                    terms = three([(awo[:, 0, D * c + P * m:D * c + P * (m + 1)], awo[:, 1, D * c + P * m:D * c + P * (m + 1)],
                                    xz[:, c, tok], xz[:, KC + c, tok]) for c in range(KC)])
                    for k, (a, b) in enumerate(terms):
                        mm = e.matmul(ps[:, 2 * m + half, :], a, b, start=(k == 0), stop=(k == len(terms) - 1))
            mm.then_inc(s("sums"), 1)
            pe_finish(e, p)

        @block.tensor
        def _(e):
            e.wait_ge(consts, n_consts)
            e.wait_ge(setup, 7)
            for p, cfg in enumerate(phases):
                (pe_ffn if cfg["kind"] == "ffn" else pe_attn)(e, p, cfg)

        def act_to_features(e, p, tag):
            for k in range(4):
                half, c = k // 2, k % 2
                e.wait_ge(*nth(p, tag + "_banks", k + 1))
                e.activation(xz[:, c, HALF * half:HALF * (half + 1)], ps[:, 4 + 2 * c + half, :], ACT.Copy)\
                    .then_inc(s(tag + "_hi"), 1)

        def act_norm(e, p):
            e.wait_ge(*nth(p, "var", TILES))
            e.activation(std[:, :], mv[:, :, 1], ACT.Sqrt, bias=eps[:, 0:1]).then_inc(s("std"), 1)

        def act_finish(e, p, bias):
            e.wait_ge(*nth(p, "sums", 1))
            for o in range(0, 4, 2):
                if bias:
                    e.activation(ot[:, o, :], ps[:, o, :], ACT.Identity, bias=cols[:, 4 + o // 2:5 + o // 2])\
                        .then_inc(s("ot_done"), 1)
                else:
                    e.activation(ot[:, o, :], ps[:, o, :], ACT.Copy).then_inc(s("ot_done"), 1)

        def act_tables(e):
            e.activation(qxr[QX:P, :], qxf[QX:P, :], ACT.Copy).then_inc(qxr_done, 1)
            e.wait_ge(srow_done, 1)
            for g in range(QUADS):
                if g >= 2:
                    e.wait_ge(kxl_done, g - 1)
                e.activation(kxp[:, g % 2, :], kx4[:, :], ACT.Copy, scale=srow4[:, g:g + 1]).then_inc(kxp_done, 1)
                e.wait_ge(kxp_done, g + 1)
                e.activation(kxh[:, g, :], kxp[:, g % 2, :], ACT.Copy).then_inc(kxh_done, 1)
            e.wait_ge(slope_done, 1)
            e.activation(slope_h[:, :, :], slope_i[:, :, :], ACT.Copy).then_inc(slope_hi, 1)

        def act_ffn(e, p, cfg):
            n, K, E = cfg["chunks"], cfg["topk"], cfg["experts"]

            def split_hi(c, b, pair, first=False):
                e.wait_ge(*nth(p, "w_loaded%d" % b, 16 * (pair + 1)))
                if not first:
                    e.wait_ge(*nth(p, "down_done", 2 * (c - 1)))
                e.activation(whi[:, b, :], wraw[:, b, :], ACT.Copy).then_inc(s("w_hi"), 1)

            def step(c, t):
                k = 2 * c + t
                e.wait_ge(*nth(p, "gate", k + 1))
                if not isinstance(k, int) or k >= 2:
                    e.wait_ge(*nth(p, "su_done", k - 1))
                e.activation(sg[:, t, :], ps[:, 4, :], ACT.Silu).then_inc(s("silu"), 1)
                e.wait_ge(*nth(p, "h_done", k + 1))
                if not isinstance(k, int) or k >= 2:
                    e.wait_ge(*nth(p, "down_done", k - 1))
                e.activation(hh[:, t, :], hf[:, t, :], ACT.Copy).then_inc(s("h_hi"), 1)

            act_norm(e, p)
            act_to_features(e, p, "ln")
            split_hi(0, 0, 0, True)
            split_hi(1, 1, 0, True)
            if p == 0:
                act_tables(e)
            e.wait_ge(*nth(p, "dv_done", 1))
            e.activation(ev[:, :, 0:K], dv[:, :, 0:K], ACT.Exp).then_inc(s("exps"), 1)
            if cfg["gated"]:
                e.wait_ge(*nth(p, "dl_done", 1))
                e.activation(el[:, :, 0:E], dl[:, :, 0:E], ACT.Exp).then_inc(s("exps"), 1)
                e.activation(zg[:, :], lg[:, :, E], ACT.Exp, scale=-1.0).then_inc(s("exps"), 1)
            e.wait_ge(*nth(p, "cw_banks", 1))
            for k in range(2):
                e.activation(cwT[0:RC, HALF * k:HALF * (k + 1)], ps[0:RC, 6 + k, :], ACT.Copy).then_inc(s("cwT_hi"), 1)
            step(0, 0)
            step(0, 1)
            last = n - 1 - (n - 1) % 2
            with e.Fori(0, (n - 1) // 2 - 1) as i:
                for u in range(2):
                    step(2 * i + 1 + u, 0)
                    split_hi(2 * i + 2 + u, u, i + 1)
                    step(2 * i + 1 + u, 1)
            for c in range(n - 2 if n % 2 else n - 3, n):
                step(c, 0)
                if c + 1 < n:
                    split_hi(c + 1, (c + 1) % 2, (c + 1) // 2)
                step(c, 1)
            act_finish(e, p, False)

        def act_attn(e, p, cfg):
            act_norm(e, p)
            act_to_features(e, p, "ln")
            for k in range(8):
                e.wait_ge(*nth(p, "tmp_q", k + 1))
                if k == 4:
                    e.wait_ge(*nth(p, "hi_stored0", 64))
                e.activation(chi[:, k % 4, :], tmp[:, k % 2, :], ACT.Copy).then_inc(s("hi_q"), 1)
            if cfg["causal"]:
                for t in range(TILES):
                    e.wait_ge(*nth(p, "v_banks", t + 1))
                    if t == 0:
                        e.wait_ge(*nth(p, "v_init", 1))
                    e.activation(vaug[:, t, :, 0:HD], ps[:, 4 + t % 4, 0:D].rearrange("p (h d) -> p h d", d=HD), ACT.Copy)\
                        .then_inc(s("v_done"), 1)
            nsc = nz = npv = 0
            for kind, g, arg in cfg["order"]:
                if kind == "maxend":
                    half = arg
                    if g >= 1:
                        e.wait_ge(*nth(p, "m_loaded%d" % half, 16 * 8 * g))
                    e.wait_ge(*nth(p, "m_bank", 2 * g + half + 1))
                    e.activation(mhl[0:QUAD, HALF * half:HALF * (half + 1)], ps[0:QUAD, 7, :], ACT.Copy)\
                        .then_inc(s("mh_done"), 1)
                elif kind == "score":
                    (qh, kt, off), pair, _ = arg
                    e.wait_ge(*nth(p, "score_banks", nsc + 1))
                    if nsc >= RING:
                        e.wait_ge(*nth(p, "pv_done", nsc - RING + 1))
                    b = 2 * (nsc % 2)
                    e.activation(pt[:, nsc % RING, :, off:HALF], ps[:, b:b + 2, off:HALF], ACT.Exp)\
                        .then_inc(s("exp_done"), 1)
                    nsc += 1
                elif kind == "z":
                    npv = cfg["z_pv"][nz]
                    e.wait_ge(*nth(p, "pv_done", npv))
                    if nz >= 2:
                        e.wait_ge(*nth(p, "z_bank", nz - 1))
                    e.activation(zraw[:, nz % 2, :], ps[:, 6, :], ACT.Copy).then_inc(s("z_raw"), 1)
                    nz += 1
            act_to_features(e, p, "z")
            act_finish(e, p, not cfg["causal"])

        @block.scalar
        def _(e):
            e.wait_ge(setup, 1)
            e.wait_ge(consts, n_consts)
            for p, cfg in enumerate(phases):
                (act_ffn if cfg["kind"] == "ffn" else act_attn)(e, p, cfg)

        def dve_to_features(e, p, tag):
            for k in range(4):
                half, c = k // 2, k % 2
                e.wait_ge(*nth(p, tag + "_hi", k + 1))
                sl = slice(HALF * half, HALF * (half + 1))
                e.tensor_tensor(xz[:, KC + c, sl], ps[:, 4 + 2 * c + half, :], hi_f(xz[:, c, sl]), ALU.subtract)\
                    .then_inc(s(tag + "_lo"), 1)

        def dve_norm(e, p):
            for t in range(TILES):
                if p == 0 and t == 0:
                    e.wait_ge(x_loaded, 16)
                elif p > 0:
                    e.wait_ge(*nth(p, "x_added", t // 2 + 1))
                e.bn_stats(stats[:, t, :], x[:, t, :]).then_inc(s("bn"), 1)
            for t in range(TILES):
                e.wait_ge(*nth(p, "bn", t + 1))
                e.bn_aggr(mv[:, t, :], stats[:, t, :]).then_inc(s("var"), 1)
            e.wait_ge(*nth(p, "std", 1))
            e.reciprocal(rstd[:, :], std[:, :]).then_inc(s("rstd"), 1)
            e.wait_ge(*nth(p, "rstd", 1))
            for t in range(TILES):
                e.tensor_scalar(xn[:, t, :], x[:, t, :], mv[:, t, 0:1], rstd[:, t:t + 1], ALU.subtract, ALU.mult)\
                    .then_inc(s("ln_in"), 1)

        def dve_finish(e, p):
            for o in (1, 3):
                e.wait_ge(*nth(p, "sums", 1))
                if phases[p]["kind"] == "attn" and not phases[p]["causal"]:
                    e.tensor_scalar(ot[:, o, :], ps[:, o, :], cols[:, 4 + o // 2:5 + o // 2], None, ALU.add)\
                        .then_inc(s("ot_done"), 1)
                else:
                    e.tensor_copy(ot[:, o, :], ps[:, o, :]).then_inc(s("ot_done"), 1)
            for b in range(4):
                e.wait_ge(*nth(p, "out_banks", b + 1))
                xx = x[:, 2 * b:2 * b + 2, :].rearrange("p t d -> p (t d)")
                e.tensor_tensor(xx, ps[:, 4 + b, :], xx, ALU.add).then_inc(s("x_added"), 1)

        def dve_ffn(e, p, cfg):
            n, K, E = cfg["chunks"], cfg["topk"], cfg["experts"]
            dve_norm(e, p)
            dve_to_features(e, p, "ln")
            ch, cnt = s("router_step"), router_steps

            def did(ins):
                cnt[0] += 1
                ins.then_inc(ch, 1)

            def settle():
                e.wait_ge(ch, cnt[0])

            if p == 0 or phases[p - 1]["kind"] == "attn":
                did(e.memset(hi_f(cwT[:, :]), 0.0))
            did(e.memset(cw[:, :, :], 0.0))
            e.wait_ge(*nth(p, "logits", 1))
            did(e.tensor_copy(lg[:, :, :], ps[:, 7, 0:TILES * RC].rearrange("p (t r) -> p t r", r=RC)))
            settle()
            for t in range(TILES):
                did(e.max(top8[:, t, :], lg[:, t, 0:E]))
            settle()
            best = top8[:, :, 0:1]
            e.tensor_tensor(dv[:, :, 0:K], top8[:, :, 0:K], best.to_broadcast([P, TILES, K]), ALU.subtract)\
                .then_inc(s("dv_done"), 1)
            if cfg["gated"]:
                e.tensor_tensor(dl[:, :, 0:E], lg[:, :, 0:E], best.to_broadcast([P, TILES, E]), ALU.subtract)\
                    .then_inc(s("dl_done"), 1)
            for t in range(TILES):
                did(e.max_index(idx8[:, t, :], top8[:, t, :], lg[:, t, 0:E]))
            settle()
            did(e.tensor_copy(idxf[:, :, :], idx8[:, :, :]))
            settle()
            oh = onehot[:, 0:TILES * K, 0:E].rearrange("p (t k) e -> p t k e", k=K)
            ow = onew[:, 0:TILES * K, 0:E].rearrange("p (t k) e -> p t k e", k=K)
            did(e.tensor_tensor(oh, idxf[:, :, 0:K].unsqueeze(3).to_broadcast([P, TILES, K, E]),
                                iota[:, 0:E].unsqueeze(1).unsqueeze(1).to_broadcast([P, TILES, K, E]), ALU.is_equal))
            e.wait_ge(*nth(p, "exps", 3 if cfg["gated"] else 1))
            if cfg["gated"]:
                did(e.tensor_reduce(ssum[:, :], el[:, :, 0:E], AX.X, ALU.add))
                did(e.tensor_scalar(zg1[:, :], zg[:, :], 1.0, None, ALU.add))
            else:
                did(e.tensor_reduce(ssum[:, :], ev[:, :, 0:K], AX.X, ALU.add))
            settle()
            did(e.reciprocal(rsum[:, :], ssum[:, :]))
            if cfg["gated"]:
                did(e.reciprocal(zg2[:, :], zg1[:, :]))
            settle()
            did(e.scalar_tensor_tensor(wk[:, :, 0:K], ev[:, :, 0:K], cfg["moe_scale"],
                                       rsum[:, :].unsqueeze(2).to_broadcast([P, TILES, K]), ALU.mult, ALU.mult))
            if cfg["gated"]:
                did(e.tensor_scalar(cw[:, :, E], zg2[:, :], cfg["shared_scale"], None, ALU.mult))
            else:
                did(e.memset(cw[:, :, E:E + 1], cfg["shared_scale"]))
            settle()
            did(e.tensor_tensor(ow, oh, wk[:, :, 0:K].unsqueeze(3).to_broadcast([P, TILES, K, E]), ALU.mult))
            settle()
            e.tensor_reduce(cw[:, :, 0:E], ow.rearrange("p t k e -> p t e k"), AX.X, ALU.add)\
                .then_inc(s("cw_done"), 1)
            for k in range(2):
                e.wait_ge(*nth(p, "cwT_hi", k + 1))
                sl = slice(HALF * k, HALF * (k + 1))
                e.tensor_tensor(cwT[RC:2 * RC, sl], ps[0:RC, 6 + k, :], hi_f(cwT[0:RC, sl]), ALU.subtract)\
                    .then_inc(s("cwT_lo"), 1)

            def step(c, t):
                k = 2 * c + t
                e.wait_ge(*nth(p, "up", k + 1))
                e.wait_ge(*nth(p, "silu", k + 1))
                e.tensor_tensor(su[:, t, :], ps[:, 5, :], sg[:, t, :], ALU.mult).then_inc(s("su_done"), 1)
                e.wait_ge(*nth(p, "comb", k + 1))
                e.wait_ge(*nth(p, "su_done", k + 1))
                if not isinstance(k, int) or k >= 2:
                    e.wait_ge(*nth(p, "h_hi", k - 1))
                e.tensor_tensor(hf[:, t, :], ps[:, 6, :], su[:, t, :], ALU.mult).then_inc(s("h_done"), 1)
                e.wait_ge(*nth(p, "h_hi", k + 1))
                if not isinstance(k, int) or k >= 2:
                    e.wait_ge(*nth(p, "down_done", k - 1))
                e.tensor_tensor(hl[:, t, :], hf[:, t, :], hi_f(hh[:, t, :]), ALU.subtract).then_inc(s("h_lo"), 1)

            step(0, 0)
            step(0, 1)
            with e.Fori(0, (n - 1) // 2) as i:
                for u in range(2):
                    step(2 * i + 1 + u, 0)
                    step(2 * i + 1 + u, 1)
            if n % 2 == 0:
                step(n - 1, 0)
                step(n - 1, 1)
            dve_finish(e, p)

        def dve_attn(e, p, cfg):
            dve_norm(e, p)
            dve_to_features(e, p, "ln")
            e.wait_ge(*nth(p, "region_free", 1))
            for k in range(8):
                m, w = k // 4, (k // 2) % 2
                e.wait_ge(*nth(p, "qk_banks", k + 1))
                if k >= 2:
                    e.wait_ge(*nth(p, "lo_q", k - 1))
                    e.wait_ge(*nth(p, "hi_q", k - 1))
                scale = HD ** -0.5 if w == 0 else 1.0
                if cfg["causal"]:
                    e.tensor_scalar(tmp[:, k % 2, :], ps[:, k % 4, :], scale, None, ALU.mult).then_inc(s("tmp_q"), 1)
                else:
                    e.tensor_scalar(tmp[:, k % 2, :], ps[:, k % 4, :], cols[:, 2 * w + m:2 * w + m + 1], scale,
                                    ALU.add, ALU.mult).then_inc(s("tmp_q"), 1)
                e.wait_ge(*nth(p, "hi_q", k + 1))
                if k == 4:
                    e.wait_ge(*nth(p, "lo_stored0", 64))
                e.tensor_tensor(clo[:, k % 4, :], tmp[:, k % 2, :], hi_f(chi[:, k % 4, :]), ALU.subtract)\
                    .then_inc(s("lo_q"), 1)
            if not cfg["causal"]:
                for t in range(TILES):
                    e.wait_ge(*nth(p, "v_banks", t + 1))
                    if t == 0:
                        e.wait_ge(*nth(p, "v_init", 1))
                    e.tensor_tensor(vaug[:, t, :, 0:HD], ps[:, 4 + t % 4, 0:D].rearrange("p (h d) -> p h d", d=HD),
                                    bvb[:, :].rearrange("p (h d) -> p h d", d=HD), ALU.add).then_inc(s("v_done"), 1)
            else:
                e.memset(nmax[:, :, 1], BIG).then_inc(s("nmax_init"), 1)
                e.wait_ge(*nth(p, "nmax_init", 1))
            nmx = nz = 0
            for kind, g, arg in cfg["order"]:
                if kind == "max":
                    j, qt, kh, w = arg
                    e.wait_ge(*nth(p, "max_banks", nmx + 1))
                    if nmx % cfg["nitems"] == 0 and g >= 1:
                        e.wait_ge(*nth(p, "nm_done", 2 * g))
                    e.tensor_reduce(nmax[:, QUAD * qt + j, kh:kh + 1], ps[:, 4 + nmx % 2, 0:w], AX.X, ALU.max,
                                    negate=True).then_inc(s("reduced"), 1)
                    nmx += 1
                elif kind == "maxend":
                    half = arg
                    part = slice(QUAD * 4 * half, QUAD * 4 * (half + 1))
                    sl = slice(HALF * half, HALF * (half + 1))
                    e.wait_ge(*nth(p, "reduced", nmx))
                    if g >= 2:
                        e.wait_ge(*nth(p, "m_bank", 2 * (g - 1)))
                    e.tensor_tensor(nm[:, g % 2, part], nmax[:, part, 0], nmax[:, part, 1], ALU.min)\
                        .then_inc(s("nm_done"), 1)
                    e.wait_ge(*nth(p, "mh_done", 2 * g + half + 1))
                    if g >= 1:
                        e.wait_ge(*nth(p, "m_loaded%d" % half, 16 * 8 * g))
                    e.tensor_tensor(mhl[RC:RC + QUAD, sl], ps[0:QUAD, 7, :], hi_f(mhl[0:QUAD, sl]), ALU.subtract)\
                        .then_inc(s("ml_done"), 1)
                elif kind == "z":
                    e.wait_ge(*nth(p, "z_bank", nz + 1))
                    den = ps[:, 7, :].rearrange("p (a r) -> p a r", r=32)
                    e.reciprocal(rden[:, nz % 2, :], den[:, :, HD]).then_inc(s("rden"), 1)
                    e.wait_ge(*nth(p, "rden", nz + 1))
                    qh = arg
                    e.tensor_tensor(xn[:, 4 * qh:4 * qh + 4, QUAD * HD * g:QUAD * HD * (g + 1)].rearrange(
                                        "p t (j d) -> p t j d", d=HD),
                                    ps[:, 7, :].rearrange("p (t j r) -> p t j r", t=4, r=32)[:, :, :, 0:HD],
                                    rden[:, nz % 2, :].rearrange("p (t j) -> p t j", t=4).unsqueeze(3)
                                    .to_broadcast([P, 4, QUAD, HD]), ALU.mult).then_inc(s("z_norm"), 1)
                    nz += 1
            e.wait_ge(*nth(p, "z_norm", nz))
            e.sem_inc(s("z_in"), 8)
            dve_to_features(e, p, "z")
            dve_finish(e, p)

        @block.vector
        def _(e):
            e.memset(eps[:, :], EPS).then_inc(setup, 1)
            e.memset(hi_f(zero_r[:, :]), 0.0).then_inc(setup, 1)
            e.wait_ge(consts, n_consts)
            e.tensor_copy(ident_r[:, :], ident[:, :]).then_inc(setup, 1)
            e.tensor_copy(dist_r[:, :], dist[:, :]).then_inc(setup, 1)
            e.tensor_copy(causal_r[:, :], causal[:, :]).then_inc(setup, 1)
            e.tensor_copy(wrh[:, 0, :, :], wr0[:, :, :]).then_inc(wr_hi, 1)
            e.tensor_copy(wrh[:, 1, :, :], wr1[:, :, :]).then_inc(wr_hi, 1)
            e.wait_ge(wr_hi, 2)
            e.tensor_tensor(wrl[:, 0, :, :], wr0[:, :, :], hi_f(wrh[:, 0, :, :]), ALU.subtract).then_inc(setup, 1)
            e.tensor_tensor(wrl[:, 1, :, :], wr1[:, :, :], hi_f(wrh[:, 1, :, :]), ALU.subtract).then_inc(setup, 1)
            e.tensor_scalar(srow4[:, :], slope4[:, :], keep[:, 0:1], keep[:, 1:2], ALU.mult, ALU.add).then_inc(srow_done, 1)
            e.tensor_tensor(slope_i[:, :, :], ident[:, :].unsqueeze(1).to_broadcast([P, NH, P]),
                            slopes[:, :].unsqueeze(2).to_broadcast([P, NH, P]), ALU.mult).then_inc(slope_done, 1)
            for p, cfg in enumerate(phases):
                (dve_ffn if cfg["kind"] == "ffn" else dve_attn)(e, p, cfg)

        def pool_ffn(e, p, cfg):
            n = cfg["chunks"]

            def split_lo(c, b, first=False):
                e.wait_ge(*nth(p, "w_hi", c + 1))
                if not first:
                    e.wait_ge(*nth(p, "down_done", 2 * (c - 1)))
                e.tensor_tensor(wlo[:, b, :], wraw[:, b, 0:WSEL], hi_f(whi[:, b, 0:WSEL]), ALU.subtract)\
                    .then_inc(s("w_lo"), 1)

            split_lo(0, 0, True)
            split_lo(1, 1, True)
            if p == 0:
                pool_tables(e)
            if p in ready_in:
                if p > 0:
                    e.wait_ge(*nth(p - 1, "sums", 1))
                pool_ready_attn(e, ready_in[p])
            with e.Fori(0, (n - 2) // 2) as i:
                for b in range(2):
                    split_lo(2 * i + 2 + b, b)
            if n % 2:
                split_lo(n - 1, (n - 1) % 2)

        def pool_did(ins):
            pool_steps[0] += 1
            ins.then_inc(s("pool_step"), 1)

        def pool_settle(e):
            e.wait_ge(s("pool_step"), pool_steps[0])

        def pool_tables(e):
            for g in range(QUADS):
                e.wait_ge(kxh_done, g + 1)
                e.tensor_tensor(kxl[:, g, :], kxp[:, g % 2, :], hi_f(kxh[:, g, :]), ALU.subtract).then_inc(kxl_done, 1)
            e.wait_ge(slope_hi, 1)
            e.tensor_tensor(slope_l[:, :, :], slope_i[:, :, :], hi_f(slope_h[:, :, :]), ALU.subtract).then_inc(kxl_done, 1)
            e.wait_ge(qxr_done, 1)
            e.wait_ge(kxl_done, QUADS + 1)
            for dst, src in ((qext_d, qxr[QX:P, :]), (zero_d, zero_r[QX:P, :]),
                             (kext_d[0].rearrange("(g j) r t -> (j r) g t", j=QUAD), kxh[:, :, :]),
                             (kext_d[1].rearrange("(g j) r t -> (j r) g t", j=QUAD), kxl[:, :, :]),
                             (sdiag_d[0], slope_h[:, :, :].rearrange("p h n -> p (h n)")),
                             (sdiag_d[1], slope_l[:, :, :].rearrange("p h n -> p (h n)"))):
                e.dma_start(dst, hi_f(src)).then_inc(tables, 16)

        def pool_ready_attn(e, q):
            for w in range(4):
                e.wait_ge(*nth(q, "aw_loaded%d" % (w % 2), 16 * (w // 2 + 1)))
                h_, l_ = (awh[:, w, :], awl[:, w, :]) if w < 3 else (awo[:, 0, :], awo[:, 1, :])
                pool_did(e.tensor_copy(h_, araw[:, w % 2, :]))
                pool_settle(e)
                e.tensor_tensor(l_, araw[:, w % 2, :], hi_f(h_), ALU.subtract).then_inc(s("aw_split"), 1)
            pool_did(e.memset(vaug[:, :, :, :], 0.0))
            pool_settle(e)
            e.memset(vaug[:, :, :, HD:HD + 1], 1.0).then_inc(s("v_init"), 1)

        def pool_attn(e, p, cfg):
            e.wait_ge(*nth(p - 1, "sums", 1))
            if p - 1 == 0:
                e.wait_ge(tables, 16 * 6)
            e.sem_inc(s("region_free"), 1)
            for g in range(QUADS):
                done = s("rows_loaded%d" % g)
                for part in ("hi", "lo"):
                    e.wait_ge(*nth(p, "%s_stored%d" % (part, g // 2), 64))
                if g >= SETS:
                    e.wait_ge(*nth(p, "score_banks", 2 * cfg["nsteps"] * (g - SETS + 1)))
                slots = slice(QUAD * (g % SETS), QUAD * (g % SETS + 1))
                heads = slice(QUAD * g, QUAD * (g + 1))
                for r in range(4):
                    rows = slice(HD * r, HD * (r + 1))
                    for w, dst, part in ((0, qs, r // 2), (1, ks, r % 2)):
                        e.dma_start(hi_f(dst[rows, slots, :]),
                                    qk_d[w, part, QUAD * HD * g:QUAD * HD * (g + 1), :]
                                    .rearrange("(j r) t -> r j t", j=QUAD)).then_inc(done, 16)
                if not cfg["causal"]:
                    for part in range(2):
                        e.dma_start(hi_f(ks[QX + 32 * part:QX + 32 * (part + 1), slots, :]),
                                    kext_d[part, heads, :, :].rearrange("j r t -> r j t")).then_inc(done, 16)
                    e.dma_start(hi_f(sdiag[:, g % SETS, :, :, :]).rearrange("p o j n -> p o (j n)"),
                                sdiag_d[:, :, QUAD * P * g:QUAD * P * (g + 1)].rearrange("o p n -> p o n"))\
                        .then_inc(done, 16)
                if g >= SETS:
                    e.dma_start(hi_f(qs[MROW:MROW + 2, slots, :]).rearrange("p s (h c) -> p (s h) c", h=2),
                                zero_d[0:2, :].unsqueeze(1).to_broadcast([2, 2 * QUAD, HALF])).then_inc(done, 16)

        @block.gpsimd
        def _(e):
            e.wait_ge(consts, n_consts)
            for p, cfg in enumerate(phases):
                (pool_ffn if cfg["kind"] == "ffn" else pool_attn)(e, p, cfg)


def position_tables(np):
    i = np.arange(P)
    ident = np.eye(P, dtype=np.float32)
    dist = -np.abs(i[:, None] - i[None, :]).astype(np.float32)
    causal = np.where(i[None, :] > i[:, None], np.float32(-2.0 ** 127), np.float32(0)).astype(np.float32)
    iota = np.ascontiguousarray(np.broadcast_to(np.arange(16, dtype=np.float32), (P, 16)))
    t = np.arange(T)
    tile = t // P
    qx = np.zeros((P, T), np.float32)
    kx = np.zeros((P, T), np.float32)
    for c in range(TILES):
        centre = P * c + P // 2
        side = np.sign(tile - c).astype(np.float32)
        for base in (QX, QX + 32):
            qx[base + c] = -np.abs(t - centre) * np.abs(side)
            qx[base + TILES + c] = side
        kx[QX + c] = tile == c
        kx[QX + TILES + c] = (t - centre) * (tile == c)
    kx[MROW:MROW + 2] = 1.0
    keep = np.zeros((P, 2), np.float32)
    keep[:, 0] = np.arange(P) % 32 < MROW - QX
    keep[:, 1] = 1.0 - keep[:, 0]
    return dict(ident=ident, dist=dist, causal=causal, iota=iota, qx=qx[QX:], kx4=np.tile(kx[QX:QX + 32], (4, 1)), keep=keep)


def pack_ffn(np, wg, wu, wd, sg, su, sd, experts, hidden, chunks):
    pad = chunks * P
    n = experts * hidden
    G, U = np.zeros((D, pad), np.float32), np.zeros((D, pad), np.float32)
    W = np.zeros((pad, D), np.float32)
    sel = np.zeros((P, pad), np.float32)
    m = n + sg.shape[1]
    G[:, :n] = wg.transpose(1, 0, 2).reshape(D, n)
    U[:, :n] = wu.transpose(1, 0, 2).reshape(D, n)
    G[:, n:m], U[:, n:m] = sg, su
    W[:n], W[n:m] = wd.reshape(n, D), sd
    for e in range(experts):
        sel[[e, RC + e], e * hidden:(e + 1) * hidden] = 1.0
    sel[[experts, RC + experts], n:m] = 1.0
    out = np.zeros((chunks, P, WCOLS), np.float32)
    for c in range(chunks):
        s = slice(c * P, (c + 1) * P)
        out[c, :, WG:WG + P], out[c, :, WG + P:WU] = G[:P, s], G[P:, s]
        out[c, :, WU:WU + P], out[c, :, WU + P:WD] = U[:P, s], U[P:, s]
        out[c, :, WD:WSEL] = W[s]
        out[c, :, WSEL:] = sel[:, s]
    return out


PLAN = ["f0", "a0", "f0", "f1", "a1", "f1"]


def kernel(**inputs):
    import numpy as _np
    import concourse.bacc as _bacc
    from concourse.bass_utils import run_bass_kernel_spmd as _run

    I = {k: _np.asarray(v) for k, v in inputs.items()}

    def chunked(w):
        return _np.ascontiguousarray(w.reshape(KC, P, -1).transpose(1, 0, 2))

    def router(*ws):
        r = _np.zeros((D, RC), _np.float32)
        c = 0
        for w in ws:
            r[:, c:c + w.shape[1]] = w
            c += w.shape[1]
        return chunked(r)

    def attn(*ws):
        return _np.stack([chunked(w.T).reshape(P, KC * D) for w in ws])

    arrays = position_tables(_np)
    arrays["x"] = I["L0_attn_x"]
    arrays["wr0"] = router(I["L0_ffn_Wr"], I["L0_ffn_Wsg"])
    arrays["wr1"] = router(I["L1_ffn_w_router"])
    cols = _np.zeros((P, 8), _np.float32)
    for k, name in enumerate(("bq", "bk", "bo")):
        cols[:, 2 * k:2 * k + 2] = I["L0_attn_" + name].reshape(KC, P).T
    arrays["cols"] = cols
    arrays["bvb"] = _np.ascontiguousarray(_np.broadcast_to(I["L0_attn_bv"], (P, D)))
    arrays["slopes"] = _np.ascontiguousarray(_np.broadcast_to(I["L0_attn_slopes"], (P, NH)))
    arrays["slope4"] = _np.repeat(I["L0_attn_slopes"].reshape(QUADS, QUAD).T, 32, axis=0)
    arrays["f0"] = pack_ffn(_np, I["L0_ffn_Wg"], I["L0_ffn_Wu"], I["L0_ffn_Wd"], I["L0_ffn_Sg"], I["L0_ffn_Su"],
                            I["L0_ffn_Sd"], FFN0["experts"], 176, FFN0["chunks"])
    arrays["f1"] = pack_ffn(_np, I["L1_ffn_we1"], I["L1_ffn_we3"], I["L1_ffn_we2"], I["L1_ffn_ws1"], I["L1_ffn_ws3"],
                            I["L1_ffn_ws2"], FFN1["experts"], 128, FFN1["chunks"])
    arrays["a0"] = attn(*(I["L0_attn_W" + c] for c in "qkvo"))
    arrays["a1"] = attn(*(I["L1_attn_W" + c] for c in "qkvo"))

    kinds = {
        "f0": dict(kind="ffn", w="f0", router=0, moe_scale=0.5, shared_scale=0.5, **FFN0),
        "f1": dict(kind="ffn", w="f1", router=1, moe_scale=0.5 * 4 / 5, shared_scale=0.5 / 5, **FFN1),
        "a0": dict(kind="attn", w="a0", causal=False),
        "a1": dict(kind="attn", w="a1", causal=True),
    }
    nc = _bacc.Bacc("TRN2", target_bir_lowering=False, num_devices=1)
    A = {}
    for name, a in arrays.items():
        arrays[name] = a = _np.ascontiguousarray(a)
        A[name] = nc.dram_tensor(f"in_{name}", a.shape, F32, kind="ExternalInput").ap()
    out = nc.dram_tensor("out_x", (1, T, D), F32, kind="ExternalOutput").ap()
    program(nc, A, out, [dict(kinds[k]) for k in PLAN])
    r = _run(nc, [{f"in_{name}": a for name, a in arrays.items()}], core_ids=[0])
    return r.results[0]["out_x"]
```

```python
from contextlib import ExitStack
from math import ceil

import concourse.bass as bass
from concourse import mybir

F32 = mybir.dt.float32
F32R = mybir.dt.float32r
U32 = mybir.dt.uint32
ALU = mybir.AluOpType
ACT = mybir.ActivationFunctionType
AX = mybir.AxisListType

P = 128
T = 1024
D = 256
TILES = T // P
KC = D // P
HALF = 512
HALVES = T // HALF
NH = 16
HD = D // NH
QUAD = 4
QUADS = NH // QUAD
SETS = 3
TABLE_PARTS = QUADS + 2
EPS = 1e-5
WG, WU, WD, WSEL = 0, 2 * P, 4 * P, 6 * P
WCOLS = 7 * P
RC = 32
BANKS = ((4, 7), (5, 6))
TURN = (4, 5, 7)
QX = 64
MROW = QX
BIG = 3.0e38

FFN0 = dict(experts=8, topk=2, chunks=17, gated=True)
FFN1 = dict(experts=16, topk=4, chunks=20, gated=False)


def attention_order(causal):
    items = [(j, qt, kh, min(HALF, P * (qt + 1) - HALF * kh) if causal else HALF)
             for half in range(HALVES) for j in range(QUAD) for qt in range(4 * half, 4 * half + 4)
             for kh in range(HALVES)]
    items = [it for it in items if it[3] > 0]
    nhalf = [sum(it[1] // 4 == half for it in items) for half in range(HALVES)]
    steps = [(qh, kt, max(0, kt - 4 * qh) * P if causal else 0)
             for qh in range(HALVES) for kt in range(4 * qh + 4 if causal else TILES)]
    last_kt = [max(kt for qh, kt, _ in steps if qh == h) for h in range(HALVES)]
    todo = [(g, half) for g in range(QUADS) for half in range(HALVES)]
    maxima = []
    until = {}
    for g, half in todo:
        part = items[:nhalf[0]] if half == 0 else items[nhalf[0]:]
        maxima += [("max", g, it) for it in part] + [("maxend", g, half)]
        until[g, half] = len(maxima)
    lead = until[0, 0] + 4
    order, given = maxima[:lead], lead
    before = None
    whole = None
    gap = 1
    left = len(steps) * QUADS - gap
    for n, (g, half) in enumerate(todo):
        own = [st for st in steps if st[0] == half]
        pace = (len(maxima) - given) / max(left, 1)
        due = until[todo[n + 1]] - given if n + 1 < len(todo) else 0
        pace = max(pace, due / max(len(own) - gap, 1))
        start = given
        most = until[todo[n + 2]] if n + 2 < len(todo) else len(maxima)
        for k, st in enumerate(own):
            upto = max(given, min(most, start + ceil(pace * (k + 1.5))))
            share = maxima[given:upto]
            given = upto
            third = (len(share) + 2) // 3
            order += [("score", g, (st, 0, k == 0))] + share[:third]
            order += [("score", g, (st, 1, False))] + share[third:2 * third]
            if whole:
                order.append(("z",) + whole)
                whole = None
            if before:
                order.append(("pv",) + before)
                if before[1][1] == last_kt[before[1][0]]:
                    whole = (before[0], before[1][0])
                    order.append(("zcopy",) + whole)
            order += share[2 * third:]
            if n == len(todo) - 1 and k == 2:
                order.append(("feat", g, 0))
            before = (g, st)
        left -= len(own)
    order += [("pv",) + before, ("zcopy", g, half), ("z", g, half)]

    for unit in todo:
        n = order.index(("maxend",) + unit)
        n = next(k for k in range(n, len(order)) if order[k][0] == "score")
        own = order[n][1] == unit[0] and order[n][2][0][0] == unit[1]
        order.insert(n if own else n + 1, ("mrows",) + unit)

    place, users, count = [], [], dict(max=0, mrows=0, z=0)
    for kind, g, arg in order:
        spot = (None, None)
        if kind in count:
            last_z = (kind, g, arg) == ("z", QUADS - 1, 1)
            spot = (5, None) if last_z else (TURN[len(users) % 3], users[-3] if len(users) >= 3 else None)
            count[kind] += 1
            users.append((kind, count[kind]))
        place.append(spot)

    at_copy = [n for n, (kind, _, _) in enumerate(order) if kind == "zcopy"]
    return dict(order=order, nitems=len(items), nsteps=len(steps), last_kt=last_kt, pairs=2 * QUADS * len(steps),
                z_pv=[sum(k == "pv" for k, _, _ in order[:n]) for n in at_copy],
                place=place)


def signals(cfg):
    each = dict(x_added=4, bn=TILES, var=TILES, std=2, rstd=2, shift=2, ln_in=4, ln_in_act=4, ln_banks=4,
                ln_hi=4, ln_lo=4, sums=2, ot_done=4, out_banks=4)
    if cfg["kind"] == "ffn":
        n = cfg["chunks"]
        steps = dict.fromkeys(("gate", "up", "silu", "su_done", "comb", "h_done", "h_hi", "h_lo"), 2 * n)
        steps["down_done"] = 2 * n - 1
        return dict(each, w_loaded0=16 * ((n + 1) // 2), w_loaded1=16 * (n // 2), w_hi=n, w_lo=n, wd_lo=n,
                    logits_t=2, logits_copy=2, logits=1, dv_done=1, dl_done=int(cfg["gated"]),
                    exps=3 if cfg["gated"] else 1, cw_done=1, cw_banks=1, cwT_hi=2, cwT_lo=2, **steps)
    nmax, quads, zs = QUADS * cfg["nitems"], QUADS, QUADS * HALVES
    ext = 0 if cfg["causal"] else 3
    ext_dmas = 3 if cfg["causal"] else 1
    return dict(each, aw_loaded0=32, aw_loaded1=32, aw_split=4, v_init=4, region_free=1,
                ext_loaded0=16 * ext_dmas, ext_loaded1=2 * 16 * ext_dmas, first_rows_loaded=16 * 8,
                rows_loaded0=16 * ext, rows_loaded1=16 * (8 + ext), rows_loaded2=16 * (8 + ext),
                rows_loaded3=16 * (9 + ext), hi_stored0=64, hi_stored1=64, lo_stored0=64, lo_stored1=64,
                qk_banks=8, hi_q=8, lo_q=8, v_banks=TILES, v_done=TILES, nmax_init=int(cfg["causal"]),
                bias_scaled=int(not cfg["causal"]), max_banks=nmax, reduced=nmax, nm_init=1, nm_done=2 * quads,
                nm_hi=2 * quads, nm_lo=2 * quads, m_bank=2 * quads, m_act=4 * quads, m_dve=4 * quads,
                score_banks=cfg["pairs"], exp_done=cfg["pairs"], pv_done=cfg["pairs"] // 2,
                z_raw=zs, z_bank=zs, rden=zs, z_norm=zs, z_banks=4, z_hi=4, z_lo=4)


def program(nc, A, out, phases):
    for cfg in phases:
        if cfg["kind"] == "attn":
            cfg.update(attention_order(cfg["causal"]))
    ctx = ExitStack()
    with ctx:
        def sb(name, shape, dt=F32, stack=ctx):
            return stack.enter_context(nc.sbuf_tensor(name, shape, dt))

        def sem(name):
            return ctx.enter_context(nc.semaphore(name))

        ps = ctx.enter_context(nc.psum_tensor("ps", [P, 8, 512], F32))

        x = sb("x", [P, TILES, D])
        early = ExitStack()
        ot = sb("ot", [P, 4, HALF], F32, early)
        early.close()
        xz = sb("xz", [P, 2 * KC, T], F32R)
        xn = sb("xn", [P, TILES, D])
        ident = sb("ident", [P, P])
        iota = sb("iota", [P, 16])
        eps = sb("eps", [P, 1])
        zero_r = sb("zero_r", [P, HALF], F32R)
        ident_r = sb("ident_r", [P, P], F32R)
        dist_r = sb("dist_r", [P, P], F32R)
        causal_r = sb("causal_r", [P, P], F32R)
        wrh = sb("wrh", [P, 2, KC, RC], F32R)
        wrl = sb("wrl", [P, 2, KC, RC], F32R)
        stats = sb("stats", [P, TILES, 6])
        mv = sb("mv", [P, TILES, 2])
        std = sb("std", [P, TILES])
        rstd = sb("rstd", [P, TILES])
        shift = sb("shift", [P, TILES])
        cols = sb("cols", [P, 8])
        bvb = sb("bvb", [P, D])
        slopes = sb("slopes", [P, NH])
        keep = sb("keep", [P, 2])
        srow4 = sb("srow4", [P, QUADS])
        slope4 = sb("slope4", [P, QUADS])

        awo = sb("awo", [P, 2, KC * D], F32R)
        early = ExitStack()
        awh = sb("awh", [P, 3, KC * D], F32R, early)
        awl = sb("awl", [P, 3, KC * D], F32R, early)
        early.close()
        RING = 4
        pt = sb("pt", [P, RING, 2, HALF])
        early = ExitStack()
        araw = sb("araw", [P, 2, KC * D], F32, early)
        early.close()
        zraw = sb("zraw", [P, 2, HALF])
        vaug = sb("vaug", [P, TILES, NH, 32])

        ffn = ExitStack()
        wraw = sb("wraw", [P, 2, WCOLS], F32, ffn)
        whi = sb("whi", [P, 2, WCOLS], F32R, ffn)
        wlo = sb("wlo", [P, 2, WSEL], F32R, ffn)
        sg = sb("sg", [P, 2, HALF], F32, ffn)
        su = sb("su", [P, 2, HALF], F32, ffn)
        hf = sb("hf", [P, 2, HALF], F32, ffn)
        hh = sb("hh", [P, 2, HALF], F32R, ffn)
        hl = sb("hl", [P, 2, HALF], F32R, ffn)
        cwT = sb("cwT", [P, T], F32R, ffn)
        lgT = sb("lgT", [RC, T], F32, ffn)
        lg = sb("lg", [P, TILES, RC], F32, ffn)
        top8 = sb("top8", [P, TILES, 8], F32, ffn)
        idx8 = sb("idx8", [P, TILES, 8], U32, ffn)
        idxf = sb("idxf", [P, TILES, 8], F32, ffn)
        dl = sb("dl", [P, TILES, RC], F32, ffn)
        el = sb("el", [P, TILES, RC], F32, ffn)
        ev = sb("ev", [P, TILES, 4], F32, ffn)
        dv = sb("dv", [P, TILES, 4], F32, ffn)
        wk = sb("wk", [P, TILES, 4], F32, ffn)
        ssum = sb("ssum", [P, TILES], F32, ffn)
        rsum = sb("rsum", [P, TILES], F32, ffn)
        zg = sb("zg", [P, TILES], F32, ffn)
        zg1 = sb("zg1", [P, TILES], F32, ffn)
        zg2 = sb("zg2", [P, TILES], F32, ffn)
        onehot = sb("onehot", [P, TILES * 4, 16], F32, ffn)
        onew = sb("onew", [P, TILES * 4, 16], F32, ffn)
        cw = sb("cw", [P, TILES, RC], F32, ffn)
        dist = sb("dist", [P, P], F32, ffn)
        causal = sb("causal", [P, P], F32, ffn)
        wr0 = sb("wr0", [P, KC, RC], F32, ffn)
        wr1 = sb("wr1", [P, KC, RC], F32, ffn)
        kx4 = sb("kx4", [P, T], F32, ffn)
        qxf = sb("qxf", [P, T], F32, ffn)
        qxr = sb("qxr", [P, T], F32R, ffn)
        kxp = sb("kxp", [P, 2, T], F32, ffn)
        kxh = sb("kxh", [P, QUADS, T], F32R, ffn)
        kxl = sb("kxl", [P, QUADS, T], F32R, ffn)
        early = ExitStack()
        slope_i = sb("slope_i", [P, NH, P], F32, early)
        early.close()
        slope_l = sb("slope_l", [P, NH, P], F32R, ffn)
        slope_h = sb("slope_h", [P, NH, P], F32R, ffn)
        ffn.close()

        qs = sb("qs", [P, SETS * QUAD, T], F32R)
        ks = sb("ks", [P, SETS * QUAD, T], F32R)
        early = ExitStack()
        ot_attn = sb("ot_attn", [P, 4, HALF], F32, early)
        early.close()
        chi = sb("chi", [P, 4, HALF], F32R)
        clo = sb("clo", [P, 4, HALF], F32R)
        nmp = sb("nmp", [P, 2, 4, P], F32R)
        sdiag = sb("sdiag", [P, SETS, 2, QUAD, P], F32R)
        nmax = sb("nmax", [P, QUAD * TILES, 2])
        nm = sb("nm", [P, 2, QUAD * TILES])
        rden = sb("rden", [P, 2, 16])

        def dram(name, shape):
            return nc.dram_tensor(name, shape, F32, kind="Internal").ap()

        qk_d = dram("qk_d", (2, 2, D, T))
        kext_d = dram("kext_d", (2, NH, 32, T))
        qext_d = dram("qext_d", (P - QX, T))
        sdiag_d = dram("sdiag_d", (2, P, NH * P))
        zero_d = dram("zero_d", (P - QX, HALF))

        S = {}
        router_steps, pool_steps = [0], [0]
        def s(name):
            if name not in S:
                S[name] = sem(name)
            return S[name]

        def nth(p, name, n):
            last = p - 1 if name == "x_added" else p
            return s(name), n + sum(signals(phases[q])[name] for q in range(last) if name in signals(phases[q]))

        consts = sem("consts_loaded")
        x_loaded = [sem("x_loaded%d" % half) for half in range(HALVES)]
        ident_loaded = sem("ident_loaded")
        wr_hi = sem("router_hi_split")
        setup = sem("setup_done")
        out_done = sem("out_written")
        srow_done = sem("slope_rows_done")
        slope_done = sem("slope_identity_done")
        slope_hi = sem("slope_identity_hi_done")
        kxp_done = sem("key_rows_done")
        kxh_done = sem("key_rows_hi_done")
        kxl_done = sem("key_rows_lo_done")
        qxr_done = sem("query_rows_done")
        tables = sem("tables_stored")

        def slope_part(part):
            n = NH // (TABLE_PARTS - QUADS)
            return slice(n * (part - QUADS), n * (part - QUADS + 1))

        def hi_f(ap):
            return ap.bitcast(F32)

        def three(pairs):
            r = []
            for a_h, a_l, b_h, b_l in pairs:
                r += [(a_h, b_h), (a_l, b_h), (a_h, b_l)]
            return r

        n_consts = 0
        const_loads = []
        for tile, name in ((dist, "dist"), (causal, "causal"), (iota, "iota"), (cols, "cols"),
                           (bvb, "bvb"), (slopes, "slopes"), (keep, "keep")):
            const_loads.append((tile[:, :], A[name]))
        const_loads.append((slope4[:, :], A["slope4"]))
        const_loads.append((kx4[:, :], A["kx4"]))
        const_loads.append((qxf[QX:P, :], A["qx"]))
        const_loads.append((wr0[:, :, :], A["wr0"]))
        const_loads.append((wr1[:, :, :], A["wr1"]))
        n_consts = 16 * len(const_loads)

        attn_at = [p for p, cfg in enumerate(phases) if cfg["kind"] == "attn"]
        ready_in = {0 if n == 0 else attn_at[n - 1] + 1: p for n, p in enumerate(attn_at)}

        block = ctx.enter_context(nc.Block())
        nphase = len(phases)

        def sp_ffn(e, p, cfg):
            n = cfg["chunks"]
            w = A[cfg["w"]]

            def load(c, b):
                e.dma_start(wraw[:, b, :], w[bass.ds(c, 1), :, :].rearrange("o p n -> (o p) n"))\
                    .then_inc(s("w_loaded%d" % b), 16)

            if p > 0:
                prev = phases[p - 1]
                if prev["kind"] == "ffn":
                    e.wait_ge(*nth(p - 1, "w_hi", prev["chunks"]))
                    e.wait_ge(*nth(p - 1, "wd_lo", prev["chunks"]))
                else:
                    e.wait_ge(*nth(p - 1, "pv_done", prev["pairs"] // 2))
            load(0, 0)
            load(1, 1)

            def next_chunk(c, b):
                e.wait_ge(*nth(p, "w_hi", c - 1))
                e.wait_ge(*nth(p, "wd_lo", c - 1))
                load(c, b)
                if p == 0 and isinstance(c, int) and 5 <= c < 5 + TABLE_PARTS:
                    store_tables(e, c - 5)

            c = 2
            if p in ready_in:
                q = ready_in[p]
                if p > 0:
                    e.wait_ge(*nth(p - 1, "sums", 2))
                split_at = 2 + (TABLE_PARTS if p == 0 else 0)
                for k in range(4):
                    if k == 2:
                        while c < split_at + 2:
                            next_chunk(c, c % 2)
                            c += 1
                    if k >= 2:
                        next_chunk(c, c % 2)
                        c += 1
                        e.wait_ge(*nth(q, "aw_split", k - 1))
                    e.dma_start(araw[:, k % 2, :], A[phases[q]["w"]][k, :, :]).then_inc(s("aw_loaded%d" % (k % 2)), 16)
            with e.Fori(0, (n - c) // 2) as i:
                for b in range(2):
                    next_chunk(2 * i + c + b, b)
            if n % 2:
                next_chunk(n - 1, (n - 1) % 2)

        def store_tables(e, part):
            e.wait_ge(kxl_done, part + 1)
            if part < QUADS:
                heads = slice(QUAD * part, QUAD * (part + 1))
                stores = [(kext_d[k, heads, :, :].rearrange("j r t -> (j r) t"), table[:, part, :])
                          for k, table in enumerate((kxh, kxl))]
            else:
                heads = slope_part(part)
                stores = [(sdiag_d[k, :, P * heads.start:P * heads.stop],
                           table[:, heads, :].rearrange("p h n -> p (h n)"))
                          for k, table in enumerate((slope_h, slope_l))]
            if part == TABLE_PARTS - 1:
                e.wait_ge(setup, 7)
                e.wait_ge(qxr_done, 1)
                stores += [(qext_d, qxr[QX:P, :]), (zero_d, zero_r[QX:P, :])]
            for dst, src in stores:
                e.dma_start(dst, hi_f(src)).then_inc(tables, 16)

        def row_loads(e, p, g, name):
            slots = slice(QUAD * (g % SETS), QUAD * (g % SETS + 1))
            for r in range(4):
                rows = slice(HD * r, HD * (r + 1))
                for w, dst, part in ((0, qs, r // 2), (1, ks, r % 2)):
                    e.dma_start(hi_f(dst[rows, slots, :]),
                                qk_d[w, part, QUAD * HD * g:QUAD * HD * (g + 1), :]
                                .rearrange("(j r) t -> r j t", j=QUAD)).then_inc(s(name), 16)

        def sp_attn(e, p, cfg):
            def constant_rows(k, done):
                slots = slice(QUAD * k, QUAD * (k + 1))
                if cfg["causal"]:
                    e.dma_start(hi_f(qs[QX:P, slots, :]).rearrange("p s (h c) -> p (s h) c", h=2),
                                zero_d.unsqueeze(1).to_broadcast([P - QX, QUAD * 2, HALF])).then_inc(done, 16)
                    for part in range(2):
                        e.dma_start(hi_f(ks[QX + 32 * part:QX + 32 * (part + 1), slots, :]),
                                    kext_d[part, 0, :, :].unsqueeze(1).to_broadcast([32, QUAD, T])).then_inc(done, 16)
                else:
                    e.dma_start(hi_f(qs[QX:P, slots, :]), qext_d.unsqueeze(1).to_broadcast([P - QX, QUAD, T]))\
                        .then_inc(done, 16)

            e.wait_ge(*nth(p, "region_free", 1))
            constant_rows(0, s("ext_loaded0"))
            for k in range(8):
                m, w, half = k // 4, (k // 2) % 2, k % 2
                if k == 4:
                    for part in ("hi", "lo"):
                        e.wait_ge(*nth(p, part + "_stored0", 64))
                    row_loads(e, p, 0, "first_rows_loaded")
                for name, part, src in (("hi", 0, chi), ("lo", 1, clo)):
                    e.wait_ge(*nth(p, name + "_q", k + 1))
                    e.dma_start(qk_d[w, part, P * m:P * (m + 1), HALF * half:HALF * (half + 1)],
                                hi_f(src[:, k % 4, :])).then_inc(s("%s_stored%d" % (name, m)), 16)
            for k in range(1, SETS):
                constant_rows(k, s("ext_loaded1"))

        @block.sync
        def _(e):
            for half in range(HALVES):
                tiles = slice(4 * half, 4 * (half + 1))
                e.dma_start(x[:, tiles, :], A["x"].rearrange("o (t p) d -> p (o t) d", p=P)[:, tiles, :])\
                    .then_inc(x_loaded[half], 16)
                if half == 0:
                    e.dma_start(ident[:, :], A["ident"]).then_inc(ident_loaded, 16)
            for dst, src in const_loads:
                e.dma_start(dst, src).then_inc(consts, 16)
            for p, cfg in enumerate(phases):
                if cfg["kind"] == "ffn":
                    sp_ffn(e, p, cfg)
                else:
                    sp_attn(e, p, cfg)
            for half in range(HALVES):
                e.wait_ge(*nth(nphase, "x_added", 2 * (half + 1)))
                tiles = slice(4 * half, 4 * (half + 1))
                e.dma_start(out.rearrange("o (t p) d -> p (o t) d", p=P)[:, tiles, :], x[:, tiles, :])\
                    .then_inc(out_done, 16)
            e.wait_ge(out_done, 16 * HALVES)

        def ot_of(p):
            return ot if phases[p]["kind"] == "ffn" else ot_attn

        def pe_to_features(e, p, tag, half):
            if tag == "ln":
                e.wait_ge(*nth(p, "ln_in", 2 * (half + 1)))
                e.wait_ge(*nth(p, "ln_in_act", 2 * (half + 1)))
            else:
                e.wait_ge(*nth(p, "z_norm", HALVES * (QUADS - 1) + half + 1))
            for c in range(KC):
                for t in range(4):
                    mm = e.transpose(ps[:, BANKS[half][c], P * t:P * (t + 1)], xn[:, 4 * half + t, P * c:P * (c + 1)],
                                     ident[:, :])
                mm.then_inc(s(tag + "_banks"), 1)

        def pe_finish(e, p, half):
            e.wait_ge(*nth(p, "ot_done", 2 * (half + 1)))
            for k in range(2):
                for u in range(2):
                    t = 2 * k + u
                    for c in range(KC):
                        mm = e.transpose(ps[:, BANKS[half][k], D * u + P * c:D * u + P * (c + 1)],
                                         ot_of(p)[:, 2 * c + half, P * t:P * (t + 1)], ident[:, :])
                mm.then_inc(s("out_banks"), 1)

        def pe_ffn(e, p, cfg):
            n, r = cfg["chunks"], cfg["router"]
            for half in range(HALVES):
                pe_to_features(e, p, "ln", half)
            if p == 0:
                e.wait_ge(setup, 7)
            for half in range(HALVES):
                e.wait_ge(*nth(p, "ln_hi", 2 * (half + 1)))
                e.wait_ge(*nth(p, "ln_lo", 2 * (half + 1)))
                tok = slice(HALF * half, HALF * (half + 1))
                terms = three([(wrh[:, r, c, :], wrl[:, r, c, :], xz[:, c, tok], xz[:, KC + c, tok]) for c in range(KC)])
                for k, (a, b) in enumerate(terms):
                    mm = e.matmul(ps[0:RC, half, :], a, b, start=(k == 0), stop=(k == len(terms) - 1))
                mm.then_inc(s("logits_t"), 1)

            def proj(c, b, t, bank, col, last):
                tok = slice(HALF * t, HALF * (t + 1))
                terms = three([(whi[:, b, col + P * k:col + P * (k + 1)], wlo[:, b, col + P * k:col + P * (k + 1)],
                                xz[:, k, tok], xz[:, KC + k, tok]) for k in range(KC)])
                for k, (w, v) in enumerate(terms):
                    mm = e.matmul(ps[:, bank, :], w, v, start=(k == 0), stop=(k == len(terms) - 1))
                mm.then_inc(s(last), 1)

            def down(step, b, t, first=False, last=False):
                e.wait_ge(*nth(p, "h_hi", step + 1))
                e.wait_ge(*nth(p, "h_lo", step + 1))
                for d in range(KC):
                    terms = three([(whi[:, b, WD + P * d:WD + P * (d + 1)], wlo[:, b, WD + P * d:WD + P * (d + 1)],
                                    hh[:, t, :], hl[:, t, :])])
                    for k, (w, v) in enumerate(terms):
                        mm = e.matmul(ps[:, 2 * d + t, :], w, v, start=first and k == 0,
                                      stop=last and k == len(terms) - 1, skip_group_check=True)
                if not last:
                    mm.then_inc(s("down_done"), 1)
                return mm

            def comb(b, t):
                e.matmul(ps[:, 6, :], whi[:, b, WSEL:WSEL + P], cwT[:, HALF * t:HALF * (t + 1)],
                         start=True, stop=True).then_inc(s("comb"), 1)

            def step(c, b, t):
                k = 2 * c + t
                if t == 0:
                    e.wait_ge(*nth(p, "w_hi", c + 1))
                    e.wait_ge(*nth(p, "w_lo", c + 1))
                e.wait_ge(*nth(p, "silu", k))
                proj(c, b, t, 4, WG, "gate")
                e.wait_ge(*nth(p, "h_done", k))
                comb(b, t)
                e.wait_ge(*nth(p, "su_done", k))
                proj(c, b, t, 5, WU, "up")
                if t == 1:
                    e.wait_ge(*nth(p, "wd_lo", c + 1))
                down(k - 1, b if t else 1 - b, 1 - t)

            e.wait_ge(*nth(p, "logits_copy", 2))
            for t in range(TILES):
                mm = e.transpose(ps[:, 2, RC * t:RC * (t + 1)], lgT[:, P * t:P * (t + 1)], ident[0:RC, 0:RC])
            mm.then_inc(s("logits"), 1)
            e.wait_ge(*nth(p, "w_hi", 1))
            e.wait_ge(*nth(p, "w_lo", 1))
            proj(0, 0, 0, 4, WG, "gate")
            proj(0, 0, 0, 5, WU, "up")
            proj(0, 0, 1, 6, WG, "gate")
            proj(0, 0, 1, 7, WU, "up")
            e.wait_ge(*nth(p, "cw_done", 1))
            for t in range(TILES):
                mm = e.transpose(ps[0:RC, t // 4, P * (t % 4):P * (t % 4 + 1)], cw[:, t, :], ident[:, :])
            mm.then_inc(s("cw_banks"), 1)

            def zeros(banks, **group):
                for o in banks:
                    mm = e.matmul(ps[:, o, :], zero_r[:, 0:P], zero_r[:, :], skip_group_check=True, **group)
                return mm

            zeros((3,), start=True, stop=False)
            e.wait_ge(*nth(p, "silu", 2))
            e.wait_ge(*nth(p, "cwT_lo", 1))
            comb(0, 0)
            e.wait_ge(*nth(p, "cwT_lo", 2))
            zeros((1,), start=True, stop=False)
            e.wait_ge(*nth(p, "h_done", 1))
            comb(0, 1)
            e.wait_ge(*nth(p, "wd_lo", 1))
            down(0, 0, 0, first=True)
            with e.Fori(0, (n - 1) // 2) as i:
                for u in range(2):
                    for t in range(2):
                        step(2 * i + 1 + u, (1 + u) % 2, t)
            if n % 2 == 0:
                step(n - 1, (n - 1) % 2, 0)
                step(n - 1, (n - 1) % 2, 1)
            zeros((0, 2), start=False, stop=True).then_inc(s("sums"), 1)
            e.wait_ge(*nth(p, "silu", 2 * n))
            pe_finish(e, p, 0)
            down(2 * n - 1, (n - 1) % 2, 1, last=True).then_inc(s("sums"), 1)
            pe_finish(e, p, 1)

        def pe_attn(e, p, cfg):
            for half in range(HALVES):
                pe_to_features(e, p, "ln", half)
            n = 0
            e.wait_ge(*nth(p, "aw_split", 4))
            for m in range(KC):
                for w in range(2):
                    for half in range(HALVES):
                        if n >= 4:
                            e.wait_ge(*nth(p, "lo_q", n - 3))
                        if n < 2:
                            e.wait_ge(*nth(p, "ln_hi", 2 * (half + 1)))
                            e.wait_ge(*nth(p, "ln_lo", 2 * (half + 1)))
                        tok = slice(HALF * half, HALF * (half + 1))
                        terms = three([(awh[:, w, D * c + P * m:D * c + P * (m + 1)],
                                        awl[:, w, D * c + P * m:D * c + P * (m + 1)],
                                        xz[:, c, tok], xz[:, KC + c, tok]) for c in range(KC)])
                        for k, (a, b) in enumerate(terms):
                            mm = e.matmul(ps[:, n % 4, :], a, b, start=(k == 0), stop=(k == len(terms) - 1))
                        mm.then_inc(s("qk_banks"), 1)
                        n += 1
            for t in range(TILES):
                if t >= 4:
                    e.wait_ge(*nth(p, "v_done", t - 3))
                tok = slice(P * t, P * (t + 1))
                terms = three([(xz[:, c, tok], xz[:, KC + c, tok],
                                awh[:, 2, D * c:D * (c + 1)], awl[:, 2, D * c:D * (c + 1)])
                               for c in range(KC)])
                for k, (a, b) in enumerate(terms):
                    mm = e.matmul(ps[:, 4 + t % 4, 0:D], a, b, start=(k == 0), stop=(k == len(terms) - 1))
                mm.then_inc(s("v_banks"), 1)
            e.wait_ge(*nth(p, "lo_q", 8))
            e.wait_ge(*nth(p, "v_done", 8))

            def bank_read(before):
                if before:
                    kind, n = before
                    if kind == "max":
                        e.wait_ge(*nth(p, "reduced", n))
                    elif kind == "mrows":
                        e.wait_ge(*nth(p, "m_act", 2 * n))
                        e.wait_ge(*nth(p, "m_dve", 2 * n))
                    else:
                        e.wait_ge(*nth(p, "z_norm", n))

            nmx = nsc = npv = nz = 0
            for (kind, g, arg), (bank, before) in zip(cfg["order"], cfg["place"]):
                par = g % SETS
                if kind == "max":
                    j, qt, kh, w = arg
                    sl = QUAD * par + j
                    if nmx == cfg["nitems"]:
                        e.wait_ge(*nth(p, "ext_loaded1", signals(cfg)["ext_loaded1"]))
                    if nmx == 0:
                        e.wait_ge(*nth(p, "first_rows_loaded", 16 * 8))
                        e.wait_ge(*nth(p, "ext_loaded0", signals(cfg)["ext_loaded0"]))
                    if nmx % cfg["nitems"] == 0 and (g or not cfg["causal"]):
                        e.wait_ge(*nth(p, "rows_loaded%d" % g, signals(cfg)["rows_loaded%d" % g]))
                    bank_read(before)
                    diag = qt // 4 == kh
                    mm = e.matmul(ps[:, bank, 0:w], qs[:, sl, P * qt:P * (qt + 1)], ks[:, sl, HALF * kh:HALF * kh + w],
                                  start=True, stop=not diag)
                    if diag:
                        o = ps[:, bank, P * (qt % 4):P * (qt % 4 + 1)]
                        if cfg["causal"]:
                            mm = e.matmul(o, ident_r[:, :], causal_r[:, :], start=False, stop=True)
                        else:
                            e.matmul(o, sdiag[:, par, 0, j, :], dist_r[:, :], start=False, stop=False)
                            mm = e.matmul(o, sdiag[:, par, 1, j, :], dist_r[:, :], start=False, stop=True)
                    mm.then_inc(s("max_banks"), 1)
                    nmx += 1
                elif kind == "mrows":
                    u = 2 * g + arg
                    e.wait_ge(*nth(p, "nm_hi", u + 1))
                    e.wait_ge(*nth(p, "nm_lo", u + 1))
                    bank_read(before)
                    for t in range(4):
                        mm = e.transpose(ps[:, bank, P * t:P * (t + 1)], hi_f(nmp[:, u % 2, t, :]), ident[:, :])
                    mm.then_inc(s("m_bank"), 1)
                elif kind == "score":
                    (qh, kt, off), pair, first = arg
                    if first:
                        e.wait_ge(*nth(p, "m_act", 2 * (2 * g + qh + 1)))
                        e.wait_ge(*nth(p, "m_dve", 2 * (2 * g + qh + 1)))
                    if nsc >= 2:
                        e.wait_ge(*nth(p, "exp_done", nsc - 1))
                    diag = kt // 4 == qh
                    for u in range(2):
                        j = 2 * pair + u
                        sl = QUAD * par + j
                        sbank = 2 * (nsc % 2) + u
                        mm = e.matmul(ps[:, sbank, off:HALF], ks[:, sl, P * kt:P * (kt + 1)],
                                      qs[:, sl, HALF * qh + off:HALF * (qh + 1)], start=True, stop=not diag)
                        if diag:
                            dcol = P * (kt - 4 * qh)
                            o = ps[:, sbank, dcol:dcol + P]
                            if cfg["causal"]:
                                mm = e.matmul(o, causal_r[:, :], ident_r[:, :], start=False, stop=True)
                            else:
                                e.matmul(o, sdiag[:, par, 0, j, :], dist_r[:, :], start=False, stop=False)
                                mm = e.matmul(o, sdiag[:, par, 1, j, :], dist_r[:, :], start=False, stop=True)
                    mm.then_inc(s("score_banks"), 1)
                    nsc += 1
                elif kind == "pv":
                    qh, kt, off = arg
                    e.wait_ge(*nth(p, "exp_done", 2 * npv + 2))
                    if kt == 0 and (g or qh):
                        e.wait_ge(*nth(p, "z_raw", 2 * g + qh))
                    for j in range(QUAD):
                        mm = e.matmul(ps[32 * j:32 * (j + 1), 6, off:HALF], vaug[:, kt, QUAD * g + j, :],
                                      pt[:, (2 * npv + j // 2) % RING, j % 2, off:HALF],
                                      start=(kt == 0), stop=(kt == cfg["last_kt"][qh]))
                    mm.then_inc(s("pv_done"), 1)
                    npv += 1
                elif kind == "z":
                    e.wait_ge(*nth(p, "z_raw", nz + 1))
                    bank_read(before)
                    for t in range(4):
                        mm = e.transpose(ps[:, bank, P * t:P * (t + 1)], zraw[:, nz % 2, P * t:P * (t + 1)], ident[:, :])
                    mm.then_inc(s("z_bank"), 1)
                    nz += 1
                elif kind == "feat":
                    e.wait_ge(*nth(p, "reduced", nmx))
                    e.wait_ge(*nth(p, "m_act", 2 * HALVES * QUADS))
                    e.wait_ge(*nth(p, "m_dve", 2 * HALVES * QUADS))
                    pe_to_features(e, p, "z", 0)

            def project(half):
                e.wait_ge(*nth(p, "z_hi", 2 * (half + 1)))
                e.wait_ge(*nth(p, "z_lo", 2 * (half + 1)))
                tok = slice(HALF * half, HALF * (half + 1))
                for m in range(KC):
                    terms = three([(awo[:, 0, D * c + P * m:D * c + P * (m + 1)],
                                    awo[:, 1, D * c + P * m:D * c + P * (m + 1)],
                                    xz[:, c, tok], xz[:, KC + c, tok]) for c in range(KC)])
                    for k, (a, b) in enumerate(terms):
                        mm = e.matmul(ps[:, 2 * m + half, :], a, b, start=(k == 0), stop=(k == len(terms) - 1))
                mm.then_inc(s("sums"), 1)

            e.wait_ge(*nth(p, "exp_done", nsc))
            project(0)
            pe_to_features(e, p, "z", 1)
            pe_finish(e, p, 0)
            project(1)
            pe_finish(e, p, 1)

        @block.tensor
        def _(e):
            e.wait_ge(ident_loaded, 16)
            for p, cfg in enumerate(phases):
                (pe_ffn if cfg["kind"] == "ffn" else pe_attn)(e, p, cfg)

        def act_to_features(e, p, tag, half):
            for c in range(KC):
                e.wait_ge(*nth(p, tag + "_banks", 2 * half + c + 1))
                e.activation(xz[:, c, HALF * half:HALF * (half + 1)], ps[:, BANKS[half][c], :], ACT.Copy)\
                    .then_inc(s(tag + "_hi"), 1)

        def act_split(e, p, c, b, pair):
            e.wait_ge(*nth(p, "w_loaded%d" % b, 16 * (pair + 1)))
            if not isinstance(c, int) or c >= 2:
                e.wait_ge(*nth(p, "down_done", 2 * (c - 1)))
            e.activation(whi[:, b, :], wraw[:, b, :], ACT.Copy).then_inc(s("w_hi"), 1)

        def act_norm(e, p):
            for half in range(HALVES):
                part = slice(4 * half, 4 * (half + 1))
                e.wait_ge(*nth(p, "var", 4 * (half + 1)))
                e.activation(std[:, part], mv[:, part, 1], ACT.Sqrt, bias=eps[:, 0:1]).then_inc(s("std"), 1)
                e.wait_ge(*nth(p, "shift", half + 1))
                for t in range(4 * half + 2, 4 * half + 4):
                    e.activation(xn[:, t, :], x[:, t, :], ACT.Identity, bias=shift[:, t:t + 1], scale=rstd[:, t:t + 1])\
                        .then_inc(s("ln_in_act"), 1)
                if half == 1 and phases[p]["kind"] == "ffn":
                    act_split(e, p, 0, 0, 0)
                act_to_features(e, p, "ln", half)

        def act_finish(e, p, half, chunks=range(KC)):
            e.wait_ge(*nth(p, "sums", half + 1))
            bias = phases[p]["kind"] == "attn" and not phases[p]["causal"]
            for c in chunks:
                o = 2 * c + half
                if bias:
                    e.activation(ot_of(p)[:, o, :], ps[:, o, :], ACT.Identity, bias=cols[:, 4 + c:5 + c])\
                        .then_inc(s("ot_done"), 1)
                else:
                    e.activation(ot_of(p)[:, o, :], ps[:, o, :], ACT.Copy).then_inc(s("ot_done"), 1)

        def act_tables(e, part):
            if part < QUADS:
                e.wait_ge(kxp_done, part + 1)
                e.activation(kxh[:, part, :], kxp[:, part % 2, :], ACT.Copy).then_inc(kxh_done, 1)
            else:
                heads = slope_part(part)
                e.wait_ge(slope_done, 1)
                e.activation(slope_h[:, heads, :], slope_i[:, heads, :], ACT.Copy).then_inc(slope_hi, 1)
                if part == TABLE_PARTS - 1:
                    e.activation(qxr[QX:P, :], qxf[QX:P, :], ACT.Copy).then_inc(qxr_done, 1)

        def act_ffn(e, p, cfg):
            n, K, E = cfg["chunks"], cfg["topk"], cfg["experts"]

            def silu(k, t, bank):
                e.wait_ge(*nth(p, "gate", k + 1))
                if not isinstance(k, int) or k >= 2:
                    e.wait_ge(*nth(p, "su_done", k - 1))
                e.activation(sg[:, t, :], ps[:, bank, :], ACT.Silu).then_inc(s("silu"), 1)

            def h_hi(k, t):
                e.wait_ge(*nth(p, "h_done", k + 1))
                if not isinstance(k, int) or k >= 2:
                    e.wait_ge(*nth(p, "down_done", k - 1))
                e.activation(hh[:, t, :], hf[:, t, :], ACT.Copy).then_inc(s("h_hi"), 1)

            def step(c, t):
                silu(2 * c + t, t, 4)
                h_hi(2 * c + t, t)

            first = TABLE_PARTS + 1 if p == 0 else 1
            act_norm(e, p)
            for half in range(HALVES):
                e.wait_ge(*nth(p, "logits_t", half + 1))
                e.activation(lgT[:, HALF * half:HALF * (half + 1)], ps[0:RC, half, :], ACT.Copy)\
                    .then_inc(s("logits_copy"), 1)
            e.wait_ge(*nth(p, "dv_done", 1))
            e.activation(ev[:, :, 0:K], dv[:, :, 0:K], ACT.Exp).then_inc(s("exps"), 1)
            if cfg["gated"]:
                e.wait_ge(*nth(p, "dl_done", 1))
                e.activation(el[:, :, 0:E], dl[:, :, 0:E], ACT.Exp).then_inc(s("exps"), 1)
                e.activation(zg[:, :], lg[:, :, E], ACT.Exp, scale=-1.0).then_inc(s("exps"), 1)
            silu(0, 0, 4)
            silu(1, 1, 6)
            act_split(e, p, 1, 1, 0)
            e.wait_ge(*nth(p, "cw_banks", 1))
            for k in range(2):
                e.activation(cwT[0:RC, HALF * k:HALF * (k + 1)], ps[0:RC, k, :], ACT.Copy).then_inc(s("cwT_hi"), 1)
            h_hi(0, 0)
            h_hi(1, 1)
            if p == 0:
                e.wait_ge(consts, n_consts)
            for c in range(1, first):
                step(c, 0)
                act_split(e, p, c + 1, (c + 1) % 2, (c + 1) // 2)
                step(c, 1)
                act_tables(e, c - 1)
            with e.Fori(0, (n - 1) // 2 - 1 - first // 2) as i:
                for u in range(2):
                    step(first + 2 * i + u, 0)
                    act_split(e, p, first + 2 * i + u + 1, u, first // 2 + i + 1)
                    step(first + 2 * i + u, 1)
            for c in range(n - 2 if n % 2 else n - 3, n):
                step(c, 0)
                if c + 1 < n:
                    act_split(e, p, c + 1, (c + 1) % 2, (c + 1) // 2)
                    step(c, 1)
            silu(2 * n - 1, 1, 4)
            act_finish(e, p, 0, (0,))
            h_hi(2 * n - 1, 1)
            act_finish(e, p, 0, (1,))
            act_finish(e, p, 1)

        def act_attn(e, p, cfg):
            act_norm(e, p)
            e.wait_ge(*nth(p, "region_free", 1))
            if not cfg["causal"]:
                e.wait_ge(*nth(p, "bias_scaled", 1))
            for k in range(8):
                m, w = k // 4, (k // 2) % 2
                e.wait_ge(*nth(p, "qk_banks", k + 1))
                if k == 4:
                    e.wait_ge(*nth(p, "hi_stored0", 64))
                if cfg["causal"]:
                    e.activation(chi[:, k % 4, :], ps[:, k % 4, :], ACT.Copy).then_inc(s("hi_q"), 1)
                else:
                    e.activation(chi[:, k % 4, :], ps[:, k % 4, :], ACT.Identity, bias=cols[:, 2 * w + m:2 * w + m + 1])\
                        .then_inc(s("hi_q"), 1)
            if cfg["causal"]:
                for t in range(TILES):
                    e.wait_ge(*nth(p, "v_banks", t + 1))
                    if t == 0:
                        e.wait_ge(*nth(p, "v_init", 4))
                    e.activation(vaug[:, t, :, 0:HD], ps[:, 4 + t % 4, 0:D].rearrange("p (h d) -> p h d", d=HD),
                                 ACT.Copy)\
                        .then_inc(s("v_done"), 1)
            nsc = nz = 0
            for (kind, g, arg), (bank, before) in zip(cfg["order"], cfg["place"]):
                if kind == "mrows":
                    sl = slice(HALF * arg, HALF * (arg + 1))
                    e.wait_ge(*nth(p, "m_bank", 2 * g + arg + 1))
                    for j in range(2):
                        e.activation(qs[MROW:MROW + 2, QUAD * (g % SETS) + j, sl], ps[RC * j:RC * j + 2, bank, :],
                                     ACT.Copy)\
                            .then_inc(s("m_act"), 1)
                elif kind == "score":
                    (qh, kt, off), pair, _ = arg
                    e.wait_ge(*nth(p, "score_banks", nsc + 1))
                    if nsc >= RING:
                        e.wait_ge(*nth(p, "pv_done", nsc // 2 - 1))
                    b = 2 * (nsc % 2)
                    e.activation(pt[:, nsc % RING, :, off:HALF], ps[:, b:b + 2, off:HALF], ACT.Exp)\
                        .then_inc(s("exp_done"), 1)
                    nsc += 1
                elif kind == "zcopy":
                    e.wait_ge(*nth(p, "pv_done", cfg["z_pv"][nz]))
                    if nz >= 2:
                        e.wait_ge(*nth(p, "z_bank", nz - 1))
                    e.activation(zraw[:, nz % 2, :], ps[:, 6, :], ACT.Copy).then_inc(s("z_raw"), 1)
                    nz += 1
                elif kind == "feat":
                    act_to_features(e, p, "z", 0)
            act_finish(e, p, 0)
            act_to_features(e, p, "z", 1)
            act_finish(e, p, 1)

        @block.scalar
        def _(e):
            e.wait_ge(setup, 1)
            for p, cfg in enumerate(phases):
                (act_ffn if cfg["kind"] == "ffn" else act_attn)(e, p, cfg)

        def dve_to_features(e, p, tag, half):
            for c in range(KC):
                e.wait_ge(*nth(p, tag + "_hi", 2 * half + c + 1))
                sl = slice(HALF * half, HALF * (half + 1))
                e.tensor_tensor(xz[:, KC + c, sl], ps[:, BANKS[half][c], :], hi_f(xz[:, c, sl]), ALU.subtract)\
                    .then_inc(s(tag + "_lo"), 1)

        def dve_add(e, p, half):
            for k in range(2):
                e.wait_ge(*nth(p - 1, "out_banks", 2 * half + k + 1))
                t = 4 * half + 2 * k
                xx = x[:, t:t + 2, :].rearrange("p t d -> p (t d)")
                e.tensor_tensor(xx, ps[:, BANKS[half][k], :], xx, ALU.add).then_inc(s("x_added"), 1)

        def dve_round_constants(e):
            e.wait_ge(ident_loaded, 16)
            e.wait_ge(consts, n_consts)
            e.tensor_copy(ident_r[:, :], ident[:, :]).then_inc(setup, 1)
            e.tensor_copy(dist_r[:, :], dist[:, :]).then_inc(setup, 1)
            e.tensor_copy(causal_r[:, :], causal[:, :]).then_inc(setup, 1)
            e.tensor_copy(wrh[:, 0, :, :], wr0[:, :, :]).then_inc(wr_hi, 1)
            e.tensor_copy(wrh[:, 1, :, :], wr1[:, :, :]).then_inc(wr_hi, 1)
            e.wait_ge(wr_hi, 2)
            e.tensor_tensor(wrl[:, 0, :, :], wr0[:, :, :], hi_f(wrh[:, 0, :, :]), ALU.subtract).then_inc(setup, 1)
            e.tensor_tensor(wrl[:, 1, :, :], wr1[:, :, :], hi_f(wrh[:, 1, :, :]), ALU.subtract).then_inc(setup, 1)

        def dve_slopes(e):
            e.tensor_scalar(srow4[:, :], slope4[:, :], keep[:, 0:1], keep[:, 1:2], ALU.mult, ALU.add)\
                .then_inc(srow_done, 1)
            e.tensor_tensor(slope_i[:, :, :], ident[:, :].unsqueeze(1).to_broadcast([P, NH, P]),
                            slopes[:, :].unsqueeze(2).to_broadcast([P, NH, P]), ALU.mult).then_inc(slope_done, 1)
            e.wait_ge(srow_done, 1)

        def dve_norm(e, p):
            for half in range(HALVES):
                if p > 0:
                    dve_add(e, p, half)
                part = slice(4 * half, 4 * (half + 1))
                for t in range(4 * half, 4 * (half + 1)):
                    if p == 0 and t % 4 == 0:
                        e.wait_ge(x_loaded[half], 16)
                    if p > 0:
                        e.wait_ge(*nth(p, "x_added", t // 2 + 1))
                    e.bn_stats(stats[:, t, :], x[:, t, :]).then_inc(s("bn"), 1)
                for t in range(4 * half, 4 * (half + 1)):
                    e.wait_ge(*nth(p, "bn", t + 1))
                    e.bn_aggr(mv[:, t, :], stats[:, t, :]).then_inc(s("var"), 1)
                e.wait_ge(*nth(p, "std", half + 1))
                e.reciprocal(rstd[:, part], std[:, part]).then_inc(s("rstd"), 1)
                e.wait_ge(*nth(p, "rstd", half + 1))
                e.scalar_tensor_tensor(shift[:, part], mv[:, part, 0], -1.0, rstd[:, part], ALU.mult, ALU.mult)\
                    .then_inc(s("shift"), 1)
                for t in range(4 * half, 4 * half + 2):
                    e.tensor_scalar(xn[:, t, :], x[:, t, :], mv[:, t, 0:1], rstd[:, t:t + 1], ALU.subtract, ALU.mult)\
                        .then_inc(s("ln_in"), 1)
            if p == 0:
                dve_round_constants(e)
            for half in range(HALVES):
                dve_to_features(e, p, "ln", half)

        def dve_ffn(e, p, cfg):
            n, K, E = cfg["chunks"], cfg["topk"], cfg["experts"]
            dve_norm(e, p)
            ch, cnt = s("router_step"), router_steps

            def did(ins):
                cnt[0] += 1
                ins.then_inc(ch, 1)

            def settle():
                e.wait_ge(ch, cnt[0])

            if p == 0 or phases[p - 1]["kind"] == "attn":
                did(e.memset(hi_f(cwT[:, :]), 0.0))
            did(e.memset(cw[:, :, :], 0.0))
            e.wait_ge(*nth(p, "logits", 1))
            did(e.tensor_copy(lg[:, :, :], ps[:, 2, 0:TILES * RC].rearrange("p (t r) -> p t r", r=RC)))
            settle()
            for t in range(TILES):
                did(e.max(top8[:, t, :], lg[:, t, 0:E]))
            settle()
            best = top8[:, :, 0:1]
            e.tensor_tensor(dv[:, :, 0:K], top8[:, :, 0:K], best.to_broadcast([P, TILES, K]), ALU.subtract)\
                .then_inc(s("dv_done"), 1)
            if cfg["gated"]:
                e.tensor_tensor(dl[:, :, 0:E], lg[:, :, 0:E], best.to_broadcast([P, TILES, E]), ALU.subtract)\
                    .then_inc(s("dl_done"), 1)
            for t in range(TILES):
                did(e.max_index(idx8[:, t, :], top8[:, t, :], lg[:, t, 0:E]))
            settle()
            did(e.tensor_copy(idxf[:, :, :], idx8[:, :, :]))
            settle()
            oh = onehot[:, 0:TILES * K, 0:E].rearrange("p (t k) e -> p t k e", k=K)
            ow = onew[:, 0:TILES * K, 0:E].rearrange("p (t k) e -> p t k e", k=K)
            did(e.tensor_tensor(oh, idxf[:, :, 0:K].unsqueeze(3).to_broadcast([P, TILES, K, E]),
                                iota[:, 0:E].unsqueeze(1).unsqueeze(1).to_broadcast([P, TILES, K, E]), ALU.is_equal))
            e.wait_ge(*nth(p, "exps", 3 if cfg["gated"] else 1))
            if cfg["gated"]:
                did(e.tensor_reduce(ssum[:, :], el[:, :, 0:E], AX.X, ALU.add))
                did(e.tensor_scalar(zg1[:, :], zg[:, :], 1.0, None, ALU.add))
            else:
                did(e.tensor_reduce(ssum[:, :], ev[:, :, 0:K], AX.X, ALU.add))
            settle()
            did(e.reciprocal(rsum[:, :], ssum[:, :]))
            if cfg["gated"]:
                did(e.reciprocal(zg2[:, :], zg1[:, :]))
            settle()
            did(e.scalar_tensor_tensor(wk[:, :, 0:K], ev[:, :, 0:K], cfg["moe_scale"],
                                       rsum[:, :].unsqueeze(2).to_broadcast([P, TILES, K]), ALU.mult, ALU.mult))
            if cfg["gated"]:
                did(e.tensor_scalar(cw[:, :, E], zg2[:, :], cfg["shared_scale"], None, ALU.mult))
            else:
                did(e.memset(cw[:, :, E:E + 1], cfg["shared_scale"]))
            settle()
            did(e.tensor_tensor(ow, oh, wk[:, :, 0:K].unsqueeze(3).to_broadcast([P, TILES, K, E]), ALU.mult))
            settle()
            e.tensor_reduce(cw[:, :, 0:E], ow.rearrange("p t k e -> p t e k"), AX.X, ALU.add)\
                .then_inc(s("cw_done"), 1)

            def gate(k, t, bank):
                e.wait_ge(*nth(p, "up", k + 1))
                e.wait_ge(*nth(p, "silu", k + 1))
                e.tensor_tensor(su[:, t, :], ps[:, bank, :], sg[:, t, :], ALU.mult).then_inc(s("su_done"), 1)

            def weigh(k, t):
                e.wait_ge(*nth(p, "comb", k + 1))
                e.wait_ge(*nth(p, "su_done", k + 1))
                if not isinstance(k, int) or k >= 2:
                    e.wait_ge(*nth(p, "h_hi", k - 1))
                e.tensor_tensor(hf[:, t, :], ps[:, 6, :], su[:, t, :], ALU.mult).then_inc(s("h_done"), 1)

            def h_lo(k, t):
                e.wait_ge(*nth(p, "h_hi", k + 1))
                if not isinstance(k, int) or k >= 2:
                    e.wait_ge(*nth(p, "down_done", k - 1))
                e.tensor_tensor(hl[:, t, :], hf[:, t, :], hi_f(hh[:, t, :]), ALU.subtract).then_inc(s("h_lo"), 1)

            def step(c, t):
                gate(2 * c + t, t, 5)
                weigh(2 * c + t, t)
                h_lo(2 * c + t, t)

            gate(0, 0, 5)
            gate(1, 1, 7)
            for k in range(2):
                e.wait_ge(*nth(p, "cwT_hi", k + 1))
                sl = slice(HALF * k, HALF * (k + 1))
                e.tensor_tensor(cwT[RC:2 * RC, sl], ps[0:RC, k, :], hi_f(cwT[0:RC, sl]), ALU.subtract)\
                    .then_inc(s("cwT_lo"), 1)
            weigh(0, 0)
            weigh(1, 1)
            h_lo(0, 0)
            h_lo(1, 1)
            first = TABLE_PARTS + 1 if p == 0 else 1
            if p == 0:
                dve_slopes(e)
                for c in range(1, first):
                    step(c, 0)
                    if c <= QUADS:
                        if c > 2:
                            e.wait_ge(kxl_done, c - 2)
                        e.tensor_scalar(kxp[:, (c - 1) % 2, :], kx4[:, :], srow4[:, c - 1:c], None, ALU.mult)\
                            .then_inc(kxp_done, 1)
                    step(c, 1)
            with e.Fori(0, (n - 1) // 2 - first // 2) as i:
                for u in range(2):
                    step(2 * i + first + u, 0)
                    step(2 * i + first + u, 1)
            if n % 2 == 0:
                step(n - 1, 0)
                step(n - 1, 1)

        def dve_attn(e, p, cfg):
            dve_norm(e, p)
            if not cfg["causal"]:
                e.tensor_scalar(cols[:, 0:2], cols[:, 0:2], HD ** -0.5, None, ALU.mult).then_inc(s("bias_scaled"), 1)
                e.wait_ge(*nth(p, "bias_scaled", 1))
            for k in range(8):
                m, w = k // 4, (k // 2) % 2
                e.wait_ge(*nth(p, "hi_q", k + 1))
                if k == 4:
                    e.wait_ge(*nth(p, "lo_stored0", 64))
                if cfg["causal"]:
                    e.tensor_tensor(clo[:, k % 4, :], ps[:, k % 4, :], hi_f(chi[:, k % 4, :]), ALU.subtract)\
                        .then_inc(s("lo_q"), 1)
                else:
                    e.scalar_tensor_tensor(clo[:, k % 4, :], ps[:, k % 4, :], cols[:, 2 * w + m:2 * w + m + 1],
                                           hi_f(chi[:, k % 4, :]), ALU.add, ALU.subtract).then_inc(s("lo_q"), 1)
            if not cfg["causal"]:
                for t in range(TILES):
                    e.wait_ge(*nth(p, "v_banks", t + 1))
                    if t == 0:
                        e.wait_ge(*nth(p, "v_init", 4))
                    e.tensor_tensor(vaug[:, t, :, 0:HD], ps[:, 4 + t % 4, 0:D].rearrange("p (h d) -> p h d", d=HD),
                                    bvb[:, :].rearrange("p (h d) -> p h d", d=HD), ALU.add).then_inc(s("v_done"), 1)
            else:
                e.memset(nmax[:, :, 1], BIG).then_inc(s("nmax_init"), 1)
                e.wait_ge(*nth(p, "nmax_init", 1))
            e.memset(hi_f(nmp[:, :, :, :]), 0.0).then_inc(s("nm_init"), 1)
            e.wait_ge(*nth(p, "nm_init", 1))
            nmx = nz = 0
            for (kind, g, arg), (bank, before) in zip(cfg["order"], cfg["place"]):
                if kind == "max":
                    j, qt, kh, w = arg
                    e.wait_ge(*nth(p, "max_banks", nmx + 1))
                    if nmx % cfg["nitems"] == 0 and g >= 1:
                        e.wait_ge(*nth(p, "nm_done", 2 * g))
                    e.tensor_reduce(nmax[:, QUAD * qt + j, kh:kh + 1], ps[:, bank, 0:w], AX.X, ALU.max,
                                    negate=True).then_inc(s("reduced"), 1)
                    nmx += 1
                elif kind == "maxend":
                    half, u = arg, 2 * g + arg
                    part = slice(QUAD * 4 * half, QUAD * 4 * (half + 1))
                    e.wait_ge(*nth(p, "reduced", nmx))
                    if u >= 2:
                        e.wait_ge(*nth(p, "m_bank", u - 1))
                    e.tensor_tensor(nm[:, g % 2, part], nmax[:, part, 0], nmax[:, part, 1], ALU.min)\
                        .then_inc(s("nm_done"), 1)
                    e.wait_ge(*nth(p, "nm_done", u + 1))
                    src = nm[:, g % 2, part].rearrange("p (t j) -> p t j", j=QUAD)
                    dst = nmp[:, u % 2, :, :].rearrange("p t (j r) -> p t j r", j=QUAD)
                    e.tensor_copy(dst[:, :, :, 0], src).then_inc(s("nm_hi"), 1)
                    e.wait_ge(*nth(p, "nm_hi", u + 1))
                    e.tensor_tensor(dst[:, :, :, 1], src, hi_f(dst[:, :, :, 0]), ALU.subtract).then_inc(s("nm_lo"), 1)
                elif kind == "mrows":
                    sl = slice(HALF * arg, HALF * (arg + 1))
                    e.wait_ge(*nth(p, "m_bank", 2 * g + arg + 1))
                    for j in range(2, QUAD):
                        e.tensor_copy(qs[MROW:MROW + 2, QUAD * (g % SETS) + j, sl], ps[RC * j:RC * j + 2, bank, :])\
                            .then_inc(s("m_dve"), 1)
                elif kind == "z":
                    e.wait_ge(*nth(p, "z_bank", nz + 1))
                    den = ps[:, bank, :].rearrange("p (a r) -> p a r", r=32)
                    e.reciprocal(rden[:, nz % 2, :], den[:, :, HD]).then_inc(s("rden"), 1)
                    e.wait_ge(*nth(p, "rden", nz + 1))
                    qh = arg
                    e.tensor_tensor(xn[:, 4 * qh:4 * qh + 4, QUAD * HD * g:QUAD * HD * (g + 1)].rearrange(
                                        "p t (j d) -> p t j d", d=HD),
                                    ps[:, bank, :].rearrange("p (t j r) -> p t j r", t=4, r=32)[:, :, :, 0:HD],
                                    rden[:, nz % 2, :].rearrange("p (t j) -> p t j", t=4).unsqueeze(3)
                                    .to_broadcast([P, 4, QUAD, HD]), ALU.mult).then_inc(s("z_norm"), 1)
                    nz += 1
                elif kind == "feat":
                    dve_to_features(e, p, "z", 0)
            dve_to_features(e, p, "z", 1)

        @block.vector
        def _(e):
            e.memset(eps[:, :], EPS).then_inc(setup, 1)
            e.memset(hi_f(zero_r[:, :]), 0.0).then_inc(setup, 1)
            for p, cfg in enumerate(phases):
                (dve_ffn if cfg["kind"] == "ffn" else dve_attn)(e, p, cfg)
            for half in range(HALVES):
                dve_add(e, nphase, half)

        def pool_ffn(e, p, cfg):
            n = cfg["chunks"]

            def split_lo(c, b):
                e.wait_ge(*nth(p, "w_hi", c + 1))
                if not isinstance(c, int) or c >= 2:
                    e.wait_ge(*nth(p, "down_done", 2 * (c - 1)))
                for part, done in ((slice(0, WD), "w_lo"), (slice(WD, WSEL), "wd_lo")):
                    e.tensor_tensor(wlo[:, b, part], wraw[:, b, part], hi_f(whi[:, b, part]), ALU.subtract)\
                        .then_inc(s(done), 1)

            split_lo(0, 0)
            split_lo(1, 1)
            done = 2
            if p == 0:
                for part in range(TABLE_PARTS):
                    split_lo(done, done % 2)
                    pool_tables(e, part)
                    done += 1
            if p in ready_in:
                if p > 0:
                    e.wait_ge(*nth(p - 1, "sums", 2))
                for part in range(8):
                    split_lo(done, done % 2)
                    pool_ready_attn(e, ready_in[p], part)
                    done += 1
            if n - done >= 2:
                with e.Fori(0, (n - done) // 2) as i:
                    for b in range(2):
                        split_lo(2 * i + done + b, b)
            if n % 2 and done < n:
                split_lo(n - 1, (n - 1) % 2)

        def pool_did(ins):
            pool_steps[0] += 1
            ins.then_inc(s("pool_step"), 1)

        def pool_settle(e):
            e.wait_ge(s("pool_step"), pool_steps[0])

        def pool_tables(e, part):
            if part < QUADS:
                e.wait_ge(kxh_done, part + 1)
                e.tensor_tensor(kxl[:, part, :], kxp[:, part % 2, :], hi_f(kxh[:, part, :]), ALU.subtract)\
                    .then_inc(kxl_done, 1)
            else:
                heads = slope_part(part)
                e.wait_ge(slope_hi, part - QUADS + 1)
                e.tensor_tensor(slope_l[:, heads, :], slope_i[:, heads, :], hi_f(slope_h[:, heads, :]), ALU.subtract)\
                    .then_inc(kxl_done, 1)

        def pool_ready_attn(e, q, part):
            if part < 4:
                w = part
                e.wait_ge(*nth(q, "aw_loaded%d" % (w % 2), 16 * (w // 2 + 1)))
                h_, l_ = (awh[:, w, :], awl[:, w, :]) if w < 3 else (awo[:, 0, :], awo[:, 1, :])
                if w == 0:
                    pool_did(e.tensor_scalar(araw[:, 0, :], araw[:, 0, :], HD ** -0.5, None, ALU.mult))
                    pool_settle(e)
                pool_did(e.tensor_copy(h_, araw[:, w % 2, :]))
                pool_settle(e)
                e.tensor_tensor(l_, araw[:, w % 2, :], hi_f(h_), ALU.subtract).then_inc(s("aw_split"), 1)
            else:
                tiles = slice(2 * (part - 4), 2 * (part - 3))
                pool_did(e.memset(vaug[:, tiles, :, :], 0.0))
                pool_settle(e)
                e.memset(vaug[:, tiles, :, HD:HD + 1], 1.0).then_inc(s("v_init"), 1)

        def pool_attn(e, p, cfg):
            e.wait_ge(*nth(p - 1, "sums", 2))
            if p - 1 == 0:
                e.wait_ge(tables, 16 * (2 * TABLE_PARTS + 2))
            e.sem_inc(s("region_free"), 1)

            def tables_of(g):
                done = s("rows_loaded%d" % g)
                slots = slice(QUAD * (g % SETS), QUAD * (g % SETS + 1))
                for part in range(2):
                    e.dma_start(hi_f(ks[QX + 32 * part:QX + 32 * (part + 1), slots, :]),
                                kext_d[part, QUAD * g:QUAD * (g + 1), :, :].rearrange("j r t -> r j t"))\
                        .then_inc(done, 16)
                e.dma_start(hi_f(sdiag[:, g % SETS, :, :, :]).rearrange("p o j n -> p o (j n)"),
                            sdiag_d[:, :, QUAD * P * g:QUAD * P * (g + 1)].rearrange("o p n -> p o n"))\
                    .then_inc(done, 16)

            if not cfg["causal"]:
                tables_of(0)
            e.wait_ge(*nth(p, "first_rows_loaded", 16 * 8))
            for g in range(1, QUADS):
                done = s("rows_loaded%d" % g)
                for part in ("hi", "lo"):
                    e.wait_ge(*nth(p, "%s_stored%d" % (part, g // 2), 64))
                if g >= SETS:
                    e.wait_ge(*nth(p, "score_banks", 2 * cfg["nsteps"] * (g - SETS + 1)))
                row_loads(e, p, g, "rows_loaded%d" % g)
                if not cfg["causal"]:
                    tables_of(g)
                if g >= SETS:
                    slots = slice(QUAD * (g % SETS), QUAD * (g % SETS + 1))
                    e.dma_start(hi_f(qs[MROW:MROW + 2, slots, :]).rearrange("p s (h c) -> p (s h) c", h=2),
                                zero_d[0:2, :].unsqueeze(1).to_broadcast([2, 2 * QUAD, HALF])).then_inc(done, 16)

        @block.gpsimd
        def _(e):
            e.wait_ge(consts, n_consts)
            for p, cfg in enumerate(phases):
                (pool_ffn if cfg["kind"] == "ffn" else pool_attn)(e, p, cfg)


def position_tables(np):
    i = np.arange(P)
    ident = np.eye(P, dtype=np.float32)
    dist = -np.abs(i[:, None] - i[None, :]).astype(np.float32)
    causal = np.where(i[None, :] > i[:, None], np.float32(-2.0 ** 127), np.float32(0)).astype(np.float32)
    iota = np.ascontiguousarray(np.broadcast_to(np.arange(16, dtype=np.float32), (P, 16)))
    t = np.arange(T)
    tile = t // P
    qx = np.zeros((P, T), np.float32)
    kx = np.zeros((P, T), np.float32)
    for c in range(TILES):
        centre = P * c + P // 2
        side = np.sign(tile - c).astype(np.float32)
        for base in (QX, QX + 32):
            qx[base + 2 + c] = -np.abs(t - centre) * np.abs(side)
            qx[base + 2 + TILES + c] = side
        kx[QX + 2 + c] = tile == c
        kx[QX + 2 + TILES + c] = (t - centre) * (tile == c)
    kx[MROW:MROW + 2] = 1.0
    keep = np.zeros((P, 2), np.float32)
    keep[:, 0] = np.arange(P) % 32 >= 2
    keep[:, 1] = 1.0 - keep[:, 0]
    return dict(ident=ident, dist=dist, causal=causal, iota=iota, qx=qx[QX:],
                kx4=np.tile(kx[QX:QX + 32], (4, 1)), keep=keep)


def pack_ffn(np, wg, wu, wd, sg, su, sd, experts, hidden, chunks):
    pad = chunks * P
    n = experts * hidden
    G, U = np.zeros((D, pad), np.float32), np.zeros((D, pad), np.float32)
    W = np.zeros((pad, D), np.float32)
    sel = np.zeros((P, pad), np.float32)
    m = n + sg.shape[1]
    G[:, :n] = wg.transpose(1, 0, 2).reshape(D, n)
    U[:, :n] = wu.transpose(1, 0, 2).reshape(D, n)
    G[:, n:m], U[:, n:m] = sg, su
    W[:n], W[n:m] = wd.reshape(n, D), sd
    for e in range(experts):
        sel[[e, RC + e], e * hidden:(e + 1) * hidden] = 1.0
    sel[[experts, RC + experts], n:m] = 1.0
    out = np.zeros((chunks, P, WCOLS), np.float32)
    for c in range(chunks):
        s = slice(c * P, (c + 1) * P)
        out[c, :, WG:WG + P], out[c, :, WG + P:WU] = G[:P, s], G[P:, s]
        out[c, :, WU:WU + P], out[c, :, WU + P:WD] = U[:P, s], U[P:, s]
        out[c, :, WD:WSEL] = W[s]
        out[c, :, WSEL:] = sel[:, s]
    return out


PLAN = ["f0", "a0", "f0", "f1", "a1", "f1"]


def kernel(**inputs):
    import numpy as _np
    import concourse.bacc as _bacc
    from concourse.bass_utils import run_bass_kernel_spmd as _run

    I = {k: _np.asarray(v) for k, v in inputs.items()}

    def chunked(w):
        return _np.ascontiguousarray(w.reshape(KC, P, -1).transpose(1, 0, 2))

    def router(*ws):
        r = _np.zeros((D, RC), _np.float32)
        c = 0
        for w in ws:
            r[:, c:c + w.shape[1]] = w
            c += w.shape[1]
        return chunked(r)

    def attn(*ws):
        return _np.stack([chunked(w.T).reshape(P, KC * D) for w in ws])

    arrays = position_tables(_np)
    arrays["x"] = I["L0_attn_x"]
    arrays["wr0"] = router(I["L0_ffn_Wr"], I["L0_ffn_Wsg"])
    arrays["wr1"] = router(I["L1_ffn_w_router"])
    cols = _np.zeros((P, 8), _np.float32)
    for k, name in enumerate(("bq", "bk", "bo")):
        cols[:, 2 * k:2 * k + 2] = I["L0_attn_" + name].reshape(KC, P).T
    arrays["cols"] = cols
    arrays["bvb"] = _np.ascontiguousarray(_np.broadcast_to(I["L0_attn_bv"], (P, D)))
    arrays["slopes"] = _np.ascontiguousarray(_np.broadcast_to(I["L0_attn_slopes"], (P, NH)))
    arrays["slope4"] = _np.repeat(I["L0_attn_slopes"].reshape(QUADS, QUAD).T, 32, axis=0)
    arrays["f0"] = pack_ffn(_np, I["L0_ffn_Wg"], I["L0_ffn_Wu"], I["L0_ffn_Wd"], I["L0_ffn_Sg"], I["L0_ffn_Su"],
                            I["L0_ffn_Sd"], FFN0["experts"], 176, FFN0["chunks"])
    arrays["f1"] = pack_ffn(_np, I["L1_ffn_we1"], I["L1_ffn_we3"], I["L1_ffn_we2"], I["L1_ffn_ws1"], I["L1_ffn_ws3"],
                            I["L1_ffn_ws2"], FFN1["experts"], 128, FFN1["chunks"])
    arrays["a0"] = attn(*(I["L0_attn_W" + c] for c in "qkvo"))
    arrays["a1"] = attn(*(I["L1_attn_W" + c] for c in "qkvo"))

    kinds = {
        "f0": dict(kind="ffn", w="f0", router=0, moe_scale=0.5, shared_scale=0.5, **FFN0),
        "f1": dict(kind="ffn", w="f1", router=1, moe_scale=0.5 * 4 / 5, shared_scale=0.5 / 5, **FFN1),
        "a0": dict(kind="attn", w="a0", causal=False),
        "a1": dict(kind="attn", w="a1", causal=True),
    }
    nc = _bacc.Bacc("TRN2", target_bir_lowering=False, num_devices=1)
    A = {}
    for name, a in arrays.items():
        arrays[name] = a = _np.ascontiguousarray(a)
        A[name] = nc.dram_tensor(f"in_{name}", a.shape, F32, kind="ExternalInput").ap()
    out = nc.dram_tensor("out_x", (1, T, D), F32, kind="ExternalOutput").ap()
    program(nc, A, out, [dict(kinds[k]) for k in PLAN])
    r = _run(nc, [{f"in_{name}": a for name, a in arrays.items()}], core_ids=[0])
    return r.results[0]["out_x"]
```
